# Optimizing a Trainium2 kernel written in Bass

```python
import numpy as np
import jax
import jax.numpy as jnp

def _softmax(x, axis=-1):
    return jax.nn.softmax(x, axis=axis)

def _gelu(x):
    return jax.nn.gelu(x, approximate=True)

def _silu(x):
    return jax.nn.silu(x)

def _sigmoid(x):
    return jax.nn.sigmoid(x)

def _layernorm(x, axis=-1, eps=1e-05):
    m = jnp.mean(x, axis=axis, keepdims=True)
    v = jnp.var(x, axis=axis, keepdims=True)
    return (x - m) / jnp.sqrt(v + eps)

def _scatter_add(tgt, idx, src, axis=0):
    return tgt.at[idx].add(src)

def _segment_sum(src, seg, n):
    return jax.ops.segment_sum(src, seg, n)
kernel_name = 'mk_vit_tower_d2_tok_img256_r4_3d72ec'

def setup_inputs(seed: int=0):
    np.random.seed(seed)
    _w = jnp.asarray

    def _rec_inputs():
        import jax
        import jax.numpy as jnp
        _rk = jax.random.key(seed)
        x = 7.22013e-05 + 1.00017 * jax.random.normal(jax.random.fold_in(_rk, 1), (64, 1, 64, 64), jnp.float32)
        return x
    x = _rec_inputs()

    def _L0_tok_setup():
        import jax, jax.numpy as jnp
        import numpy as np
        P = 8
        C = 1
        D = 64
        key = jax.random.key(seed)
        k1, k2, k3 = jax.random.split(key, 3)
        x = jax.random.normal(k1, (128, C, 64, 64), dtype=jnp.float32)
        patch_dim = P * P * C
        bound = 1.0 / np.sqrt(patch_dim)
        W = jax.random.uniform(k2, (D, patch_dim), dtype=jnp.float32, minval=-bound, maxval=bound)
        b = jax.random.uniform(k3, (D,), dtype=jnp.float32, minval=-bound, maxval=bound)
        return {'x': x, 'W': W, 'b': b}
    _L0_tok_all = _L0_tok_setup()
    _L0_tok_in = {k: v for k, v in _L0_tok_all.items() if k in ('W', 'b')}
    del _L0_tok_all

    def _L0_attn_setup():
        import jax, jax.numpy as jnp
        import numpy as np
        DIM = 64
        NUM_HEADS = 8
        HEAD_DIM = DIM // NUM_HEADS
        WINDOW = 64
        NW = 1024
        key = jax.random.key(seed)
        ks = jax.random.split(key, 6)
        x = jax.random.normal(ks[0], (NW, WINDOW, DIM), dtype=jnp.float32)
        w_qkv = jax.random.normal(ks[1], (DIM, 3 * DIM), dtype=jnp.float32) * DIM ** (-0.5)
        b_qkv = jnp.zeros((3 * DIM,), dtype=jnp.float32)
        w_proj = jax.random.normal(ks[2], (DIM, DIM), dtype=jnp.float32) * DIM ** (-0.5)
        b_proj = jnp.zeros((DIM,), dtype=jnp.float32)
        rel_pos_bias = jax.random.normal(ks[3], (NUM_HEADS, 2 * WINDOW - 1), dtype=jnp.float32) * 0.02
        return {'x': x, 'w_qkv': w_qkv, 'b_qkv': b_qkv, 'w_proj': w_proj, 'b_proj': b_proj, 'rel_pos_bias': rel_pos_bias}
    _L0_attn_all = _L0_attn_setup()
    _L0_attn_in = {k: v for k, v in _L0_attn_all.items() if k in ('w_qkv', 'b_qkv', 'w_proj', 'b_proj', 'rel_pos_bias')}
    del _L0_attn_all

    def _L0_ffn_setup():
        import jax, jax.numpy as jnp
        import numpy as np
        B, N, D = (16, 1024, 64)
        NUM_EXPERTS, TOP_K, HEADS = (4, 2, 4)
        N_EDGES = 262144
        LN_EPS = 1e-05

        def _layernorm(x, g, b):
            mu = x.mean(-1, keepdims=True)
            var = ((x - mu) ** 2).mean(-1, keepdims=True)
            return (x - mu) * jax.lax.rsqrt(var + LN_EPS) * g + b

        def _forward(x, edge_index, W_gat, att_src, att_dst, b_gat, ln_gamma, ln_beta, W1, b1, W2, b2):
            Bc, Nc, Dc = x.shape
            M = Bc * Nc
            x_flat = x.reshape(M, Dc)
            h = (x_flat @ W_gat).reshape(M, HEADS, NUM_EXPERTS)
            loops = jnp.arange(M, dtype=edge_index.dtype)
            src = jnp.concatenate([edge_index[0], loops])
            dst = jnp.concatenate([edge_index[1], loops])
            a_src = (h * att_src).sum(-1)
            a_dst = (h * att_dst).sum(-1)
            e = jax.nn.leaky_relu(a_src[src] + a_dst[dst], negative_slope=0.2)
            e_max = jax.ops.segment_max(e, dst, num_segments=M)
            ee = jnp.exp(e - e_max[dst])
            denom = jax.ops.segment_sum(ee, dst, num_segments=M)
            alpha = ee / (denom[dst] + 1e-16)
            msg = h[src] * alpha[:, :, None]
            agg = jax.ops.segment_sum(msg, dst, num_segments=M).reshape(M, HEADS * NUM_EXPERTS) + b_gat
            scores = _layernorm(agg, ln_gamma, ln_beta).reshape(M, HEADS, NUM_EXPERTS).mean(1)
            scores = scores.reshape(Bc, Nc, NUM_EXPERTS)
            topk_s, topk_i = jax.lax.top_k(scores, TOP_K)
            w = jax.nn.softmax(topk_s, axis=-1)
            out = jnp.zeros_like(x)
            for ei in range(NUM_EXPERTS):
                g = jnp.where(topk_i == ei, w, 0.0).sum(-1)
                hh = jax.nn.gelu(x @ W1[ei] + b1[ei], approximate=False)
                out = out + g[..., None] * (hh @ W2[ei] + b2[ei])
            return out
        key = jax.random.key(seed)
        ks = jax.random.split(key, 8)
        s = 0.05
        return {'x': jax.random.normal(ks[0], (B, N, D), jnp.float32), 'W_gat': jax.random.normal(ks[1], (D, HEADS * NUM_EXPERTS), jnp.float32) * s, 'att_src': jax.random.normal(ks[2], (HEADS, NUM_EXPERTS), jnp.float32) * s, 'att_dst': jax.random.normal(ks[3], (HEADS, NUM_EXPERTS), jnp.float32) * s, 'b_gat': jnp.zeros((HEADS * NUM_EXPERTS,), jnp.float32), 'ln_gamma': jnp.ones((HEADS * NUM_EXPERTS,), jnp.float32), 'ln_beta': jnp.zeros((HEADS * NUM_EXPERTS,), jnp.float32), 'W1': jax.random.normal(ks[4], (NUM_EXPERTS, D, 2 * D), jnp.float32) * s, 'b1': jnp.zeros((NUM_EXPERTS, 2 * D), jnp.float32), 'W2': jax.random.normal(ks[5], (NUM_EXPERTS, 2 * D, D), jnp.float32) * s, 'b2': jnp.zeros((NUM_EXPERTS, D), jnp.float32), 'edge_index': jax.random.randint(ks[6], (2, N_EDGES), 0, B * N, jnp.int32)}
    _L0_ffn_all = _L0_ffn_setup()
    _L0_ffn_in = {k: v for k, v in _L0_ffn_all.items() if k in ('W_gat', 'att_src', 'att_dst', 'b_gat', 'ln_gamma', 'ln_beta', 'W1', 'b1', 'W2', 'b2', 'edge_index')}
    del _L0_ffn_all

    def _L1_attn_setup():
        import jax, jax.numpy as jnp
        import numpy as np
        BN_EPS = 1e-05
        key = jax.random.key(seed)
        ks = jax.random.split(key, 12)
        B, N, d_e, d_a = (16, 512, 64, 64)
        s_e = 1.0 / np.sqrt(d_e)
        return {'x': jax.random.normal(ks[0], (B, N, d_e), dtype=jnp.float32), 'Wq': jax.random.uniform(ks[1], (d_e, d_a), jnp.float32, -s_e, s_e), 'bq': jax.random.uniform(ks[2], (d_a,), jnp.float32, -s_e, s_e), 'Wk': jax.random.uniform(ks[3], (d_e, d_a), jnp.float32, -s_e, s_e), 'bk': jax.random.uniform(ks[4], (d_a,), jnp.float32, -s_e, s_e), 'Wv': jax.random.uniform(ks[5], (d_e, d_e), jnp.float32, -s_e, s_e), 'bv': jax.random.uniform(ks[6], (d_e,), jnp.float32, -s_e, s_e), 'Wl': jax.random.uniform(ks[7], (d_e, d_e), jnp.float32, -s_e, s_e), 'bl': jax.random.uniform(ks[8], (d_e,), jnp.float32, -s_e, s_e), 'gamma': jnp.ones((d_e,), jnp.float32), 'beta': jnp.zeros((d_e,), jnp.float32)}
    _L1_attn_all = _L1_attn_setup()
    _L1_attn_in = {k: v for k, v in _L1_attn_all.items() if k in ('Wq', 'bq', 'Wk', 'bk', 'Wv', 'bv', 'Wl', 'bl', 'gamma', 'beta')}
    del _L1_attn_all

    def _L1_ffn_setup():
        import jax, jax.numpy as jnp
        import numpy as np
        E = 8
        K = 2
        D = 64
        H = 128
        DOUT = 64
        EPS = 1e-05
        key = jax.random.key(seed)
        ks = jax.random.split(key, 9)
        s = 0.02
        return {'x': jax.random.normal(ks[0], (4, 2048, D), jnp.float32), 'gamma': 1.0 + 0.05 * jax.random.normal(ks[1], (D,), jnp.float32), 'beta': 0.05 * jax.random.normal(ks[2], (D,), jnp.float32), 'Wr': 0.01 * jax.random.normal(ks[3], (D, E), jnp.float32), 'br': jnp.zeros((E,), jnp.float32), 'W1': s * jax.random.normal(ks[4], (E, D, H), jnp.float32), 'b1': s * jax.random.normal(ks[5], (E, H), jnp.float32), 'W2': s * jax.random.normal(ks[6], (E, H, DOUT), jnp.float32), 'b2': s * jax.random.normal(ks[7], (E, DOUT), jnp.float32)}
    _L1_ffn_all = _L1_ffn_setup()
    _L1_ffn_in = {k: v for k, v in _L1_ffn_all.items() if k in ('gamma', 'beta', 'Wr', 'br', 'W1', 'b1', 'W2', 'b2')}
    del _L1_ffn_all
    return {'x': x, 'L0_tok_W': _L0_tok_in['W'], 'L0_tok_b': _L0_tok_in['b'], 'L0_attn_w_qkv': _L0_attn_in['w_qkv'], 'L0_attn_b_qkv': _L0_attn_in['b_qkv'], 'L0_attn_w_proj': _L0_attn_in['w_proj'], 'L0_attn_b_proj': _L0_attn_in['b_proj'], 'L0_attn_rel_pos_bias': _L0_attn_in['rel_pos_bias'], 'L0_ffn_W_gat': _L0_ffn_in['W_gat'], 'L0_ffn_att_src': _L0_ffn_in['att_src'], 'L0_ffn_att_dst': _L0_ffn_in['att_dst'], 'L0_ffn_b_gat': _L0_ffn_in['b_gat'], 'L0_ffn_ln_gamma': _L0_ffn_in['ln_gamma'], 'L0_ffn_ln_beta': _L0_ffn_in['ln_beta'], 'L0_ffn_W1': _L0_ffn_in['W1'], 'L0_ffn_b1': _L0_ffn_in['b1'], 'L0_ffn_W2': _L0_ffn_in['W2'], 'L0_ffn_b2': _L0_ffn_in['b2'], 'L0_ffn_edge_index': _L0_ffn_in['edge_index'], 'L1_attn_Wq': _L1_attn_in['Wq'], 'L1_attn_bq': _L1_attn_in['bq'], 'L1_attn_Wk': _L1_attn_in['Wk'], 'L1_attn_bk': _L1_attn_in['bk'], 'L1_attn_Wv': _L1_attn_in['Wv'], 'L1_attn_bv': _L1_attn_in['bv'], 'L1_attn_Wl': _L1_attn_in['Wl'], 'L1_attn_bl': _L1_attn_in['bl'], 'L1_attn_gamma': _L1_attn_in['gamma'], 'L1_attn_beta': _L1_attn_in['beta'], 'L1_ffn_gamma': _L1_ffn_in['gamma'], 'L1_ffn_beta': _L1_ffn_in['beta'], 'L1_ffn_Wr': _L1_ffn_in['Wr'], 'L1_ffn_br': _L1_ffn_in['br'], 'L1_ffn_W1': _L1_ffn_in['W1'], 'L1_ffn_b1': _L1_ffn_in['b1'], 'L1_ffn_W2': _L1_ffn_in['W2'], 'L1_ffn_b2': _L1_ffn_in['b2']}

def reference(x, L0_tok_W, L0_tok_b, L0_attn_w_qkv, L0_attn_b_qkv, L0_attn_w_proj, L0_attn_b_proj, L0_attn_rel_pos_bias, L0_ffn_W_gat, L0_ffn_att_src, L0_ffn_att_dst, L0_ffn_b_gat, L0_ffn_ln_gamma, L0_ffn_ln_beta, L0_ffn_W1, L0_ffn_b1, L0_ffn_W2, L0_ffn_b2, L0_ffn_edge_index, L1_attn_Wq, L1_attn_bq, L1_attn_Wk, L1_attn_bk, L1_attn_Wv, L1_attn_bv, L1_attn_Wl, L1_attn_bl, L1_attn_gamma, L1_attn_beta, L1_ffn_gamma, L1_ffn_beta, L1_ffn_Wr, L1_ffn_br, L1_ffn_W1, L1_ffn_b1, L1_ffn_W2, L1_ffn_b2):
    import jax
    import jax.numpy as jnp

    def _L0_tok_ref(x, W, b):
        import jax, jax.numpy as jnp
        import numpy as np
        P = 8
        C = 1
        D = 64
        B, c, h, w = x.shape
        p = P
        xp = x.reshape(B, c, h // p, p, w // p, p)
        xp = jnp.transpose(xp, (0, 2, 4, 3, 5, 1))
        xp = xp.reshape(B, h // p * (w // p), p * p * c)
        return jnp.einsum('bnk,dk->bnd', xp, W) + b

    def _L0_attn_ref(x, w_qkv, b_qkv, w_proj, b_proj, rel_pos_bias):
        import jax, jax.numpy as jnp
        import numpy as np
        DIM = 64
        NUM_HEADS = 8
        HEAD_DIM = DIM // NUM_HEADS
        WINDOW = 64
        NW = 1024
        NWb, W, D = x.shape
        scale = HEAD_DIM ** (-0.5)
        qkv = x @ w_qkv + b_qkv
        qkv = qkv.reshape(NWb, W, 3, NUM_HEADS, HEAD_DIM).transpose(2, 0, 3, 1, 4)
        q, k, v = (qkv[0], qkv[1], qkv[2])
        attn = jnp.einsum('nhqd,nhkd->nhqk', q, k) * scale
        pos = jnp.arange(W)
        rel_idx = jnp.clip(pos[None, :] - pos[:, None] + (WINDOW - 1), 0, 2 * WINDOW - 2)
        bias = rel_pos_bias[:, rel_idx]
        attn = jax.nn.softmax(attn + bias[None], axis=-1)
        out = jnp.einsum('nhqk,nhkd->nhqd', attn, v)
        out = out.transpose(0, 2, 1, 3).reshape(NWb, W, D)
        return out @ w_proj + b_proj

    def _L0_ffn_ref(x, W_gat, att_src, att_dst, b_gat, ln_gamma, ln_beta, W1, b1, W2, b2, edge_index):
        import jax, jax.numpy as jnp
        import numpy as np
        B, N, D = (16, 1024, 64)
        NUM_EXPERTS, TOP_K, HEADS = (4, 2, 4)
        N_EDGES = 262144
        LN_EPS = 1e-05

        def _layernorm(x, g, b):
            mu = x.mean(-1, keepdims=True)
            var = ((x - mu) ** 2).mean(-1, keepdims=True)
            return (x - mu) * jax.lax.rsqrt(var + LN_EPS) * g + b

        def _forward(x, edge_index, W_gat, att_src, att_dst, b_gat, ln_gamma, ln_beta, W1, b1, W2, b2):
            Bc, Nc, Dc = x.shape
            M = Bc * Nc
            x_flat = x.reshape(M, Dc)
            h = (x_flat @ W_gat).reshape(M, HEADS, NUM_EXPERTS)
            loops = jnp.arange(M, dtype=edge_index.dtype)
            src = jnp.concatenate([edge_index[0], loops])
            dst = jnp.concatenate([edge_index[1], loops])
            a_src = (h * att_src).sum(-1)
            a_dst = (h * att_dst).sum(-1)
            e = jax.nn.leaky_relu(a_src[src] + a_dst[dst], negative_slope=0.2)
            e_max = jax.ops.segment_max(e, dst, num_segments=M)
            ee = jnp.exp(e - e_max[dst])
            denom = jax.ops.segment_sum(ee, dst, num_segments=M)
            alpha = ee / (denom[dst] + 1e-16)
            msg = h[src] * alpha[:, :, None]
            agg = jax.ops.segment_sum(msg, dst, num_segments=M).reshape(M, HEADS * NUM_EXPERTS) + b_gat
            scores = _layernorm(agg, ln_gamma, ln_beta).reshape(M, HEADS, NUM_EXPERTS).mean(1)
            scores = scores.reshape(Bc, Nc, NUM_EXPERTS)
            topk_s, topk_i = jax.lax.top_k(scores, TOP_K)
            w = jax.nn.softmax(topk_s, axis=-1)
            out = jnp.zeros_like(x)
            for ei in range(NUM_EXPERTS):
                g = jnp.where(topk_i == ei, w, 0.0).sum(-1)
                hh = jax.nn.gelu(x @ W1[ei] + b1[ei], approximate=False)
                out = out + g[..., None] * (hh @ W2[ei] + b2[ei])
            return out
        return _forward(x, edge_index, W_gat, att_src, att_dst, b_gat, ln_gamma, ln_beta, W1, b1, W2, b2)

    def _L1_attn_ref(x, Wq, bq, Wk, bk, Wv, bv, Wl, bl, gamma, beta):
        import jax, jax.numpy as jnp
        import numpy as np
        BN_EPS = 1e-05
        q = x @ Wq + bq
        k = x @ Wk + bk
        v = x @ Wv + bv
        d_a = q.shape[-1]
        score = jnp.einsum('bnd,bmd->bnm', q, k) / jnp.asarray(d_a, q.dtype)
        score = jax.nn.softmax(score, axis=2)
        attn = jnp.einsum('bnm,bmd->bnd', score, v)
        h = attn @ Wl + bl
        mean = jnp.mean(h, axis=(0, 1))
        var = jnp.mean((h - mean) ** 2, axis=(0, 1))
        y = jax.nn.relu((h - mean) * jax.lax.rsqrt(var + BN_EPS) * gamma + beta)
        return y + x

    def _L1_ffn_ref(x, gamma, beta, Wr, br, W1, b1, W2, b2):
        import jax, jax.numpy as jnp
        import numpy as np
        E = 8
        K = 2
        D = 64
        H = 128
        DOUT = 64
        EPS = 1e-05
        mu = jnp.mean(x, axis=-1, keepdims=True)
        var = jnp.mean(jnp.square(x - mu), axis=-1, keepdims=True)
        xn = (x - mu) * jax.lax.rsqrt(var + EPS) * gamma + beta
        logits = jnp.einsum('bsd,de->bse', xn, Wr) + br
        top_vals, top_idx = jax.lax.top_k(logits, K)
        w = jax.nn.softmax(top_vals, axis=-1)
        w_full = jnp.einsum('bsk,bske->bse', w, jax.nn.one_hot(top_idx, E, dtype=w.dtype))
        y = jnp.zeros(x.shape[:-1] + (DOUT,), x.dtype)
        for e in range(E):
            h = jax.nn.gelu(jnp.einsum('bsd,dh->bsh', xn, W1[e]) + b1[e], approximate=False)
            y_e = jnp.einsum('bsh,hd->bsd', h, W2[e]) + b2[e]
            y = y + y_e * w_full[..., e, None]
        return y
    h = _L0_tok_ref(x, L0_tok_W, L0_tok_b)
    h = h + _L0_attn_ref(_layernorm(h, axis=-1), L0_attn_w_qkv, L0_attn_b_qkv, L0_attn_w_proj, L0_attn_b_proj, L0_attn_rel_pos_bias)
    h = h + _L0_ffn_ref(_layernorm(h, axis=-1), L0_ffn_W_gat, L0_ffn_att_src, L0_ffn_att_dst, L0_ffn_b_gat, L0_ffn_ln_gamma, L0_ffn_ln_beta, L0_ffn_W1, L0_ffn_b1, L0_ffn_W2, L0_ffn_b2, L0_ffn_edge_index)
    h = h + _L1_attn_ref(_layernorm(h, axis=-1), L1_attn_Wq, L1_attn_bq, L1_attn_Wk, L1_attn_bk, L1_attn_Wv, L1_attn_bv, L1_attn_Wl, L1_attn_bl, L1_attn_gamma, L1_attn_beta)
    h = h + _L1_ffn_ref(_layernorm(h, axis=-1), L1_ffn_gamma, L1_ffn_beta, L1_ffn_Wr, L1_ffn_br, L1_ffn_W1, L1_ffn_b1, L1_ffn_W2, L1_ffn_b2)
    return h

_drawn_inputs = setup_inputs


def setup_inputs(seed=0):
    import zlib

    import numpy as np

    out = dict(_drawn_inputs(seed))
    spreads = {'L0_attn_b_qkv': (0.0, 0.1),
     'L0_attn_b_proj': (0.0, 0.1),
     'L0_ffn_b_gat': (0.0, 0.44),
     'L0_ffn_ln_gamma': (1.0, 0.6),
     'L0_ffn_ln_beta': (0.0, 0.8),
     'L0_ffn_b1': (0.0, 0.268),
     'L0_ffn_b2': (0.0, 0.1),
     'L1_attn_gamma': (1.0, 0.2),
     'L1_attn_beta': (0.0, 0.1),
     'L1_ffn_br': (0.0, 0.8)}
    factors = {'L0_attn_rel_pos_bias': 8.0,
     'L0_ffn_att_src': 8.0,
     'L0_ffn_att_dst': 8.0,
     'L1_attn_Wq': 3.332,
     'L1_attn_bq': 8.0,
     'L1_attn_Wk': 2.952,
     'L1_attn_bk': 64.0,
     'L1_attn_bv': 64.0,
     'L1_attn_bl': 64.0,
     'L1_ffn_gamma': 8.0,
     'L1_ffn_beta': 8.0,
     'L1_ffn_Wr': 7.09,
     'L1_ffn_W1': 7.977,
     'L1_ffn_b1': 27.743,
     'L1_ffn_W2': 8.0,
     'L1_ffn_b2': 38.27}
    for name, (base, spread) in spreads.items():
        noise = np.random.default_rng([zlib.crc32(name.encode()), seed]).standard_normal(out[name].shape)
        drawn = base * np.exp(spread * noise) if base else spread * noise
        out[name] = jnp.asarray(drawn.astype(out[name].dtype))
    for name, factor in factors.items():
        out[name] = (out[name] * factor).astype(out[name].dtype)
    return out
```

```python
from contextlib import ExitStack

import concourse.bass as bass
from concourse import mybir

F32 = mybir.dt.float32
BF16 = mybir.dt.bfloat16
I32 = mybir.dt.int32
ALU = mybir.AluOpType
ACT = mybir.ActivationFunctionType
AX = mybir.AxisListType

P = 128
D = 64
IMG = 64
WIN = 64
M = IMG * WIN
TILES = M // P
HD = 8
NH = D // HD
GH, GE = 4, 4
E0, E1 = 4, 8
HID = 128
EDGES = 262144
EC = EDGES // P
EPS = 1e-5
CLASS_LAST = float(1 << 24)
CLASS_NONE = float(1 << 25)
GCH = 8
CCH = 16
NSRC = GH * GE + GH
NDST = 2 * GH
NV = GH * (GE + 1)


def twice(eng, n, body):
    body(0, 0, True)
    body(1, 1, True)
    with eng.Fori(1, n // 2) as i:
        for b in range(2):
            body(2 * i + b, b, False)


def bc(ap, n):
    return ap.unsqueeze(len(ap.shape)).broadcast_to([*ap.shape, n])


def bc_at(ap, axis, n):
    a = ap.unsqueeze(axis)
    return a.broadcast_to([*a.shape[:axis], n, *a.shape[axis + 1:]])


class Memory:

    def __init__(self, nc, ctx):
        self.nc, self.ctx = nc, ctx

    def sb(self, name, shape, dt=F32):
        return self.ctx.enter_context(self.nc.sbuf_tensor(name, shape, dt))

    def ps(self, name, shape, dt=F32):
        return self.ctx.enter_context(self.nc.psum_tensor(name, shape, dt))

    def sem(self, name):
        return self.ctx.enter_context(self.nc.semaphore(name))


class Stage:

    def __init__(self, mem):
        self.nc, self.sem, self.ctx = mem.nc, mem.sem, ExitStack()
        m = Memory(mem.nc, self.ctx)
        self.sb, self.ps = m.sb, m.ps

    def __enter__(self):
        return self

    def __exit__(self, *exc):
        self.ctx.close()


def load_constants(nc, mem, a, k):
    loaded = mem.sem("constants_loaded")
    made = mem.sem("constants_made")
    turned = mem.sem("token_weight_turned")
    k.ident = mem.sb("ident", [P, P])
    k.wqkv = mem.sb("wqkv", [D + 1, 3 * D])
    k.wproj = mem.sb("wproj", [D + 1, D])
    k.wtok = mem.sb("wtok", [D + 1, D])
    k.wtok_raw = mem.sb("wtok_raw", [D, D])
    k.relbias = mem.sb("relbias", [P, NH, WIN])
    k.wgat = mem.sb("wgat", [D + 1, GH * GE])
    k.att_src = mem.sb("att_src", [P, GH * GE])
    k.att_dst = mem.sb("att_dst", [P, GH * GE])
    k.b_gat = mem.sb("b_gat", [P, GH * GE])
    k.ln_gamma = mem.sb("ln_gamma", [P, GH * GE])
    k.ln_beta = mem.sb("ln_beta", [P, GH * GE])
    k.w1 = [mem.sb("moe0_w1", [D + 1, E0, HID]), mem.sb("moe1_w1", [D + 1, E1, HID])]
    k.w2 = [mem.sb("moe0_w2", [HID, E0, D]), mem.sb("moe1_w2", [HID, E1, D])]
    k.b2 = [mem.sb("moe0_b2", [4 * E0, 4, D]), mem.sb("moe1_b2", [4 * E1, 4, D])]
    b2_zeroed = mem.sem("b2_zeroed")
    k.wl1 = mem.sb("attn1_w", [D + 1, 4, D])
    k.bn = mem.sb("attn1_bn", [D, 2])
    k.affine = mem.sb("moe1_affine", [D, 2])
    k.wr = mem.sb("moe1_wr", [D + 1, E1])
    k.eps = mem.sb("eps", [P, 1])
    k.headmask = mem.sb("headmask", [P, 2, NH])
    k.iota_lo = mem.sb("iota_lo", [P, P])
    k.lower = mem.sb("lower", [P, E1, E1])
    k.lower0 = mem.sb("lower0", [P, E0, E0])
    k.zero_mm = mem.sb("zero_mm", [P, 512])
    turn = mem.ps("turn_token_weight", [D, D])
    bias_rows = mem.sb("bias_rows", [WIN, NH, WIN])
    reverse = mem.sb("reverse", [WIN, 2, WIN])
    bias_ps = mem.ps("bias_ps", [P, NH, WIN])

    def row(v):
        return v.rearrange("(a n) -> a n", a=1)

    def everywhere(v, n):
        return bass.AP(v.tensor, 0, [[0, P], [1, n]])

    loads = [
        (k.wtok_raw[:], a["L0_tok_W"]), (k.wtok[D:D + 1, :], row(a["L0_tok_b"])),
        (k.wqkv[0:D, :], a["L0_attn_w_qkv"]), (k.wqkv[D:D + 1, :], row(a["L0_attn_b_qkv"])),
        (k.wproj[0:D, :], a["L0_attn_w_proj"]), (k.wproj[D:D + 1, :], row(a["L0_attn_b_proj"])),
        (k.wgat[0:D, :], a["L0_ffn_W_gat"]),
        (k.bn[:, 0:1], a["L1_attn_gamma"].rearrange("(p a) -> p a", a=1)),
        (k.bn[:, 1:2], a["L1_attn_beta"].rearrange("(p a) -> p a", a=1)),
        (k.affine[:, 0:1], a["L1_ffn_gamma"].rearrange("(p a) -> p a", a=1)),
        (k.affine[:, 1:2], a["L1_ffn_beta"].rearrange("(p a) -> p a", a=1)),
        (k.wr[0:D, :], a["L1_ffn_Wr"]), (k.wr[D:D + 1, :], row(a["L1_ffn_br"])),
    ]
    loads.append((bias_rows[:], bass.AP(a["L0_attn_rel_pos_bias"].tensor, 0,
                                        [[1, WIN], [2 * WIN - 1, NH], [1, WIN]])))
    for dst, name in ((k.att_src, "L0_ffn_att_src"), (k.att_dst, "L0_ffn_att_dst")):
        loads.append((dst[:], everywhere(a[name], GH * GE)))
    for dst, name in ((k.b_gat, "L0_ffn_b_gat"), (k.ln_gamma, "L0_ffn_ln_gamma"), (k.ln_beta, "L0_ffn_ln_beta")):
        loads.append((dst[:], everywhere(a[name], GH * GE)))
    for n, e in ((0, E0), (1, E1)):
        loads += [
            (k.w1[n][0:D], a[f"L{n}_ffn_W1"].rearrange("e d h -> d e h")),
            (k.w1[n][D:D + 1], a[f"L{n}_ffn_b1"].rearrange("(a e) h -> a e h", a=1)),
            (k.w2[n][:], a[f"L{n}_ffn_W2"].rearrange("e h d -> h e d")),
        ]
    for n, (w, b) in enumerate((("Wq", "bq"), ("Wk", "bk"), ("Wv", "bv"), ("Wl", "bl"))):
        loads += [(k.wl1[0:D, n, :], a[f"L1_attn_{w}"]), (k.wl1[D:D + 1, n, :], row(a[f"L1_attn_{b}"]))]
    with nc.Block() as block:
        @block.sync
        def _(sp):
            for dst, src in loads:
                sp.dma_start(dst, src).then_inc(loaded, 16)
            sp.wait_ge(b2_zeroed, 2)
            for n, e in ((0, E0), (1, E1)):
                for t in range(4):
                    sp.dma_start(k.b2[n][t * e:(t + 1) * e, t, :], a[f"L{n}_ffn_b2"]).then_inc(loaded, 16)
            sp.wait_ge(loaded, 16 * (len(loads) + 8))

        @block.vector
        def _(dve):
            for b2 in k.b2:
                dve.memset(b2[:], 0.0).then_inc(b2_zeroed, 1)

        @block.gpsimd
        def _(pool):
            n = 0
            for t, v in ((k.ident, 0.0), (k.eps, EPS), (k.headmask, 1.0),
                         (k.lower, 1.0), (k.lower0, 1.0), (k.zero_mm, 0.0), (reverse, 0.0)):
                pool.memset(t[:], v).then_inc(made, 1)
                n += 1
            pool.iota(k.iota_lo[:], [[1, P]], base=0, channel_multiplier=0,
                      allow_small_or_imprecise_dtypes=True).then_inc(made, 1)
            n += 1
            pool.wait_ge(made, n)
            pool.affine_select(k.ident[:], k.ident[:], [[-1, P]], ALU.not_equal, 1.0, base=0,
                               channel_multiplier=1).then_inc(made, 1)
            pool.affine_select(reverse[:], reverse[:], [[0, 2], [1, WIN]], ALU.not_equal, 1.0,
                               base=1 - WIN, channel_multiplier=1).then_inc(made, 1)
            pool.affine_select(k.headmask[:], k.headmask[:], [[-D, 2], [-HD, NH]], ALU.is_ge, 0.0,
                               base=0, channel_multiplier=1).then_inc(made, 1)
            for t, e in ((k.lower, E1), (k.lower0, E0)):
                pool.affine_select(t[:], t[:], [[1, e], [-1, e]], ALU.is_gt, 0.0, base=0,
                                   channel_multiplier=0).then_inc(made, 1)
            n += 5
            pool.wait_ge(made, n)
            pool.affine_select(k.headmask[:], k.headmask[:], [[D, 2], [HD, NH]], ALU.is_ge, 0.0,
                               base=HD - 1, channel_multiplier=-1).then_inc(made, 1)
            pool.wait_ge(made, n + 1)

    with nc.Block() as block:
        @block.tensor
        def _(pe):
            pe.transpose(turn[:], k.wtok_raw[:], k.ident[0:D, 0:D]).then_inc(turned, 1)
            pe.matmul(bias_ps[:].rearrange("q h j -> q (h j)"), reverse[:].rearrange("r t q -> r (t q)"),
                      bias_rows[:].rearrange("r h j -> r (h j)")).then_inc(turned, 1)

        @block.vector
        def _(dve):
            dve.memset(k.wgat[D:D + 1, :], 0.0)
            dve.tensor_tensor(k.headmask[:, 0, :], k.headmask[:, 0, :], k.headmask[:, 1, :], ALU.add)
            dve.wait_ge(turned, 1)
            dve.tensor_copy(k.wtok[0:D, :], turn[:])
            dve.wait_ge(turned, 2)
            dve.tensor_copy(k.relbias[:], bias_ps[:])


def tokenize(nc, mem, a, k, h):
    rows = a["x"].rearrange("b c (i p) w -> (b c i) (p w)", p=8)
    xrow = [mem.sb(f"xrow{b}", [P, 512]) for b in range(2)]
    patch = [mem.sb(f"patch{b}", [P, 8, D]) for b in range(2)]
    xT = [mem.sb(f"patchT{b}", [D + 1, 1024]) for b in range(2)]
    pT = [mem.ps(f"patchT_ps{b}", [D, 8, P]) for b in range(2)]
    ph = [mem.ps(f"token_ps{b}", [P, 8, D]) for b in range(2)]
    loaded = [mem.sem(f"images_loaded{b}") for b in range(2)]
    ones = mem.sem("patch_ones")
    cut, turned, copied, mapped, saved = (
        mem.sem(f"patch_{x}") for x in ("cut", "turned", "copied", "mapped", "saved"))
    n = 4
    with nc.Block() as block:
        @block.sync
        def _(sp):
            def chunk(c, b, first):
                if not first:
                    sp.wait_ge(cut, c - 1)
                sp.dma_start(xrow[b][:], rows[bass.ts(c, P), :]).then_inc(loaded[b], 16)
            twice(sp, n, chunk)

        @block.tensor
        def _(pe):
            def chunk(c, b, first):
                pe.wait_ge(cut, c + 1)
                if not first:
                    pe.wait_ge(copied, c - 1)
                for j in range(8):
                    ins = pe.transpose(pT[b][:, j, :], patch[b][:, j, :], k.ident[:])
                ins.then_inc(turned, 1)
                pe.wait_ge(copied, c + 1)
                if not first:
                    pe.wait_ge(saved, c - 1)
                else:
                    pe.wait_ge(ones, 2)
                for t in range(8):
                    ins = pe.matmul(ph[b][:, t, :], xT[b][:, t * P:(t + 1) * P], k.wtok[:])
                ins.then_inc(mapped, 1)
            twice(pe, n, chunk)

        @block.scalar
        def _(act):
            def chunk(c, b, first):
                act.wait_ge(turned, c + 1)
                if not first:
                    act.wait_ge(mapped, c - 1)
                act.activation(xT[b][0:D, :].rearrange("k (s j) -> k s j", j=8),
                               pT[b][:].rearrange("k j s -> k s j"), ACT.Copy).then_inc(copied, 1)
            twice(act, n, chunk)

        @block.vector
        def _(dve):
            for b in range(2):
                dve.memset(xT[b][D:D + 1, :], 1.0).then_inc(ones, 1)

            def save(c, b):
                dve.wait_ge(mapped, c + 1)
                dve.tensor_copy(h[:, bass.ts(c, 8), :], ph[b][:]).then_inc(saved, 1)

            def chunk(c, b, first):
                if not first:
                    save(c - 2, b)
                dve.wait_ge(loaded[b], 16 if first else 8 * (c + 2 - b))
                if not first:
                    dve.wait_ge(turned, c - 1)
                dve.tensor_copy(patch[b][:].rearrange("s j (p q) -> s j p q", p=8),
                                xrow[b][:].rearrange("s (p j q) -> s j p q", p=8, j=8)).then_inc(cut, 1)
            twice(dve, n, chunk)
            save(n - 2, 0)
            save(n - 1, 1)


def normalize(nc, mem, k, h, xn, xT, call, projections, weight=None, out=None, affine=None):
    s, xc, sq = k.ln_s, xn, k.big
    step, centered, squared, summed, rooted, scaled, turned, evacuated, kept, mapped, saved = k.ln_sems
    xs, xts, pT, pj = k.ln_xs, k.ln_xts, k.ln_pT, k.ln_pj
    N = weight.shape[-1] if weight is not None else 0
    n = TILES // 4
    calls, chunks, projected = call, call * n, projections * n
    with nc.Block() as block:
        @block.vector
        def _(dve):
            dve.tensor_reduce(s[:, 0, :], h[:], AX.X, ALU.add).then_inc(step, 1)
            dve.wait_ge(step, 3 * calls + 1)
            dve.tensor_scalar(s[:, 1, :], s[:, 0, :], 1.0 / D, None, ALU.mult).then_inc(step, 1)
            dve.wait_ge(step, 3 * calls + 2)
            dve.tensor_tensor(xc[:], h[:], bc(s[:, 1, :], D), ALU.subtract).then_inc(centered, 1)
            dve.wait_ge(squared, calls + 1)
            dve.tensor_reduce(s[:, 2, :], sq[:], AX.X, ALU.add).then_inc(summed, 1)
            dve.wait_ge(rooted, calls + 1)
            dve.reciprocal(s[:, 4, :], s[:, 3, :]).then_inc(step, 1)
            dve.wait_ge(step, 3 * calls + 3)

            def scale(c, b, first):
                if not first:
                    dve.wait_ge(turned, chunks + c - 1)
                dve.tensor_tensor(xs[b][:], xc[:, bass.ts(c, 4), :], bc(s[:, 4, bass.ts(c, 4)], D),
                                  ALU.mult).then_inc(scaled, 1)

            def save(c, b):
                dve.wait_ge(mapped, projected + c + 1)
                dve.tensor_copy(out[:, bass.ts(c, 4), :], pj[b][:, :, 0:N]).then_inc(saved, 1)

            def chunk(c, b, first):
                if N and not first:
                    save(c - 2, b)
                scale(c, b, first)
            twice(dve, n, chunk)
            if N:
                save(n - 2, 0)
                save(n - 1, 1)

        @block.scalar
        def _(act):
            act.wait_ge(centered, calls + 1)
            act.activation(sq[:], xc[:], ACT.Square).then_inc(squared, 1)
            act.wait_ge(summed, calls + 1)
            act.activation(s[:, 3, :], s[:, 2, :], ACT.Sqrt, bias=k.eps[:, 0:1], scale=1.0 / D).then_inc(rooted, 1)

            def chunk(c, b, first):
                act.wait_ge(turned, chunks + c + 1)
                if not first:
                    act.wait_ge(kept, chunks + c - 1)
                    if N:
                        act.wait_ge(mapped, projected + c - 1)
                if affine is None:
                    ins = act.activation(xts[b][0:D, :], pT[b][:], ACT.Copy)
                else:
                    ins = act.activation(xts[b][0:D, :], pT[b][:], ACT.Identity, bias=affine[:, 1:2],
                                         scale=affine[:, 0:1])
                ins.then_inc(evacuated, 1)
            twice(act, n, chunk)

        @block.gpsimd
        def _(pool):
            def chunk(c, b, first):
                pool.wait_ge(evacuated, chunks + c + 1)
                pool.tensor_copy(xT[:, bass.ts(c, 512)], xts[b][:]).then_inc(kept, 1)
            twice(pool, n, chunk)

        @block.tensor
        def _(pe):
            def turn(c, b, first):
                pe.wait_ge(scaled, chunks + c + 1)
                if not first:
                    pe.wait_ge(evacuated, chunks + c - 1)
                pe.sem_inc(k.pe_passed, 1)
                for t in range(4):
                    ins = pe.transpose(pT[b][:, t * P:(t + 1) * P], xs[b][:, t, :], k.ident[:])
                ins.then_inc(turned, 1)

            def project(c, b, first):
                pe.wait_ge(evacuated, chunks + c + 1)
                if not first:
                    pe.wait_ge(saved, projected + c - 1)
                for t in range(4):
                    ins = pe.matmul(pj[b][:, t, 0:N], xts[b][:, t * P:(t + 1) * P], weight)
                ins.then_inc(mapped, 1)

            if not N:
                twice(pe, n, turn)
                return
            turn(0, 0, True)
            turn(1, 1, True)
            project(0, 0, True)
            turn(2, 0, False)
            project(1, 1, True)
            turn(3, 1, False)
            with pe.Fori(2, n // 2) as i:
                for b in range(2):
                    project(2 * i + b - 2, b, False)
                    turn(2 * i + b, b, False)
            project(n - 2, 0, False)
            project(n - 1, 1, False)


def window_attention(nc, mem, k, xT, h):
    xs = [mem.sb(f"wa_x{b}", [D + 1, 2, 2, WIN]) for b in range(2)]
    qk = [mem.sb(f"wa_qk{b}", [P, 2, WIN]) for b in range(2)]
    kbd = [mem.sb(f"wa_kbd{b}", [P, NH, WIN]) for b in range(2)]
    vbd = [mem.sb(f"wa_vbd{b}", [P, 2, NH // 2, 2, HD]) for b in range(2)]
    sc = [mem.sb(f"wa_scores{b}", [P, NH, WIN]) for b in range(2)]
    pr = [mem.sb(f"wa_probs{b}", [P, NH, WIN]) for b in range(2)]
    prT = [mem.sb(f"wa_probsT{b}", [P, NH // 2, P]) for b in range(2)]
    mx = [mem.sb(f"wa_max{b}", [P, NH]) for b in range(2)]
    sm = [mem.sb(f"wa_sum{b}", [P, NH]) for b in range(2)]
    rs = [mem.sb(f"wa_rsum{b}", [P, NH]) for b in range(2)]
    o = [mem.sb(f"wa_o{b}", [P, D]) for b in range(2)]
    oT = [mem.sb(f"wa_oT{b}", [D + 1, P]) for b in range(2)]
    qkv_ps = [mem.ps(f"wa_qkv_ps{b}", [P, 512]) for b in range(2)]
    s_ps = [mem.ps(f"wa_s_ps{b}", [P, NH, WIN]) for b in range(2)]
    t_ps = [mem.ps(f"wa_t_ps{b}", [P, NH // 2, P]) for b in range(2)]
    o_ps = [mem.ps(f"wa_o_ps{b}", [P, 512]) for b in range(2)]
    names = ("x_ready", "qkv_done", "qk_ready", "kbd_ready", "v0_ready", "vbd_ready", "scores_done", "biased",
             "max_done", "shifted", "exp_done", "sum_done", "rsum_done", "probs_turned", "probsT_ready",
             "o_done", "o_scaled", "o_turned", "oT_ready", "proj_done", "added", "zeroed", "ones")
    (x_ready, qkv_done, qk_ready, kbd_ready, v0_ready, vbd_ready, scores_done, biased, max_done, shifted,
     exp_done, sum_done, rsum_done, probs_turned, probsT_ready, o_done, o_scaled, o_turned, oT_ready,
     proj_done, added, zeroed, ones) = (mem.sem("wa_" + x) for x in names)
    n = TILES

    with nc.Block() as block:
        @block.gpsimd
        def _(pool):
            for b in range(2):
                pool.memset(vbd[b][:], 0.0).then_inc(zeroed, 1)

            def take(c, b, first):
                if not first:
                    pool.wait_ge(qkv_done, c - 1)
                pair = xT[:, bass.ts(c, P)].rearrange("d (r s) -> d r s", r=2)
                pool.tensor_copy(xs[b][:], bc_at(pair, 2, 2)).then_inc(x_ready, 1)

            def shift(c, b, first):
                pool.wait_ge(max_done, c + 1)
                pool.tensor_tensor(sc[b][:], sc[b][:], bc(mx[b][:], WIN), ALU.subtract).then_inc(shifted, 1)

            take(0, 0, True)
            take(1, 1, True)
            with pool.Fori(0, n // 2 - 1) as i:
                for b in range(2):
                    shift(2 * i + b, b, False)
                    take(2 * i + b + 2, b, False)
            shift(n - 2, 0, False)
            shift(n - 1, 1, False)

        @block.tensor
        def _(pe):
            def qkv(c, b, first):
                pe.wait_ge(x_ready, c + 1)
                if not first:
                    pe.wait_ge(qk_ready, c - 1)
                    pe.wait_ge(vbd_ready, c - 1)
                pe.sem_inc(k.pe_passed, 1)
                for r in range(2):
                    half = xs[b][:, r, 0, :]
                    for j in range(2):
                        pe.matmul(qkv_ps[b][r * D:(r + 1) * D, j * WIN:(j + 1) * WIN],
                                  k.wqkv[:, j * D:(j + 1) * D], half)
                for r in range(2):
                    both = xs[b][:, r].rearrange("d t s -> d (t s)")
                    ins = pe.matmul(qkv_ps[b][:, (2 + r) * D:(3 + r) * D], both, k.wqkv[:, 2 * D:3 * D])
                ins.then_inc(qkv_done, 1)

            def scores(c, b, first):
                pe.wait_ge(qk_ready, c + 1)
                pe.wait_ge(kbd_ready, c + 1)
                if not first:
                    pe.wait_ge(biased, c - 1)
                pe.sem_inc(k.pe_passed, 1)
                for r in range(2):
                    half = slice(r * D, (r + 1) * D)
                    ins = pe.matmul(s_ps[b][half], qk[b][half, 0, :], kbd[b][half])
                ins.then_inc(scores_done, 1)

            def turn(c, b, first):
                pe.wait_ge(exp_done, c + 1)
                if not first:
                    pe.wait_ge(probsT_ready, c - 1)
                for g in range(NH // 2):
                    ins = pe.transpose(t_ps[b][:, g, :], pr[b][:, 2 * g:2 * g + 2, :], k.ident[:])
                ins.then_inc(probs_turned, 1)

            def values(c, b, first):
                pe.wait_ge(probsT_ready, c + 1)
                pe.wait_ge(vbd_ready, c + 1)
                if not first:
                    pe.wait_ge(added, c - 1)
                for r in range(2):
                    for g in range(NH // 2):
                        ins = pe.matmul(o_ps[b][r * WIN:(r + 1) * WIN, 2 * HD * g:2 * HD * (g + 1)],
                                        prT[b][:, g, r * WIN:(r + 1) * WIN], vbd[b][:, r, g])
                ins.then_inc(o_done, 1)

            def project(c, b, first):
                pe.wait_ge(o_scaled, c + 1)
                pe.sem_inc(k.pe_passed, 1)
                pe.transpose(o_ps[b][0:D, 128:256], o[b][:], k.ident[:]).then_inc(o_turned, 1)
                pe.wait_ge(oT_ready, c + 1)
                pe.matmul(o_ps[b][:, 64:128], oT[b][:], k.wproj[:]).then_inc(proj_done, 1)

            def step(c, b, first):
                turn(c, b, first)
                values(c, b, first)

            pe.wait_ge(ones, 2)
            qkv(0, 0, True)
            scores(0, 0, True)
            qkv(1, 1, True)
            scores(1, 1, True)
            step(0, 0, True)
            qkv(2, 0, False)
            scores(2, 0, False)
            step(1, 1, True)
            project(0, 0, True)
            qkv(3, 1, False)
            scores(3, 1, False)
            with pe.Fori(1, n // 2 - 1) as i:
                for b in range(2):
                    step(2 * i + b, b, False)
                    project(2 * i + b - 1, 1 - b, False)
                    qkv(2 * i + b + 2, b, False)
                    scores(2 * i + b + 2, b, False)
            step(n - 2, 0, False)
            project(n - 3, 1, False)
            step(n - 1, 1, False)
            project(n - 2, 0, False)
            project(n - 1, 1, False)

        @block.scalar
        def _(act):
            act.wait_ge(zeroed, 2)

            def inputs(c, b, first):
                act.wait_ge(qkv_done, c + 1)
                if not first:
                    act.wait_ge(scores_done, c - 1)
                    act.wait_ge(o_done, c - 1)
                act.activation(qk[b][:].rearrange("d j s -> d (j s)"), qkv_ps[b][:, 0:2 * WIN],
                               ACT.Copy).then_inc(qk_ready, 1)
                v = qkv_ps[b][:, 2 * D:4 * D].rearrange("s (r g t d) -> s r g t d", r=2, t=2, d=HD)
                for t in range(2):
                    half = slice(t * WIN, (t + 1) * WIN)
                    act.activation(vbd[b][half, :, :, t, :], v[half, :, :, t, :], ACT.Copy)\
                       .then_inc((v0_ready, vbd_ready)[t], 1)

            def probs(c, b, first):
                act.wait_ge(shifted, c + 1)
                if not first:
                    act.wait_ge(probs_turned, c - 1)
                    act.wait_ge(sum_done, c - 1)
                act.activation(pr[b][:], sc[b][:], ACT.Exp).then_inc(exp_done, 1)

            def turned(c, b, first):
                act.wait_ge(probs_turned, c + 1)
                if not first:
                    act.wait_ge(o_done, c - 1)
                act.activation(prT[b][:], t_ps[b][:], ACT.Copy).then_inc(probsT_ready, 1)

            def outT(c, b, first):
                act.wait_ge(o_turned, c + 1)
                act.activation(oT[b][0:D, :], o_ps[b][0:D, 128:256], ACT.Copy).then_inc(oT_ready, 1)

            inputs(0, 0, True)
            inputs(1, 1, True)
            probs(0, 0, True)
            turned(0, 0, True)
            inputs(2, 0, False)
            probs(1, 1, True)
            turned(1, 1, True)
            outT(0, 0, True)
            inputs(3, 1, False)
            with act.Fori(1, n // 2 - 1) as i:
                for b in range(2):
                    probs(2 * i + b, b, False)
                    turned(2 * i + b, b, False)
                    outT(2 * i + b - 1, 1 - b, False)
                    inputs(2 * i + b + 2, b, False)
            probs(n - 2, 0, False)
            turned(n - 2, 0, False)
            outT(n - 3, 1, False)
            probs(n - 1, 1, False)
            turned(n - 1, 1, False)
            outT(n - 2, 0, False)
            outT(n - 1, 1, False)

        @block.vector
        def _(dve):
            def keys(c, b, first):
                dve.wait_ge(qk_ready, c + 1)
                if not first:
                    dve.wait_ge(scores_done, c - 1)
                dve.tensor_tensor(kbd[b][:], bc_at(qk[b][:, 1, :], 1, NH),
                                  bc(k.headmask[:, 0, :], WIN), ALU.mult).then_inc(kbd_ready, 1)

            def bias(c, b, first):
                dve.wait_ge(scores_done, c + 1)
                if not first:
                    dve.wait_ge(exp_done, c - 1)
                dve.scalar_tensor_tensor(sc[b][:], s_ps[b][:], float(HD) ** -0.5, k.relbias[:], ALU.mult,
                                         ALU.add).then_inc(biased, 1)
                dve.wait_ge(biased, c + 1)
                if not first:
                    dve.wait_ge(shifted, c - 1)
                dve.tensor_reduce(mx[b][:], sc[b][:], AX.X, ALU.max).then_inc(max_done, 1)

            def sums(c, b, first):
                dve.wait_ge(exp_done, c + 1)
                dve.tensor_reduce(sm[b][:], pr[b][:], AX.X, ALU.add).then_inc(sum_done, 1)
                dve.wait_ge(sum_done, c + 1)
                dve.reciprocal(rs[b][:], sm[b][:]).then_inc(rsum_done, 1)

            def scale(c, b, first):
                dve.wait_ge(rsum_done, c + 1)
                dve.wait_ge(o_done, c + 1)
                if not first:
                    dve.wait_ge(o_turned, c - 1)
                dve.tensor_tensor(o[b][:].rearrange("q (h d) -> q h d", d=HD),
                                  o_ps[b][:, 0:D].rearrange("q (h d) -> q h d", d=HD),
                                  bc(rs[b][:], HD), ALU.mult).then_inc(o_scaled, 1)

            def add(c, b, first):
                dve.wait_ge(proj_done, c + 1)
                dve.tensor_tensor(h[:, bass.ds(c, 1), :].rearrange("p a d -> p (a d)"),
                                  h[:, bass.ds(c, 1), :].rearrange("p a d -> p (a d)"),
                                  o_ps[b][:, 64:128], ALU.add).then_inc(added, 1)

            for b in range(2):
                dve.memset(oT[b][D:D + 1, :], 1.0).then_inc(ones, 1)
            keys(0, 0, True)
            bias(0, 0, True)
            keys(1, 1, True)
            bias(1, 1, True)
            sums(0, 0, True)
            keys(2, 0, False)
            scale(0, 0, True)
            bias(2, 0, False)
            sums(1, 1, True)
            keys(3, 1, False)
            scale(1, 1, True)
            bias(3, 1, False)
            with dve.Fori(1, n // 2 - 1) as i:
                for b in range(2):
                    sums(2 * i + b, b, False)
                    add(2 * i + b - 2, b, False)
                    keys(2 * i + b + 2, b, False)
                    scale(2 * i + b, b, False)
                    bias(2 * i + b + 2, b, False)
            sums(n - 2, 0, False)
            add(n - 4, 0, False)
            scale(n - 2, 0, False)
            sums(n - 1, 1, False)
            add(n - 3, 1, False)
            scale(n - 1, 1, False)
            add(n - 2, 0, False)
            add(n - 1, 1, False)



def sort_edges(nc, mem, a, k, keys, start_end, counts):
    src, dst = mem.sb("edge_src", [P, EC], I32), mem.sb("edge_dst", [P, EC], I32)
    other = mem.sb("sort_other", [P, EC])
    work = mem.sb("sort_work", [P, EC])
    stat, top = mem.sb("edge_stat", [P, 4]), mem.sb("edge_top", [P, 4])
    lim = mem.sb("edge_limits", [P, 4], I32)
    loaded = mem.sem("edges_loaded")
    step = mem.sem("sort_step")
    counted, reduced = mem.sem("classes_counted"), mem.sem("classes_reduced")
    edges = a["L0_ffn_edge_index"].rearrange("a (p c) -> a p c", p=P)
    with nc.Block() as block:
        @block.sync
        def _(sp):
            sp.dma_start(src[:], edges[0]).then_inc(loaded, 16)
            sp.dma_start(dst[:], edges[1]).then_inc(loaded, 16)

        @block.vector
        def _(dve):
            done = 0

            def after(ins):
                nonlocal done
                ins.then_inc(step, 1)
                done += 1
                dve.wait_ge(step, done)

            A, B, C = keys[:, 0:EC], other[:], work[:]
            dve.wait_ge(loaded, 32)
            after(dve.tensor_scalar(A, src[:], float(M - 1), None, ALU.min))
            after(dve.scalar_tensor_tensor(B, dst[:], float(M), A, ALU.mult, ALU.add))
            after(dve.tensor_scalar(C, dst[:], float(2 - M), CLASS_LAST - (M - 1), ALU.mult, ALU.add))
            after(dve.scalar_tensor_tensor(C, A, float(M - 1), C, ALU.is_equal, ALU.mult))
            after(dve.tensor_tensor(B, B, C, ALU.add))
            after(dve.tensor_scalar(C, dst[:], float(M), CLASS_NONE, ALU.is_ge, ALU.mult))
            after(dve.tensor_tensor(A, B, C, ALU.max))
            cur, nxt = A, B
            run = 2
            while run <= EC:
                x = cur.rearrange("p (n r) -> p n r", r=run)
                y = nxt.rearrange("p (n r) -> p n r", r=run)
                low, high = slice(0, run // 2), slice(run - 1, run // 2 - 1, -1)
                dve.tensor_tensor(y[:, :, low], x[:, :, low], x[:, :, high], ALU.min).then_inc(step, 1)
                done += 1
                after(dve.tensor_tensor(y[:, :, high], x[:, :, low], x[:, :, high], ALU.max))
                cur, nxt = nxt, cur
                dist = run // 4
                while dist:
                    x = cur.rearrange("p (n t r) -> p n t r", t=2, r=dist)
                    y = nxt.rearrange("p (n t r) -> p n t r", t=2, r=dist)
                    dve.tensor_tensor(y[:, :, 0], x[:, :, 0], x[:, :, 1], ALU.min).then_inc(step, 1)
                    done += 1
                    after(dve.tensor_tensor(y[:, :, 1], x[:, :, 0], x[:, :, 1], ALU.max))
                    cur, nxt = nxt, cur
                    dist //= 2
                run *= 2
            assert cur is A, "the sorted keys are in their place"
            after(dve.tensor_scalar(C, A, CLASS_LAST, 0.0, ALU.is_lt, ALU.add, accum_out=stat[:, 0:1]))
            after(dve.tensor_scalar(C, A, CLASS_NONE, 0.0, ALU.is_lt, ALU.add, accum_out=stat[:, 1:2]))
            dve.tensor_scalar(stat[:, 2:3], stat[:, 0:1], -1.0, None, ALU.mult).then_inc(counted, 1)
            dve.wait_ge(reduced, 1)
            after(dve.tensor_scalar(lim[:, 0:1], top[:, 0:1], -1.0, None, ALU.add))
            after(dve.tensor_scalar(lim[:, 1:2], top[:, 1:2], float(2 * CCH - 1), None, ALU.add))
            after(dve.tensor_scalar(lim[:, 2:3], top[:, 2:3], -1.0, float(EC - 1), ALU.mult, ALU.min))
            sh = (2 * GCH).bit_length() - 1
            after(dve.tensor_scalar(lim[:, 0:1], lim[:, 0:1], sh, None, ALU.arith_shift_right))
            sh = (2 * CCH).bit_length() - 1
            after(dve.tensor_scalar(lim[:, 1:3], lim[:, 1:3], sh, None, ALU.arith_shift_right))
            after(dve.tensor_scalar(start_end[:, 0:1], lim[:, 0:1], 1.0, None, ALU.max))
            after(dve.tensor_tensor(lim[:, 3:4], lim[:, 1:2], lim[:, 2:3], ALU.subtract))
            after(dve.tensor_scalar(start_end[:, 1:2], lim[:, 3:4], 1.0, None, ALU.max))
            after(dve.tensor_copy(start_end[:, 2:3], lim[:, 2:3]))

        @block.gpsimd
        def _(pool):
            pool.wait_ge(counted, 1)
            pool.partition_all_reduce(top[:, 0:3], stat[:, 0:3], P, bass.bass_isa.ReduceOp.max).then_inc(reduced, 1)


def count_last(nc, mem, k, keys, start_end, counts):
    work = [mem.sb(f"count_int{b}", [P, CCH], I32) for b in range(2)]
    dst = [mem.sb(f"count_dst{b}", [P, CCH], I32) for b in range(2)]
    lo = [mem.sb(f"count_lo{b}", [P, CCH], I32) for b in range(2)]
    hi = [mem.sb(f"count_hi{b}", [P, CCH], I32) for b in range(2)]
    olo = [mem.sb(f"count_onehot_lo{b}", [P, CCH, P], BF16) for b in range(2)]
    ohi = [mem.sb(f"count_onehot_hi{b}", [P, CCH, TILES], BF16) for b in range(2)]
    zero = mem.sb("count_zero", [P, P], BF16)
    acc = mem.ps("count_acc", [P, TILES])
    zeroed, split, lo_ready, hi_ready, used, summed, step = (
        mem.sem(f"count_{x}") for x in ("zeroed", "split", "lo_ready", "hi_ready", "used", "summed", "step"))
    with nc.Block() as block:
        @block.vector
        def _(dve):
            dve.memset(zero[:], 0.0).then_inc(zeroed, 1)
            n = dve.value_load(start_end[0:1, 1:2], min_val=1, max_val=EC // (2 * CCH))
            at = dve.value_load(start_end[0:1, 2:3], min_val=0, max_val=EC // (2 * CCH) - 1)
            with dve.Fori(0, n) as i:
                pair = nc.s_assert_within(at + i, 0, EC // (2 * CCH) - 1)
                for b in range(2):
                    c = 2 * i + b
                    dve.wait_ge(used, c + 1)
                    dve.tensor_scalar(work[b][:], keys[:, bass.ds(pair * (2 * CCH) + b * CCH, CCH)],
                                      CLASS_LAST, None, ALU.subtract).then_inc(step, 1)
                    dve.wait_ge(step, 2 * c + 1)
                    dve.tensor_scalar(lo[b][:], work[b][:], 1, P - 1, ALU.arith_shift_right,
                                      ALU.bitwise_and).then_inc(split, 1)
                    dve.tensor_scalar(hi[b][:], work[b][:], 8, None, ALU.arith_shift_right).then_inc(step, 1)
                    dve.wait_ge(split, c + 1)
                    dve.tensor_tensor(olo[b][:], bc_at(k.iota_lo[:], 1, CCH), bc(lo[b][:], P),
                                      ALU.is_equal).then_inc(lo_ready, 1)
                    dve.wait_ge(step, 2 * c + 2)
                    dve.tensor_tensor(ohi[b][:], bc_at(k.iota_lo[:, 0:TILES], 1, CCH), bc(hi[b][:], TILES),
                                      ALU.is_equal).then_inc(hi_ready, 1)
            dve.wait_ge(summed, 1)
            dve.tensor_copy(counts[:], acc[:])

        @block.tensor
        def _(pe):
            pe.sem_inc(used, 2)
            n = pe.value_load(start_end[0:1, 1:2], min_val=1, max_val=EC // (2 * CCH))
            pe.wait_ge(zeroed, 1)
            pe.matmul(acc[:], zero[:], zero[:, 0:TILES], start=True, stop=False, skip_group_check=True)
            with pe.Fori(0, n) as i:
                for b in range(2):
                    pe.wait_ge(lo_ready, 2 * i + b + 1)
                    pe.wait_ge(hi_ready, 2 * i + b + 1)
                    for j in range(CCH):
                        ins = pe.matmul(acc[:], olo[b][:, j, :], ohi[b][:, j, :], start=False, stop=False,
                                        skip_group_check=True)
                    ins.then_inc(used, 1)
            pe.matmul(acc[:], zero[:], zero[:, 0:TILES], start=False, stop=True,
                      skip_group_check=True).then_inc(summed, 1)


def graph_router(nc, mem, a, k, hg, keys, start_end, counts, gates):
    W = GH * GE
    srow, drow = mem.sb("src_rows", [P, TILES, NSRC]), mem.sb("dst_rows", [P, TILES, NDST])
    srow_dram = nc.dram_tensor("src_rows_dram", (M, NSRC), F32, kind="Internal").ap()
    drow_dram = nc.dram_tensor("dst_rows_dram", (M, NDST), F32, kind="Internal").ap()
    last = mem.sb("last_row", [P, NSRC])
    prod = mem.sb("router_prod", [P, TILES, W])
    e = mem.sb("router_e", [P, 3, TILES, GH])
    mx, top = mem.sb("src_max", [P, GH]), mem.sb("src_top", [P, GH])
    own = mem.sb("own_values", [P, TILES, GH, GE + 1])
    step = mem.sem("nodes_step")
    src_ready, dst_ready, max_ready, top_ready = (
        mem.sem(x) for x in ("src_rows_ready", "dst_rows_ready", "src_max_ready", "src_top_ready"))
    src_stored, last_loaded, dst_stored = mem.sem("src_rows_stored"), mem.sem("last_row_loaded"), mem.sem("dst_rows_stored")
    self_shift, last_shift, self_exp, last_exp = (
        mem.sem(x) for x in ("self_shifted", "last_shifted", "self_exp", "last_exp"))
    sview = srow[:, :, W:NSRC]
    dview, mview = drow[:, :, 0:GH], drow[:, :, GH:NDST]
    with nc.Block() as block:
        @block.vector
        def _(dve):
            done = 0

            def after(ins):
                nonlocal done
                ins.then_inc(step, 1)
                done += 1
                dve.wait_ge(step, done)

            after(dve.tensor_tensor(prod[:], hg[:], bc_at(k.att_src[:], 1, TILES), ALU.mult))
            dve.tensor_copy(srow[:, :, 0:W], hg[:]).then_inc(src_ready, 1)
            dve.tensor_reduce(sview, prod[:].rearrange("p t (h e) -> p t h e", e=GE), AX.X,
                              ALU.add).then_inc(src_ready, 1)
            dve.wait_ge(src_ready, 2)
            dve.tensor_reduce(mx[:], sview.rearrange("p t h -> p h t"), AX.X, ALU.max).then_inc(max_ready, 1)
            after(dve.tensor_tensor(prod[:], hg[:], bc_at(k.att_dst[:], 1, TILES), ALU.mult))
            after(dve.tensor_reduce(dview, prod[:].rearrange("p t (h e) -> p t h e", e=GE), AX.X, ALU.add))
            dve.wait_ge(top_ready, 1)
            after(dve.tensor_tensor(e[:, 0], dview, bc_at(top[:], 1, TILES), ALU.add))
            dve.scalar_tensor_tensor(mview, e[:, 0], 0.2, e[:, 0], ALU.mult, ALU.max).then_inc(dst_ready, 1)
            dve.wait_ge(dst_ready, 1)
            after(dve.tensor_tensor(e[:, 0], dview, sview, ALU.add))
            after(dve.scalar_tensor_tensor(e[:, 1], e[:, 0], 0.2, e[:, 0], ALU.mult, ALU.max))
            dve.tensor_tensor(e[:, 0], e[:, 1], mview, ALU.subtract).then_inc(self_shift, 1)
            dve.wait_ge(last_loaded, 16)
            dve.wait_ge(self_shift, 1)
            after(dve.tensor_tensor(e[:, 1], dview, bc_at(last[:, W:NSRC], 1, TILES), ALU.add))
            after(dve.scalar_tensor_tensor(e[:, 2], e[:, 1], 0.2, e[:, 1], ALU.mult, ALU.max))
            dve.tensor_tensor(e[:, 1], e[:, 2], mview, ALU.subtract).then_inc(last_shift, 1)
            dve.wait_ge(last_exp, 1)
            after(dve.tensor_tensor(e[:, 1], e[:, 1], bc(counts[:], GH), ALU.mult))
            dve.wait_ge(self_exp, 1)
            dve.tensor_tensor(own[:, :, :, GE], e[:, 0], e[:, 1], ALU.add).then_inc(step, 1)
            done += 1
            after(dve.tensor_tensor(own[:, :, :, 0:GE], hg[:].rearrange("p t (h e) -> p t h e", e=GE),
                                    bc(e[:, 0], GE), ALU.mult))
            for hh in range(GH):
                after(dve.tensor_tensor(prod[:, :, hh * GE:(hh + 1) * GE],
                                        bc_at(last[:, hh * GE:(hh + 1) * GE], 1, TILES),
                                        bc(e[:, 1, :, hh], GE), ALU.mult))
            after(dve.tensor_tensor(own[:, :, :, 0:GE], own[:, :, :, 0:GE],
                                    prod[:].rearrange("p t (h e) -> p t h e", e=GE), ALU.add))

        @block.scalar
        def _(act):
            act.wait_ge(self_shift, 1)
            act.activation(e[:, 0], e[:, 0], ACT.Exp).then_inc(self_exp, 1)
            act.wait_ge(last_shift, 1)
            act.activation(e[:, 1], e[:, 1], ACT.Exp).then_inc(last_exp, 1)

        @block.gpsimd
        def _(pool):
            pool.wait_ge(max_ready, 1)
            pool.partition_all_reduce(top[:], mx[:], P, bass.bass_isa.ReduceOp.max).then_inc(top_ready, 1)

        @block.sync
        def _(sp):
            sp.wait_ge(src_ready, 2)
            sp.dma_start(srow_dram.rearrange("(t p) f -> p t f", p=P), srow[:]).then_inc(src_stored, 16)
            sp.wait_ge(src_stored, 16)
            sp.dma_start(last[:], bass.AP(srow_dram.tensor, (M - 1) * NSRC, [[0, P], [1, NSRC]]))\
              .then_inc(last_loaded, 16)
            sp.wait_ge(dst_ready, 1)
            sp.dma_start(drow_dram.rearrange("(t p) f -> p t f", p=P), drow[:]).then_inc(dst_stored, 16)
            sp.wait_ge(dst_stored, 16)

    ki = [mem.sb(f"edge_key{b}", [P, GCH], I32) for b in range(2)]
    si = [mem.sb(f"edge_src_index{b}", [P, GCH], I32) for b in range(2)]
    dr = [mem.sb(f"edge_dst_raw{b}", [P, GCH], I32) for b in range(2)]
    di = [mem.sb(f"edge_dst_index{b}", [P, GCH], I32) for b in range(2)]
    lo = [mem.sb(f"edge_lo{b}", [P, GCH], I32) for b in range(2)]
    hi = [mem.sb(f"edge_hi{b}", [P, GCH], I32) for b in range(2)]
    olo = [mem.sb(f"edge_onehot_lo{b}", [P, GCH, P]) for b in range(2)]
    ohi = [mem.sb(f"edge_onehot_hi{b}", [P, GCH, TILES]) for b in range(2)]
    gs = [mem.sb(f"edge_src_row{b}", [P, GCH, NSRC]) for b in range(2)]
    gd = [mem.sb(f"edge_dst_row{b}", [P, GCH, NDST]) for b in range(2)]
    ee = [mem.sb(f"edge_e{b}", [P, 2, GCH, GH]) for b in range(2)]
    val = [mem.sb(f"edge_values{b}", [P, GCH, GH, GE + 1]) for b in range(2)]
    spread = [mem.sb(f"edge_spread{b}", [P, GCH, TILES, NV]) for b in range(2)]
    acc = mem.ps("edge_acc", [P, 2, 512])
    HALF = TILES // 2 * NV
    (key_ready, src_index, dst_raw, dst_index, lo_ready, hi_ready, olo_ready, ohi_ready, added, leaky, shifted,
     exp_done, weighted, spread_ready, used, summed) = (mem.sem("edge_" + x) for x in (
         "key_ready", "src_index", "dst_raw", "dst_index", "lo_ready", "hi_ready", "olo_ready", "ohi_ready",
         "added", "leaky", "shifted", "exp_done", "weighted", "spread_ready", "used", "summed"))
    gathered = [mem.sem(f"edge_gathered{b}") for b in range(2)]
    PAIRS = EC // (2 * GCH)

    with nc.Block() as block:
        @block.vector
        def _(dve):
            def index(c, b, first):
                if not first:
                    dve.wait_ge(weighted, c - 1)
                    dve.wait_ge(used, c - 1)
                dve.tensor_copy(ki[b][:], keys[:, bass.ts(c, GCH)]).then_inc(key_ready, 1)
                dve.wait_ge(key_ready, c + 1)
                dve.tensor_scalar(si[b][:], ki[b][:], M - 1, None, ALU.bitwise_and).then_inc(src_index, 1)
                dve.tensor_scalar(dr[b][:], ki[b][:], 12, None, ALU.arith_shift_right).then_inc(dst_raw, 1)
                dve.wait_ge(dst_raw, c + 1)
                dve.tensor_scalar(di[b][:], dr[b][:], float(M - 1), None, ALU.min).then_inc(dst_index, 1)
                dve.tensor_scalar(lo[b][:], dr[b][:], P - 1, None, ALU.bitwise_and).then_inc(lo_ready, 1)
                dve.tensor_scalar(hi[b][:], dr[b][:], 7, None, ALU.arith_shift_right).then_inc(hi_ready, 1)
                dve.wait_ge(lo_ready, c + 1)
                dve.tensor_tensor(olo[b][:], bc_at(k.iota_lo[:], 1, GCH), bc(lo[b][:], P),
                                  ALU.is_equal).then_inc(olo_ready, 1)
                dve.wait_ge(hi_ready, c + 1)
                dve.tensor_tensor(ohi[b][:], bc_at(k.iota_lo[:, 0:TILES], 1, GCH), bc(hi[b][:], TILES),
                                  ALU.is_equal).then_inc(ohi_ready, 1)

            def values(c, b, turn):
                dve.wait_ge(gathered[b], turn)
                dve.tensor_tensor(ee[b][:, 0], gs[b][:, :, W:NSRC], gd[b][:, :, 0:GH], ALU.add).then_inc(added, 1)
                dve.wait_ge(added, c + 1)
                dve.scalar_tensor_tensor(ee[b][:, 1], ee[b][:, 0], 0.2, ee[b][:, 0], ALU.mult,
                                         ALU.max).then_inc(leaky, 1)
                dve.wait_ge(leaky, c + 1)
                dve.tensor_tensor(ee[b][:, 0], ee[b][:, 1], gd[b][:, :, GH:NDST], ALU.subtract).then_inc(shifted, 1)
                dve.wait_ge(exp_done, c + 1)
                dve.tensor_tensor(val[b][:, :, :, 0:GE], gs[b][:, :, 0:W].rearrange("p c (h e) -> p c h e", e=GE),
                                  bc(val[b][:, :, :, GE], GE), ALU.mult).then_inc(weighted, 1)
                dve.wait_ge(weighted, c + 1)
                dve.wait_ge(ohi_ready, c + 1)
                dve.tensor_tensor(spread[b][:], bc_at(val[b][:].rearrange("p c h e -> p c (h e)"), 2, TILES),
                                  bc(ohi[b][:], NV), ALU.mult).then_inc(spread_ready, 1)

            n = dve.value_load(start_end[0:1, 0:1], min_val=1, max_val=PAIRS - 1)
            index(0, 0, True)
            index(1, 1, True)
            with dve.Fori(1, n + 1) as i:
                for b in range(2):
                    values(2 * i + b - 2, b, 256 * i)
                    index(2 * i + b, b, False)
            for b in range(2):
                values(2 * n + b, b, 256 * n + 256)

        @block.gpsimd
        def _(pool):
            def gather(c, b, first):
                pool.wait_ge(src_index, c + 1)
                pool.wait_ge(dst_index, c + 1)
                if not first:
                    pool.wait_ge(weighted, c - 1)
                pool.sem_inc(k.pool_passed, 1)
                for j in range(GCH):
                    pool.indirect_dma_start(gs[b][:, j, :], None, srow_dram,
                                            bass.IndirectOffsetOnAxis(si[b][:, j:j + 1], axis=0))\
                        .then_inc(gathered[b], 16)
                    pool.indirect_dma_start(gd[b][:, j, :], None, drow_dram,
                                            bass.IndirectOffsetOnAxis(di[b][:, j:j + 1], axis=0))\
                        .then_inc(gathered[b], 16)

            pool.wait_ge(dst_stored, 16)
            n = pool.value_load(start_end[0:1, 0:1], min_val=1, max_val=PAIRS - 1)
            gather(0, 0, True)
            gather(1, 1, True)
            with pool.Fori(1, n + 1) as i:
                for b in range(2):
                    gather(2 * i + b, b, False)

        @block.scalar
        def _(act):
            def exps(c, b, first):
                act.wait_ge(shifted, c + 1)
                if not first:
                    act.wait_ge(spread_ready, c - 1)
                act.activation(val[b][:, :, :, GE], ee[b][:, 0], ACT.Exp).then_inc(exp_done, 1)

            n = act.value_load(start_end[0:1, 0:1], min_val=1, max_val=PAIRS - 1)
            exps(0, 0, True)
            exps(1, 1, True)
            with act.Fori(1, n + 1) as i:
                for b in range(2):
                    exps(2 * i + b, b, False)

        @block.tensor
        def _(pe):
            def sums(c, b, first):
                pe.wait_ge(olo_ready, c + 1)
                pe.wait_ge(spread_ready, c + 1)
                for j in range(GCH):
                    rows = spread[b][:, j].rearrange("p t v -> p (t v)")
                    for half in range(2):
                        ins = pe.matmul(acc[:, half, 0:HALF], olo[b][:, j, :],
                                        rows[:, half * HALF:(half + 1) * HALF], start=False, stop=False,
                                        skip_group_check=True)
                ins.then_inc(used, 1)

            n = pe.value_load(start_end[0:1, 0:1], min_val=1, max_val=PAIRS - 1)
            for half in range(2):
                pe.matmul(acc[:, half, 0:HALF], k.zero_mm[:, 0:P], k.zero_mm[:, 0:HALF], start=True, stop=False,
                          skip_group_check=True)
            sums(0, 0, True)
            sums(1, 1, True)
            with pe.Fori(1, n + 1) as i:
                for b in range(2):
                    sums(2 * i + b, b, False)
            for half in range(2):
                pe.matmul(acc[:, half, 0:HALF], k.zero_mm[:, 0:P], k.zero_mm[:, 0:HALF], start=False, stop=True,
                          skip_group_check=True).then_inc(summed, 1)

    agg, nrm, sq = mem.sb("agg", [P, TILES, W]), mem.sb("agg_norm", [P, TILES, W]), mem.sb("agg_sq", [P, TILES, W])
    st = mem.sb("agg_stats", [P, 5, TILES])
    scores = mem.sb("router_scores", [P, TILES, E0])
    rden = mem.sb("router_rden", [P, TILES, GH])
    centered, squared, var_ready, std_ready = (
        mem.sem(f"agg_{x}") for x in ("centered", "squared", "var_ready", "std_ready"))
    fstep = mem.sem("agg_step")
    with nc.Block() as block:
        @block.vector
        def _(dve):
            done = 0

            def after(ins):
                nonlocal done
                ins.then_inc(fstep, 1)
                done += 1
                dve.wait_ge(fstep, done)

            for half in range(2):
                part = own[:, half * 16:(half + 1) * 16].rearrange("p t h e -> p (t h e)")
                after(dve.tensor_tensor(part, part, acc[:, half, 0:HALF], ALU.add))
            after(dve.tensor_scalar(rden[:], own[:, :, :, GE], 1e-16, None, ALU.add))
            after(dve.reciprocal(rden[:], rden[:]))
            after(dve.tensor_tensor(agg[:].rearrange("p t (h e) -> p t h e", e=GE), own[:, :, :, 0:GE],
                                    bc(rden[:], GE), ALU.mult))
            after(dve.tensor_tensor(agg[:], agg[:], bc_at(k.b_gat[:], 1, TILES), ALU.add))
            after(dve.tensor_reduce(st[:, 0], agg[:], AX.X, ALU.add))
            after(dve.tensor_scalar(st[:, 1], st[:, 0], 1.0 / W, None, ALU.mult))
            dve.tensor_tensor(nrm[:], agg[:], bc(st[:, 1], W), ALU.subtract).then_inc(centered, 1)
            dve.wait_ge(squared, 1)
            dve.tensor_reduce(st[:, 2], sq[:], AX.X, ALU.add).then_inc(var_ready, 1)
            dve.wait_ge(std_ready, 1)
            after(dve.reciprocal(st[:, 4], st[:, 3]))
            after(dve.tensor_tensor(agg[:], nrm[:], bc(st[:, 4], W), ALU.mult))
            after(dve.tensor_tensor(agg[:], agg[:], bc_at(k.ln_gamma[:], 1, TILES), ALU.mult))
            after(dve.tensor_tensor(agg[:], agg[:], bc_at(k.ln_beta[:], 1, TILES), ALU.add))
            after(dve.tensor_reduce(scores[:], agg[:].rearrange("p t (h e) -> p t e h", e=GE), AX.X, ALU.add))
            after(dve.tensor_scalar(scores[:], scores[:], 1.0 / GH, None, ALU.mult))

        @block.scalar
        def _(act):
            act.wait_ge(centered, 1)
            act.activation(sq[:], nrm[:], ACT.Square).then_inc(squared, 1)
            act.wait_ge(var_ready, 1)
            act.activation(st[:, 3], st[:, 2], ACT.Sqrt, bias=k.eps[:, 0:1], scale=1.0 / W).then_inc(std_ready, 1)

    choose(nc, mem, k.lower0, E0, scores, gates, "moe0")


def choose(nc, mem, lower, E, scores, gates, name):
    ahead, same = mem.sb(f"{name}_ahead", [P, TILES, E, E]), mem.sb(f"{name}_same", [P, TILES, E, E])
    sel, z = mem.sb(f"{name}_sel", [P, TILES, E]), mem.sb(f"{name}_z", [P, TILES, E])
    s = mem.sb(f"{name}_top", [P, 3, TILES])
    step, shifted, exp_done = (mem.sem(f"{name}_choose_{x}") for x in ("step", "shifted", "exp_done"))
    with nc.Block() as block:
        @block.vector
        def _(dve):
            done = 0

            def after(ins):
                nonlocal done
                ins.then_inc(step, 1)
                done += 1
                dve.wait_ge(step, done)

            after(dve.tensor_reduce(s[:, 0], scores[:], AX.X, ALU.max))
            dve.tensor_tensor(z[:], scores[:], bc(s[:, 0], E), ALU.subtract).then_inc(shifted, 1)
            others, own = bc_at(scores[:], 2, E), bc(scores[:], E)
            after(dve.tensor_tensor(same[:], others, own, ALU.is_equal))
            low = lower[:].rearrange("p e j -> p (e j)")
            after(dve.tensor_tensor(same[:].rearrange("p t e j -> p t (e j)"),
                                    same[:].rearrange("p t e j -> p t (e j)"), bc_at(low, 1, TILES), ALU.mult))
            after(dve.tensor_tensor(ahead[:], others, own, ALU.is_gt))
            after(dve.tensor_tensor(ahead[:], ahead[:], same[:], ALU.add))
            after(dve.tensor_reduce(sel[:], ahead[:], AX.X, ALU.add))
            dve.wait_ge(exp_done, 1)
            after(dve.scalar_tensor_tensor(sel[:], sel[:], 2.0, z[:], ALU.is_lt, ALU.mult))
            after(dve.tensor_reduce(s[:, 1], sel[:], AX.X, ALU.add))
            after(dve.reciprocal(s[:, 2], s[:, 1]))
            after(dve.tensor_tensor(gates[:], sel[:], bc(s[:, 2], E), ALU.mult))

        @block.scalar
        def _(act):
            act.wait_ge(shifted, 1)
            act.activation(z[:], z[:], ACT.Exp).then_inc(exp_done, 1)


def experts(nc, mem, k, layer, E, xT, gates, h):
    w1, w2, b2 = k.w1[layer], k.w2[layer], k.b2[layer]
    nm = f"moe{layer}_"
    g = mem.sb(nm + "g", [P, 4, E])
    gT = mem.sb(nm + "gT", [4 * E, P])
    hs = [mem.sb(f"{nm}hidden{b}", [P, 512]) for b in range(2)]
    tmp = [mem.sb(f"{nm}weighted{b}", [P, 4, D]) for b in range(2)]
    acc = mem.sb(nm + "acc", [P, 4, D])
    h_ps = [mem.ps(f"{nm}h_ps{b}", [P, 512]) for b in range(2)]
    y_ps = [mem.ps(f"{nm}y_ps{b}", [P, 4, D]) for b in range(2)]
    g_ps = mem.ps(nm + "g_ps", [4 * E, P])
    b_ps = mem.ps(nm + "b_ps", [P, 4, D])
    (g_ready, g_turned, gT_ready, b_done, acc_ready, h_done, gelu_done, y_done, weighted, added) = (
        mem.sem(nm + x) for x in ("g_ready", "g_turned", "gT_ready", "b_done", "acc_ready", "h_done", "gelu_done",
                                  "y_done", "weighted", "added"))
    n = TILES // 4
    with nc.Block() as block:
        @block.tensor
        def _(pe):
            pe.sem_inc(y_done, 2)
            with pe.Fori(0, n) as c:
                u = c * E

                def hidden(e):
                    pe.wait_ge(gelu_done, u + e + 1)
                    ins = pe.matmul(h_ps[e % 2][:], w1[:, e, :], xT[:, bass.ts(c, 512)])
                    ins.then_inc(h_done, 1)

                def output(e):
                    pe.wait_ge(gelu_done, u + e + 3)
                    pe.wait_ge(weighted, u + e + 1)
                    for t in range(4):
                        ins = pe.matmul(y_ps[e % 2][:, t, :], hs[e % 2][:, t * P:(t + 1) * P], w2[:, e, :])
                    ins.then_inc(y_done, 1)

                hidden(0)
                pe.wait_ge(g_ready, c + 1)
                pe.sem_inc(k.pe_passed, 1)
                pe.transpose(g_ps[:], g[:].rearrange("p t e -> p (t e)"), k.ident[:]).then_inc(g_turned, 1)
                hidden(1)
                pe.wait_ge(gT_ready, c + 1)
                pe.wait_ge(acc_ready, c)
                pe.sem_inc(k.pe_passed, 1)
                pe.matmul(b_ps[:].rearrange("p t d -> p (t d)"), gT[:], b2[:].rearrange("g t d -> g (t d)"))\
                  .then_inc(b_done, 1)
                output(0)
                for e in range(2, E):
                    hidden(e)
                    output(e - 1)
                output(E - 1)

        @block.scalar
        def _(act):
            act.sem_inc(gelu_done, 2)
            with act.Fori(0, n) as c:
                for e in range(E):
                    act.wait_ge(h_done, c * E + e + 1)
                    act.wait_ge(y_done, c * E + e + 1)
                    act.activation(hs[e % 2][:], h_ps[e % 2][:], ACT.Gelu).then_inc(gelu_done, 1)
                    if e == 0:
                        act.wait_ge(g_turned, c + 1)
                        act.wait_ge(b_done, c)
                        act.activation(gT[:], g_ps[:], ACT.Copy).then_inc(gT_ready, 1)

        @block.vector
        def _(dve):
            dve.sem_inc(weighted, 2)
            with dve.Fori(0, n) as c:
                dve.wait_ge(g_turned, c)
                dve.wait_ge(weighted, c * E + 2)
                dve.tensor_copy(g[:], gates[:, bass.ts(c, 4), :]).then_inc(g_ready, 1)
                dve.wait_ge(added, c * E + 2)
                dve.wait_ge(b_done, c + 1)
                dve.tensor_tensor(acc[:], b_ps[:], h[:, bass.ts(c, 4), :], ALU.add).then_inc(acc_ready, 1)
                for e in range(E):
                    dve.wait_ge(y_done, c * E + e + 3)
                    dve.wait_ge(added, c * E + e + 1)
                    dve.tensor_tensor(tmp[e % 2][:], y_ps[e % 2][:], bc(g[:, :, e], D), ALU.mult)\
                       .then_inc(weighted, 1)

        @block.gpsimd
        def _(pool):
            pool.sem_inc(added, 2)
            with pool.Fori(0, n) as c:
                pool.wait_ge(acc_ready, c + 1)
                for e in range(E):
                    pool.wait_ge(weighted, c * E + e + 3)
                    pool.wait_ge(added, c * E + e + 2)
                    out = acc[:] if e < E - 1 else h[:, bass.ts(c, 4), :]
                    pool.tensor_tensor(out, acc[:], tmp[e % 2][:], ALU.add).then_inc(added, 1)


def image_attention(nc, mem, k, xT, yT, stats):
    xs = [mem.sb(f"ia_x{b}", [D + 1, 4, 2, WIN]) for b in range(2)]
    qk = [mem.sb(f"ia_qk{b}", [P, 2, 4, WIN]) for b in range(2)]
    v = [mem.sb(f"ia_v{b}", [WIN, 8, D]) for b in range(2)]
    sc = [mem.sb(f"ia_scores{b}", [P, 4, WIN]) for b in range(2)]
    ex = [mem.sb(f"ia_exp{b}", [P, 4, WIN]) for b in range(2)]
    pr = [mem.sb(f"ia_probs{b}", [P, 4, WIN]) for b in range(2)]
    prT = [mem.sb(f"ia_probsT{b}", [WIN, 4, P]) for b in range(2)]
    oT = [mem.sb(f"ia_oT{b}", [D + 1, 512]) for b in range(2)]
    mx, sm, rs = ([mem.sb(f"ia_{x}{b}", [P, 4]) for b in range(2)] for x in ("max", "sum", "rsum"))
    qk_ps = [mem.ps(f"ia_qk_ps{b}", [P, 512]) for b in range(2)]
    v_ps = [mem.ps(f"ia_v_ps{b}", [D, 512]) for b in range(2)]
    s_ps = [mem.ps(f"ia_s_ps{b}", [P, 4, WIN]) for b in range(2)]
    t_ps = [mem.ps(f"ia_t_ps{b}", [WIN, 4, P]) for b in range(2)]
    names = ("x_ready", "qk_done", "v_done", "qk_ready", "v_ready", "scores_done", "max_done", "shifted", "exp_done",
             "sum_done", "rsum_done", "probs_done", "turned", "probsT_ready", "o_done", "oT_ready", "y_done",
             "y_saved", "counted", "ones")
    (x_ready, qk_done, v_done, qk_ready, v_ready, scores_done, max_done, shifted, exp_done, sum_done, rsum_done,
     probs_done, turned, probsT_ready, o_done, oT_ready, y_done, y_saved, counted, ones) = (
         mem.sem("ia_" + x) for x in names)
    n = 8

    def pipeline(eng, front, back):
        front(0, 0, True)
        front(1, 1, True)
        back(0, 0, True)
        front(2, 0, False)
        back(1, 1, True)
        front(3, 1, False)
        with eng.Fori(1, n // 2 - 1) as i:
            for b in range(2):
                back(2 * i + b, b, False)
                front(2 * i + b + 2, b, False)
        back(n - 2, 0, False)
        back(n - 1, 1, False)

    with nc.Block() as block:
        @block.gpsimd
        def _(pool):
            def take(c, b, first):
                if not first:
                    pool.wait_ge(v_done, c - 1)
                pool.tensor_copy(xs[b][:].rearrange("d a r s -> d (a r s)"), xT[:, bass.ts(c, 512)])\
                    .then_inc(x_ready, 1)

            def normal(c, b, first):
                pool.wait_ge(rsum_done, c + 1)
                if not first:
                    pool.wait_ge(turned, c - 1)
                pool.tensor_tensor(pr[b][:], ex[b][:], bc(rs[b][:], WIN), ALU.mult).then_inc(probs_done, 1)
            pipeline(pool, take, normal)

        @block.tensor
        def _(pe):
            pe.wait_ge(ones, 2)

            def front(c, b, first):
                pe.wait_ge(x_ready, c + 1)
                if not first:
                    pe.wait_ge(oT_ready, c - 1)
                    pe.wait_ge(counted, c - 1)
                pe.sem_inc(k.pe_passed, 1)
                for j in range(2):
                    for r in range(2):
                        out = qk_ps[b][r * D:(r + 1) * D, j * 256:(j + 1) * 256]
                        ins = pe.matmul(out.rearrange("d (a s) -> d a s", a=4), k.wl1[:, j, :], xs[b][:, :, r, :])
                ins.then_inc(qk_done, 1)
                for w in range(8):
                    ins = pe.matmul(v_ps[b][:, w * D:(w + 1) * D], xs[b][:, w // 2, w % 2, :], k.wl1[:, 2, :])
                ins.then_inc(v_done, 1)
                pe.wait_ge(qk_ready, c + 1)
                if not first:
                    pe.wait_ge(shifted, c - 1)
                pe.sem_inc(k.pe_passed, 1)
                for p in range(4):
                    for r in range(2):
                        half = slice(r * D, (r + 1) * D)
                        ins = pe.matmul(s_ps[b][half, p, :], qk[b][half, 0, p, :], qk[b][half, 1, p, :])
                ins.then_inc(scores_done, 1)

            def back(c, b, first):
                pe.wait_ge(probs_done, c + 1)
                if not first:
                    pe.wait_ge(probsT_ready, c - 1)
                pe.sem_inc(k.pe_passed, 1)
                for p in range(4):
                    ins = pe.transpose(t_ps[b][:, p, :], pr[b][:, p, :], k.ident[:])
                ins.then_inc(turned, 1)
                pe.wait_ge(probsT_ready, c + 1)
                pe.wait_ge(v_ready, c + 1)
                pe.sem_inc(k.pe_passed, 1)
                for w in range(8):
                    ins = pe.matmul(qk_ps[b][0:D, w * WIN:(w + 1) * WIN], v[b][:, w, :],
                                    prT[b][:, w // 2, w % 2 * WIN:(w % 2 + 1) * WIN])
                ins.then_inc(o_done, 1)
                pe.wait_ge(oT_ready, c + 1)
                pe.sem_inc(k.pe_passed, 1)
                pe.matmul(v_ps[b][:], k.wl1[:, 3, :], oT[b][:]).then_inc(y_done, 1)
            pipeline(pe, front, back)

        @block.scalar
        def _(act):
            def front(c, b, first):
                act.wait_ge(qk_done, c + 1)
                if not first:
                    act.wait_ge(scores_done, c - 1)
                act.activation(qk[b][:].rearrange("d j a s -> d (j a s)"), qk_ps[b][:], ACT.Copy)\
                   .then_inc(qk_ready, 1)
                act.wait_ge(v_done, c + 1)
                if not first:
                    act.wait_ge(o_done, c - 1)
                act.activation(v[b][:].rearrange("s w d -> s (w d)"), v_ps[b][:], ACT.Copy).then_inc(v_ready, 1)

            def back(c, b, first):
                act.wait_ge(shifted, c + 1)
                if not first:
                    act.wait_ge(probs_done, c - 1)
                act.activation(ex[b][:], sc[b][:], ACT.Exp, scale=1.0 / D).then_inc(exp_done, 1)
                act.wait_ge(turned, c + 1)
                if not first:
                    act.wait_ge(o_done, c - 1)
                act.activation(prT[b][:], t_ps[b][:], ACT.Copy).then_inc(probsT_ready, 1)
                act.wait_ge(o_done, c + 1)
                if not first:
                    act.wait_ge(y_done, c - 1)
                act.activation(oT[b][0:D, :], qk_ps[b][0:D, :], ACT.Copy).then_inc(oT_ready, 1)
            pipeline(act, front, back)

        @block.vector
        def _(dve):
            for b in range(2):
                dve.memset(oT[b][D:D + 1, :], 1.0).then_inc(ones, 1)

            def front(c, b, first):
                dve.wait_ge(scores_done, c + 1)
                dve.tensor_reduce(mx[b][:], s_ps[b][:], AX.X, ALU.max).then_inc(max_done, 1)
                dve.wait_ge(max_done, c + 1)
                if not first:
                    dve.wait_ge(exp_done, c - 1)
                dve.tensor_tensor(sc[b][:], s_ps[b][:], bc(mx[b][:], WIN), ALU.subtract).then_inc(shifted, 1)

            def back(c, b, first):
                dve.wait_ge(exp_done, c + 1)
                dve.tensor_reduce(sm[b][:], ex[b][:], AX.X, ALU.add).then_inc(sum_done, 1)
                dve.wait_ge(sum_done, c + 1)
                if not first:
                    dve.wait_ge(probs_done, c - 1)
                dve.reciprocal(rs[b][:], sm[b][:]).then_inc(rsum_done, 1)
                dve.wait_ge(y_done, c + 1)
                dve.tensor_copy(yT[:, bass.ts(c, 512)], v_ps[b][:]).then_inc(y_saved, 1)
                dve.bn_stats(stats[:, bass.ts(c, 6)], v_ps[b][:]).then_inc(counted, 1)
            pipeline(dve, front, back)


def batch_norm_add(nc, mem, k, xT, yT, stats, h):
    mv = mem.sb("bn_mv", [D, 4])
    z = [mem.sb(f"bn_z{b}", [D, 512]) for b in range(2)]
    r = [mem.sb(f"bn_r{b}", [D, 512]) for b in range(2)]
    s = [mem.sb(f"bn_s{b}", [D, 512]) for b in range(2)]
    t_ps = [mem.ps(f"bn_ps{b}", [P, 4, D]) for b in range(2)]
    step, var_ready, std_ready, scaled, relued, summed, turned, added = (
        mem.sem("bn_" + x) for x in ("step", "var_ready", "std_ready", "scaled", "relued", "summed", "turned", "added"))
    n = 8
    with nc.Block() as block:
        @block.vector
        def _(dve):
            dve.bn_aggr(mv[:, 0:2], stats[:]).then_inc(var_ready, 1)
            dve.wait_ge(std_ready, 1)
            dve.reciprocal(mv[:, 3:4], mv[:, 2:3]).then_inc(step, 1)
            dve.wait_ge(step, 1)
            dve.tensor_tensor(mv[:, 3:4], mv[:, 3:4], k.bn[:, 0:1], ALU.mult).then_inc(step, 1)
            dve.wait_ge(step, 2)

            def scale(c, b, first):
                if not first:
                    dve.wait_ge(relued, c - 1)
                dve.tensor_scalar(z[b][:], yT[:, bass.ts(c, 512)], mv[:, 0:1], mv[:, 3:4], ALU.subtract,
                                  ALU.mult).then_inc(scaled, 1)

            def total(c, b, first):
                dve.wait_ge(relued, c + 1)
                if not first:
                    dve.wait_ge(turned, c - 1)
                dve.tensor_tensor(s[b][:], r[b][:], xT[0:D, bass.ts(c, 512)], ALU.add).then_inc(summed, 1)

            def add(c, b):
                dve.wait_ge(turned, c + 1)
                dve.tensor_tensor(h[:, bass.ts(c, 4), :], h[:, bass.ts(c, 4), :], t_ps[b][:], ALU.add)\
                   .then_inc(added, 1)

            scale(0, 0, True)
            scale(1, 1, True)
            total(0, 0, True)
            scale(2, 0, False)
            total(1, 1, True)
            scale(3, 1, False)
            with dve.Fori(1, n // 2 - 1) as i:
                for b in range(2):
                    add(2 * i + b - 2, b)
                    total(2 * i + b, b, False)
                    scale(2 * i + b + 2, b, False)
            for c in (n - 2, n - 1):
                add(c - 2, c % 2)
                total(c, c % 2, False)
            for c in (n - 2, n - 1):
                add(c, c % 2)

        @block.scalar
        def _(act):
            act.wait_ge(var_ready, 1)
            act.activation(mv[:, 2:3], mv[:, 1:2], ACT.Sqrt, bias=k.eps[0:D, 0:1]).then_inc(std_ready, 1)

            def relu(c, b, first):
                act.wait_ge(scaled, c + 1)
                if not first:
                    act.wait_ge(summed, c - 1)
                act.activation(r[b][:], z[b][:], ACT.Relu, bias=k.bn[:, 1:2]).then_inc(relued, 1)
            twice(act, n, relu)

        @block.tensor
        def _(pe):
            def turn(c, b, first):
                pe.wait_ge(summed, c + 1)
                if not first:
                    pe.wait_ge(added, c - 1)
                pe.sem_inc(k.pe_passed, 1)
                for t in range(4):
                    ins = pe.transpose(t_ps[b][:, t, :], s[b][:, t * P:(t + 1) * P], k.ident[0:D, 0:D])
                ins.then_inc(turned, 1)
            twice(pe, n, turn)




class Names:
    pass


def program(nc, a, out):
    with ExitStack() as ctx:
        mem = Memory(nc, ctx)
        k = Names()
        h = mem.sb("h", [P, TILES, D])
        xn = mem.sb("xn", [P, TILES, D])
        xT = mem.sb("xT", [D + 1, M])
        k.big = mem.sb("squares", [P, TILES, D])
        k.ln_s = mem.sb("ln_stats", [P, 5, TILES])
        k.ln_xs = [mem.sb(f"ln_xs{b}", [P, 4, D]) for b in range(2)]
        k.ln_xts = [mem.sb(f"ln_xts{b}", [D + 1, 512]) for b in range(2)]
        hg = mem.sb("router_h", [P, TILES, GH * GE])
        counts = mem.sb("last_counts", [P, TILES])
        start_end = mem.sb("column_limits", [P, 3], I32)
        gates = [mem.sb("gates0", [P, TILES, E0]), mem.sb("gates1", [P, TILES, E1])]
        logits = mem.sb("logits1", [P, TILES, E1])
        k.settled = mem.sem("constants_settled")
        k.pe_passed, k.pool_passed = mem.sem("tensor_waits_passed"), mem.sem("gpsimd_waits_passed")

        def stage():
            return Stage(mem)

        k.ln_sems = [mem.sem(f"ln_{x}") for x in (
            "step", "centered", "squared", "summed", "rooted", "scaled", "turned", "evacuated", "kept", "mapped",
            "saved")]
        calls = [0, 0]

        def norm(name, **kw):
            with stage() as m:
                k.ln_pT = [m.ps(f"{name}_pT{b}", [D, 512]) for b in range(2)]
                k.ln_pj = [m.ps(f"{name}_pj{b}", [P, 4, GH * GE]) for b in range(2)]
                normalize(nc, m, k, h, xn, xT, *calls, **kw)
            calls[0] += 1
            calls[1] += "weight" in kw

        with stage() as m:
            m.sb = mem.sb
            load_constants(nc, m, a, k)
        with nc.Block() as block:
            @block.vector
            def _(dve):
                for b in range(2):
                    ins = dve.memset(k.ln_xts[b][D:D + 1, :], 1.0)
                ins.then_inc(k.settled, 1)
        with stage() as keys_mem:
            keys = keys_mem.sb("edge_keys", [P, EC])
            with stage() as m:
                sort_edges(nc, m, a, k, keys, start_end, counts)
            with stage() as m:
                count_last(nc, m, k, keys, start_end, counts)
            with stage() as m:
                tokenize(nc, m, a, k, h)
            norm("ln0")
            with stage() as m:
                window_attention(nc, m, k, xT, h)
            norm("ln1", weight=k.wgat[:], out=hg)
            with stage() as m:
                graph_router(nc, m, a, k, hg, keys, start_end, counts, gates[0])
        with stage() as m:
            experts(nc, m, k, 0, E0, xT, gates[0], h)
        norm("ln2")
        with stage() as m:
            yT = m.sb("yT", [D, M])
            stats = m.sb("bn_stats", [D, 8 * 6])
            with stage() as m2:
                image_attention(nc, m2, k, xT, yT, stats)
            with stage() as m2:
                batch_norm_add(nc, m2, k, xT, yT, stats, h)
        norm("ln3", weight=k.wr[:], out=logits, affine=k.affine)
        with stage() as m:
            choose(nc, m, k.lower, E1, logits, gates[1], "moe1")
        with stage() as m:
            experts(nc, m, k, 1, E1, xT, gates[1], h)
        stored = mem.sem("output_stored")
        with nc.Block() as block:
            @block.sync
            def _(sp):
                sp.dma_start(out.rearrange("(t r) s d -> (r s) t d", r=2), h[:]).then_inc(stored, 16)
                sp.wait_ge(stored, 16)


_INS = ['x', 'L0_tok_W', 'L0_tok_b', 'L0_attn_w_qkv', 'L0_attn_b_qkv', 'L0_attn_w_proj', 'L0_attn_b_proj',
        'L0_attn_rel_pos_bias', 'L0_ffn_W_gat', 'L0_ffn_att_src', 'L0_ffn_att_dst', 'L0_ffn_b_gat',
        'L0_ffn_ln_gamma', 'L0_ffn_ln_beta', 'L0_ffn_W1', 'L0_ffn_b1', 'L0_ffn_W2', 'L0_ffn_b2',
        'L0_ffn_edge_index', 'L1_attn_Wq', 'L1_attn_bq', 'L1_attn_Wk', 'L1_attn_bk', 'L1_attn_Wv',
        'L1_attn_bv', 'L1_attn_Wl', 'L1_attn_bl', 'L1_attn_gamma', 'L1_attn_beta', 'L1_ffn_gamma',
        'L1_ffn_beta', 'L1_ffn_Wr', 'L1_ffn_br', 'L1_ffn_W1', 'L1_ffn_b1', 'L1_ffn_W2', 'L1_ffn_b2']


def kernel(**inputs):
    import numpy as np
    import concourse.bacc as bacc
    from concourse.bass_utils import run_bass_kernel_spmd

    nc = bacc.Bacc("TRN2", target_bir_lowering=False, num_devices=1)
    arrays, args = {}, {}
    for name in _INS:
        v = np.ascontiguousarray(inputs[name])
        arrays["in_" + name] = v
        args[name] = nc.dram_tensor("in_" + name, v.shape, mybir.dt.from_np(v.dtype), kind="ExternalInput").ap()
    out = nc.dram_tensor("out_h", (IMG, WIN, D), F32, kind="ExternalOutput").ap()
    program(nc, args, out)
    return run_bass_kernel_spmd(nc, [arrays], core_ids=[0]).results[0]["out_h"]
```

```python
from contextlib import ExitStack

import concourse.bass as bass
from concourse import mybir

F32 = mybir.dt.float32
BF16 = mybir.dt.bfloat16
I32 = mybir.dt.int32
ALU = mybir.AluOpType
ACT = mybir.ActivationFunctionType
AX = mybir.AxisListType

P = 128
D = 64
IMG = 64
WIN = 64
M = IMG * WIN
TILES = M // P
HD = 8
NH = D // HD
GH, GE = 4, 4
E0, E1 = 4, 8
HID = 128
EDGES = 262144
EC = EDGES // P
EPS = 1e-5
CLASS_LAST = float(1 << 24)
CLASS_NONE = float(1 << 25)
GCH = 8
CCH = 16
NSRC = GH * GE + GH
NDST = 2 * GH
EXPERT_PAIRS = TILES // 4
COUNT_PAIRS = 2 * (EXPERT_PAIRS - 1)
MERGES_LOADING = 4
MERGES_TOKENS = 8
NV = GH * (GE + 1)


def twice(eng, n, body):
    body(0, 0, True)
    body(1, 1, True)
    with eng.Fori(1, n // 2) as i:
        for b in range(2):
            body(2 * i + b, b, False)


def bc(ap, n):
    return ap.unsqueeze(len(ap.shape)).broadcast_to([*ap.shape, n])


def bc_at(ap, axis, n):
    a = ap.unsqueeze(axis)
    return a.broadcast_to([*a.shape[:axis], n, *a.shape[axis + 1:]])


class Memory:

    def __init__(self, nc, ctx):
        self.nc, self.ctx = nc, ctx

    def sb(self, name, shape, dt=F32):
        return self.ctx.enter_context(self.nc.sbuf_tensor(name, shape, dt))

    def ps(self, name, shape, dt=F32):
        return self.ctx.enter_context(self.nc.psum_tensor(name, shape, dt))

    def sem(self, name):
        return self.ctx.enter_context(self.nc.semaphore(name))


class Stage:

    def __init__(self, mem):
        self.nc, self.sem, self.ctx = mem.nc, mem.sem, ExitStack()
        m = Memory(mem.nc, self.ctx)
        self.sb, self.ps = m.sb, m.ps

    def __enter__(self):
        return self

    def __exit__(self, *exc):
        self.ctx.close()


def load_constants(nc, mem, a, k, sort):
    loaded = mem.sem("constants_loaded")
    made = mem.sem("constants_made")
    turned = mem.sem("token_weight_turned")
    k.ident = mem.sb("ident", [P, P])
    k.wqkv = mem.sb("wqkv", [D + 1, 3 * D])
    k.wproj = mem.sb("wproj", [D + 1, D])
    k.wtok = mem.sb("wtok", [D + 1, D])
    k.wtok_raw = mem.sb("wtok_raw", [D, D])
    k.relbias = mem.sb("relbias", [P, NH, WIN])
    k.wgat = mem.sb("wgat", [D + 1, GH * GE])
    k.att_src = mem.sb("att_src", [P, GH * GE])
    k.att_dst = mem.sb("att_dst", [P, GH * GE])
    k.b_gat = mem.sb("b_gat", [P, GH * GE])
    k.ln_gamma = mem.sb("ln_gamma", [P, GH * GE])
    k.ln_beta = mem.sb("ln_beta", [P, GH * GE])
    k.w1 = [mem.sb("moe0_w1", [D + 1, E0, HID]), mem.sb("moe1_w1", [D + 1, E1, HID])]
    k.w2 = [mem.sb("moe0_w2", [HID, E0, D]), mem.sb("moe1_w2", [HID, E1, D])]
    k.b2 = mem.sb("moe1_b2", [4 * E1, 4, D])
    k.b2_rows = mem.sb("moe0_b2_rows", [P, E0, D])
    b2_zeroed = mem.sem("b2_zeroed")
    k.wl1 = mem.sb("attn1_w", [D + 1, 4, D])
    k.bn = mem.sb("attn1_bn", [D, 2])
    k.affine = mem.sb("moe1_affine", [D, 2])
    k.wr = mem.sb("moe1_wr", [D + 1, E1])
    k.eps = mem.sb("eps", [P, 1])
    k.headmask = mem.sb("headmask", [P, 2, NH])
    k.iota_lo = mem.sb("iota_lo", [P, P])
    k.lower = mem.sb("lower", [P, E1, E1])
    k.lower0 = mem.sb("lower0", [P, E0, E0])
    k.zero_mm = mem.sb("zero_mm", [P, 512])
    turn = mem.ps("turn_token_weight", [D, D])
    bias_rows = mem.sb("bias_rows", [WIN, NH, WIN])
    reverse = mem.sb("reverse", [WIN, 2, WIN])
    bias_ps = mem.ps("bias_ps", [P, NH, WIN])

    def row(v):
        return v.rearrange("(a n) -> a n", a=1)

    def everywhere(v, n):
        return bass.AP(v.tensor, 0, [[0, P], [1, n]])

    loads = [
        (k.wtok_raw[:], a["L0_tok_W"]), (k.wtok[D:D + 1, :], row(a["L0_tok_b"])),
        (k.wqkv[0:D, :], a["L0_attn_w_qkv"]), (k.wqkv[D:D + 1, :], row(a["L0_attn_b_qkv"])),
        (k.wproj[0:D, :], a["L0_attn_w_proj"]), (k.wproj[D:D + 1, :], row(a["L0_attn_b_proj"])),
        (k.wgat[0:D, :], a["L0_ffn_W_gat"]),
        (k.bn[:, 0:1], a["L1_attn_gamma"].rearrange("(p a) -> p a", a=1)),
        (k.bn[:, 1:2], a["L1_attn_beta"].rearrange("(p a) -> p a", a=1)),
        (k.affine[:, 0:1], a["L1_ffn_gamma"].rearrange("(p a) -> p a", a=1)),
        (k.affine[:, 1:2], a["L1_ffn_beta"].rearrange("(p a) -> p a", a=1)),
        (k.wr[0:D, :], a["L1_ffn_Wr"]), (k.wr[D:D + 1, :], row(a["L1_ffn_br"])),
    ]
    loads.append((bias_rows[:], bass.AP(a["L0_attn_rel_pos_bias"].tensor, 0,
                                        [[1, WIN], [2 * WIN - 1, NH], [1, WIN]])))
    for dst, name in ((k.att_src, "L0_ffn_att_src"), (k.att_dst, "L0_ffn_att_dst")):
        loads.append((dst[:], everywhere(a[name], GH * GE)))
    loads.append((k.b2_rows[:].rearrange("p e d -> p (e d)"), everywhere(a["L0_ffn_b2"], E0 * D)))
    for dst, name in ((k.b_gat, "L0_ffn_b_gat"), (k.ln_gamma, "L0_ffn_ln_gamma"), (k.ln_beta, "L0_ffn_ln_beta")):
        loads.append((dst[:], everywhere(a[name], GH * GE)))
    for n, e in ((0, E0), (1, E1)):
        loads += [
            (k.w1[n][0:D], a[f"L{n}_ffn_W1"].rearrange("e d h -> d e h")),
            (k.w1[n][D:D + 1], a[f"L{n}_ffn_b1"].rearrange("(a e) h -> a e h", a=1)),
            (k.w2[n][:], a[f"L{n}_ffn_W2"].rearrange("e h d -> h e d")),
        ]
    for n, (w, b) in enumerate((("Wq", "bq"), ("Wk", "bk"), ("Wv", "bv"), ("Wl", "bl"))):
        loads += [(k.wl1[0:D, n, :], a[f"L1_attn_{w}"]), (k.wl1[D:D + 1, n, :], row(a[f"L1_attn_{b}"]))]
    with nc.Block() as block:
        @block.sync
        def _(sp):
            sort.load(sp, a["L0_ffn_edge_index"])
            for dst, src in loads:
                sp.dma_start(dst, src).then_inc(loaded, 16)
            sp.wait_ge(b2_zeroed, 1)
            for t in range(4):
                sp.dma_start(k.b2[t * E1:(t + 1) * E1, t, :], a["L1_ffn_b2"]).then_inc(loaded, 16)
            sp.wait_ge(loaded, 16 * (len(loads) + 4))

        @block.vector
        def _(dve):
            dve.memset(k.b2[:], 0.0).then_inc(b2_zeroed, 1)
            sort.form_keys(dve)
            sort.merge(dve, MERGES_LOADING)

        @block.gpsimd
        def _(pool):
            n = 0
            for t, v in ((k.ident, 0.0), (k.eps, EPS), (k.headmask, 1.0),
                         (k.lower, 1.0), (k.lower0, 1.0), (k.zero_mm, 0.0), (reverse, 0.0)):
                pool.memset(t[:], v).then_inc(made, 1)
                n += 1
            pool.iota(k.iota_lo[:], [[1, P]], base=0, channel_multiplier=0,
                      allow_small_or_imprecise_dtypes=True).then_inc(made, 1)
            n += 1
            pool.wait_ge(made, n)
            pool.affine_select(k.ident[:], k.ident[:], [[-1, P]], ALU.not_equal, 1.0, base=0,
                               channel_multiplier=1).then_inc(made, 1)
            pool.affine_select(reverse[:], reverse[:], [[0, 2], [1, WIN]], ALU.not_equal, 1.0,
                               base=1 - WIN, channel_multiplier=1).then_inc(made, 1)
            pool.affine_select(k.headmask[:], k.headmask[:], [[-D, 2], [-HD, NH]], ALU.is_ge, 0.0,
                               base=0, channel_multiplier=1).then_inc(made, 1)
            for t, e in ((k.lower, E1), (k.lower0, E0)):
                pool.affine_select(t[:], t[:], [[1, e], [-1, e]], ALU.is_gt, 0.0, base=0,
                                   channel_multiplier=0).then_inc(made, 1)
            n += 5
            pool.wait_ge(made, n)
            pool.affine_select(k.headmask[:], k.headmask[:], [[D, 2], [HD, NH]], ALU.is_ge, 0.0,
                               base=HD - 1, channel_multiplier=-1).then_inc(made, 1)
            pool.wait_ge(made, n + 1)

    with nc.Block() as block:
        @block.tensor
        def _(pe):
            pe.transpose(turn[:], k.wtok_raw[:], k.ident[0:D, 0:D]).then_inc(turned, 1)
            pe.matmul(bias_ps[:].rearrange("q h j -> q (h j)"), reverse[:].rearrange("r t q -> r (t q)"),
                      bias_rows[:].rearrange("r h j -> r (h j)")).then_inc(turned, 1)

        @block.vector
        def _(dve):
            dve.memset(k.wgat[D:D + 1, :], 0.0)
            dve.tensor_tensor(k.headmask[:, 0, :], k.headmask[:, 0, :], k.headmask[:, 1, :], ALU.add)
            dve.wait_ge(turned, 1)
            dve.tensor_copy(k.wtok[0:D, :], turn[:])
            dve.wait_ge(turned, 2)
            dve.tensor_copy(k.relbias[:], bias_ps[:])


def tokenize(nc, mem, a, k, h, sort):
    rows = a["x"].rearrange("b c (i p) w -> (b c i) (p w)", p=8)
    xrow = [mem.sb(f"xrow{b}", [P, 512]) for b in range(2)]
    patch = [mem.sb(f"patch{b}", [P, 8, D]) for b in range(2)]
    xT = [mem.sb(f"patchT{b}", [D + 1, 1024]) for b in range(2)]
    pT = [mem.ps(f"patchT_ps{b}", [D, 8, P]) for b in range(2)]
    ph = [mem.ps(f"token_ps{b}", [P, 8, D]) for b in range(2)]
    loaded = [mem.sem(f"images_loaded{b}") for b in range(2)]
    ones = mem.sem("patch_ones")
    cut, turned, copied, mapped, saved = (
        mem.sem(f"patch_{x}") for x in ("cut", "turned", "copied", "mapped", "saved"))
    n = 4
    with nc.Block() as block:
        @block.sync
        def _(sp):
            def chunk(c, b, first):
                if not first:
                    sp.wait_ge(cut, c - 1)
                sp.dma_start(xrow[b][:], rows[bass.ts(c, P), :]).then_inc(loaded[b], 16)
            twice(sp, n, chunk)

        @block.tensor
        def _(pe):
            def chunk(c, b, first):
                pe.wait_ge(cut, c + 1)
                if not first:
                    pe.wait_ge(copied, c - 1)
                for j in range(8):
                    ins = pe.transpose(pT[b][:, j, :], patch[b][:, j, :], k.ident[:])
                ins.then_inc(turned, 1)
                pe.wait_ge(copied, c + 1)
                if not first:
                    pe.wait_ge(saved, c - 1)
                else:
                    pe.wait_ge(ones, 2)
                for t in range(8):
                    ins = pe.matmul(ph[b][:, t, :], xT[b][:, t * P:(t + 1) * P], k.wtok[:])
                ins.then_inc(mapped, 1)
            twice(pe, n, chunk)

        @block.scalar
        def _(act):
            def chunk(c, b, first):
                act.wait_ge(turned, c + 1)
                if not first:
                    act.wait_ge(mapped, c - 1)
                act.activation(xT[b][0:D, :].rearrange("k (s j) -> k s j", j=8),
                               pT[b][:].rearrange("k j s -> k s j"), ACT.Copy).then_inc(copied, 1)
            twice(act, n, chunk)

        @block.vector
        def _(dve):
            for b in range(2):
                dve.memset(xT[b][D:D + 1, :], 1.0).then_inc(ones, 1)

            def save(c, b):
                dve.wait_ge(mapped, c + 1)
                dve.tensor_copy(h[:, bass.ts(c, 8), :], ph[b][:]).then_inc(saved, 1)

            def chunk(c, b, first):
                if not first:
                    save(c - 2, b)
                dve.wait_ge(loaded[b], 8 * (c + 2 - b))
                if not first:
                    dve.wait_ge(turned, c - 1)
                dve.tensor_copy(patch[b][:].rearrange("s j (p q) -> s j p q", p=8),
                                xrow[b][:].rearrange("s (p j q) -> s j p q", p=8, j=8)).then_inc(cut, 1)
            for c in range(n):
                chunk(c, c % 2, c < 2)
                sort.merge(dve, MERGES_LOADING + MERGES_TOKENS * (c + 1) // n)
            save(n - 2, 0)
            save(n - 1, 1)


def normalize(nc, mem, k, h, xn, xT, call, projections, weight=None, out=None, affine=None):
    s, xc, sq = k.ln_s, xn, k.big
    step, centered, squared, summed, rooted, scaled, turned, evacuated, kept, mapped, saved = k.ln_sems
    xs, xts, pT, pj = k.ln_xs, k.ln_xts, k.ln_pT, k.ln_pj
    N = weight.shape[-1] if weight is not None else 0
    n = TILES // 4
    calls, chunks, projected = call, call * n, projections * n
    with nc.Block() as block:
        @block.vector
        def _(dve):
            dve.tensor_reduce(s[:, 0, :], h[:], AX.X, ALU.add).then_inc(step, 1)
            dve.wait_ge(step, 3 * calls + 1)
            dve.tensor_scalar(s[:, 1, :], s[:, 0, :], 1.0 / D, None, ALU.mult).then_inc(step, 1)
            dve.wait_ge(step, 3 * calls + 2)
            dve.tensor_tensor(xc[:], h[:], bc(s[:, 1, :], D), ALU.subtract).then_inc(centered, 1)
            dve.wait_ge(squared, calls + 1)
            dve.tensor_reduce(s[:, 2, :], sq[:], AX.X, ALU.add).then_inc(summed, 1)
            dve.wait_ge(rooted, calls + 1)
            dve.reciprocal(s[:, 4, :], s[:, 3, :]).then_inc(step, 1)
            dve.wait_ge(step, 3 * calls + 3)

            def scale(c, b, first):
                if not first:
                    dve.wait_ge(turned, chunks + c - 1)
                dve.tensor_tensor(xs[b][:], xc[:, bass.ts(c, 4), :], bc(s[:, 4, bass.ts(c, 4)], D),
                                  ALU.mult).then_inc(scaled, 1)

            def save(c, b):
                dve.wait_ge(mapped, projected + c + 1)
                dve.tensor_copy(out[:, bass.ts(c, 4), :], pj[b][:, :, 0:N]).then_inc(saved, 1)

            def chunk(c, b, first):
                if N and not first:
                    save(c - 2, b)
                scale(c, b, first)
            twice(dve, n, chunk)
            if N:
                save(n - 2, 0)
                save(n - 1, 1)

        @block.scalar
        def _(act):
            act.wait_ge(centered, calls + 1)
            act.activation(sq[:], xc[:], ACT.Square).then_inc(squared, 1)
            act.wait_ge(summed, calls + 1)
            act.activation(s[:, 3, :], s[:, 2, :], ACT.Sqrt, bias=k.eps[:, 0:1], scale=1.0 / D).then_inc(rooted, 1)

            def chunk(c, b, first):
                act.wait_ge(turned, chunks + c + 1)
                if not first:
                    act.wait_ge(kept, chunks + c - 1)
                    if N:
                        act.wait_ge(mapped, projected + c - 1)
                if affine is None:
                    ins = act.activation(xts[b][0:D, :], pT[b][:], ACT.Copy)
                else:
                    ins = act.activation(xts[b][0:D, :], pT[b][:], ACT.Identity, bias=affine[:, 1:2],
                                         scale=affine[:, 0:1])
                ins.then_inc(evacuated, 1)
            twice(act, n, chunk)

        @block.gpsimd
        def _(pool):
            def chunk(c, b, first):
                pool.wait_ge(evacuated, chunks + c + 1)
                pool.tensor_copy(xT[:, bass.ts(c, 512)], xts[b][:]).then_inc(kept, 1)
            twice(pool, n, chunk)

        @block.tensor
        def _(pe):
            def turn(c, b, first):
                pe.wait_ge(scaled, chunks + c + 1)
                if not first:
                    pe.wait_ge(evacuated, chunks + c - 1)
                pe.sem_inc(k.pe_passed, 1)
                for t in range(4):
                    ins = pe.transpose(pT[b][:, t * P:(t + 1) * P], xs[b][:, t, :], k.ident[:])
                ins.then_inc(turned, 1)

            def project(c, b, first):
                pe.wait_ge(evacuated, chunks + c + 1)
                if not first:
                    pe.wait_ge(saved, projected + c - 1)
                for t in range(4):
                    ins = pe.matmul(pj[b][:, t, 0:N], xts[b][:, t * P:(t + 1) * P], weight)
                ins.then_inc(mapped, 1)

            if not N:
                twice(pe, n, turn)
                return
            turn(0, 0, True)
            turn(1, 1, True)
            project(0, 0, True)
            turn(2, 0, False)
            project(1, 1, True)
            turn(3, 1, False)
            with pe.Fori(2, n // 2) as i:
                for b in range(2):
                    project(2 * i + b - 2, b, False)
                    turn(2 * i + b, b, False)
            project(n - 2, 0, False)
            project(n - 1, 1, False)


def window_attention(nc, mem, k, xT, h, sort):
    xs = [mem.sb(f"wa_x{b}", [D + 1, 2, 2, WIN]) for b in range(2)]
    qk = [mem.sb(f"wa_qk{b}", [P, 2, WIN]) for b in range(2)]
    kbd = [mem.sb(f"wa_kbd{b}", [P, NH, WIN]) for b in range(2)]
    vbd = [mem.sb(f"wa_vbd{b}", [P, 2, NH // 2, 2, HD]) for b in range(2)]
    sc = [mem.sb(f"wa_scores{b}", [P, NH, WIN]) for b in range(2)]
    pr = [mem.sb(f"wa_probs{b}", [P, NH, WIN]) for b in range(2)]
    prT = [mem.sb(f"wa_probsT{b}", [P, NH // 2, P]) for b in range(2)]
    mx = [mem.sb(f"wa_max{b}", [P, NH]) for b in range(2)]
    sm = [mem.sb(f"wa_sum{b}", [P, NH]) for b in range(2)]
    rs = [mem.sb(f"wa_rsum{b}", [P, NH]) for b in range(2)]
    o = [mem.sb(f"wa_o{b}", [P, D]) for b in range(2)]
    oT = [mem.sb(f"wa_oT{b}", [D + 1, P]) for b in range(2)]
    qkv_ps = [mem.ps(f"wa_qkv_ps{b}", [P, 512]) for b in range(2)]
    s_ps = [mem.ps(f"wa_s_ps{b}", [P, NH, WIN]) for b in range(2)]
    t_ps = [mem.ps(f"wa_t_ps{b}", [P, NH // 2, P]) for b in range(2)]
    o_ps = [mem.ps(f"wa_o_ps{b}", [P, 512]) for b in range(2)]
    names = ("x_ready", "qkv_done", "qk_ready", "kbd_ready", "v0_ready", "vbd_ready", "scores_done", "biased",
             "max_done", "shifted", "exp_done", "sum_done", "rsum_done", "probs_turned", "probsT_ready",
             "o_done", "o_scaled", "o_turned", "oT_ready", "proj_done", "added", "zeroed", "ones")
    (x_ready, qkv_done, qk_ready, kbd_ready, v0_ready, vbd_ready, scores_done, biased, max_done, shifted,
     exp_done, sum_done, rsum_done, probs_turned, probsT_ready, o_done, o_scaled, o_turned, oT_ready,
     proj_done, added, zeroed, ones) = (mem.sem("wa_" + x) for x in names)
    n = TILES

    with nc.Block() as block:
        @block.gpsimd
        def _(pool):
            for b in range(2):
                pool.memset(vbd[b][:], 0.0).then_inc(zeroed, 1)

            def take(c, b, first):
                if not first:
                    pool.wait_ge(qkv_done, c - 1)
                pair = xT[:, bass.ts(c, P)].rearrange("d (r s) -> d r s", r=2)
                pool.tensor_copy(xs[b][:], bc_at(pair, 2, 2)).then_inc(x_ready, 1)

            def shift(c, b, first):
                pool.wait_ge(max_done, c + 1)
                pool.tensor_tensor(sc[b][:], sc[b][:], bc(mx[b][:], WIN), ALU.subtract).then_inc(shifted, 1)

            take(0, 0, True)
            take(1, 1, True)
            with pool.Fori(0, n // 2 - 1) as i:
                for b in range(2):
                    shift(2 * i + b, b, False)
                    take(2 * i + b + 2, b, False)
            shift(n - 2, 0, False)
            shift(n - 1, 1, False)

        @block.tensor
        def _(pe):
            def qkv(c, b, first):
                pe.wait_ge(x_ready, c + 1)
                if not first:
                    pe.wait_ge(qk_ready, c - 1)
                    pe.wait_ge(vbd_ready, c - 1)
                pe.sem_inc(k.pe_passed, 1)
                for r in range(2):
                    half = xs[b][:, r, 0, :]
                    for j in range(2):
                        pe.matmul(qkv_ps[b][r * D:(r + 1) * D, j * WIN:(j + 1) * WIN],
                                  k.wqkv[:, j * D:(j + 1) * D], half)
                for r in range(2):
                    both = xs[b][:, r].rearrange("d t s -> d (t s)")
                    ins = pe.matmul(qkv_ps[b][:, (2 + r) * D:(3 + r) * D], both, k.wqkv[:, 2 * D:3 * D])
                ins.then_inc(qkv_done, 1)

            def scores(c, b, first):
                pe.wait_ge(qk_ready, c + 1)
                pe.wait_ge(kbd_ready, c + 1)
                if not first:
                    pe.wait_ge(biased, c - 1)
                pe.sem_inc(k.pe_passed, 1)
                for r in range(2):
                    half = slice(r * D, (r + 1) * D)
                    ins = pe.matmul(s_ps[b][half], qk[b][half, 0, :], kbd[b][half])
                ins.then_inc(scores_done, 1)

            def turn(c, b, first):
                pe.wait_ge(exp_done, c + 1)
                if not first:
                    pe.wait_ge(probsT_ready, c - 1)
                for g in range(NH // 2):
                    ins = pe.transpose(t_ps[b][:, g, :], pr[b][:, 2 * g:2 * g + 2, :], k.ident[:])
                ins.then_inc(probs_turned, 1)

            def values(c, b, first):
                pe.wait_ge(probsT_ready, c + 1)
                pe.wait_ge(vbd_ready, c + 1)
                if not first:
                    pe.wait_ge(added, c - 1)
                for r in range(2):
                    for g in range(NH // 2):
                        ins = pe.matmul(o_ps[b][r * WIN:(r + 1) * WIN, 2 * HD * g:2 * HD * (g + 1)],
                                        prT[b][:, g, r * WIN:(r + 1) * WIN], vbd[b][:, r, g])
                ins.then_inc(o_done, 1)

            def turn_out(c, b):
                pe.wait_ge(o_scaled, c + 1)
                pe.sem_inc(k.pe_passed, 1)
                pe.transpose(o_ps[b][0:D, 128:256], o[b][:], k.ident[:]).then_inc(o_turned, 1)

            def project(c, b):
                pe.wait_ge(oT_ready, c + 1)
                pe.matmul(o_ps[b][:, 64:128], oT[b][:], k.wproj[:]).then_inc(proj_done, 1)

            def step(c, b, first=False, start=False, end=False):
                turn(c, b, first)
                if not end:
                    qkv(c + 2, b, False)
                if not start:
                    turn_out(c - 1, 1 - b)
                values(c, b, first)
                if not start:
                    project(c - 1, 1 - b)
                if not end:
                    scores(c + 2, b, False)

            pe.wait_ge(ones, 2)
            qkv(0, 0, True)
            qkv(1, 1, True)
            scores(0, 0, True)
            scores(1, 1, True)
            step(0, 0, first=True, start=True)
            step(1, 1, first=True)
            with pe.Fori(1, n // 2 - 1) as i:
                for b in range(2):
                    step(2 * i + b, b)
            step(n - 2, 0, end=True)
            step(n - 1, 1, end=True)
            turn_out(n - 1, 1)
            project(n - 1, 1)

        @block.scalar
        def _(act):
            act.wait_ge(zeroed, 2)

            def queries(c, b, first):
                act.wait_ge(qkv_done, c + 1)
                if not first:
                    act.wait_ge(scores_done, c - 1)
                act.activation(qk[b][:].rearrange("d j s -> d (j s)"), qkv_ps[b][:, 0:2 * WIN],
                               ACT.Copy).then_inc(qk_ready, 1)

            def values(c, b, first):
                if not first:
                    act.wait_ge(o_done, c - 1)
                v = qkv_ps[b][:, 2 * D:4 * D].rearrange("s (r g t d) -> s r g t d", r=2, t=2, d=HD)
                for t in range(2):
                    half = slice(t * WIN, (t + 1) * WIN)
                    act.activation(vbd[b][half, :, :, t, :], v[half, :, :, t, :], ACT.Copy)\
                       .then_inc((v0_ready, vbd_ready)[t], 1)

            def probs(c, b, first):
                act.wait_ge(shifted, c + 1)
                if not first:
                    act.wait_ge(probs_turned, c - 1)
                    act.wait_ge(sum_done, c - 1)
                act.activation(pr[b][:], sc[b][:], ACT.Exp).then_inc(exp_done, 1)

            def turned(c, b, first):
                act.wait_ge(probs_turned, c + 1)
                if not first:
                    act.wait_ge(o_done, c - 1)
                act.activation(prT[b][:], t_ps[b][:], ACT.Copy).then_inc(probsT_ready, 1)

            def outT(c, b):
                act.wait_ge(o_turned, c + 1)
                act.activation(oT[b][0:D, :], o_ps[b][0:D, 128:256], ACT.Copy).then_inc(oT_ready, 1)

            def step(c, b, first=False, start=False, end=False, last=False):
                turned(c, b, first)
                if not end:
                    queries(c + 2, b, False)
                if not start:
                    outT(c - 1, 1 - b)
                if not last:
                    probs(c + 1, 1 - b, start)
                if not end:
                    values(c + 2, b, False)

            for b in range(2):
                queries(b, b, True)
                values(b, b, True)
            probs(0, 0, True)
            step(0, 0, first=True, start=True)
            step(1, 1, first=True)
            with act.Fori(1, n // 2 - 1) as i:
                for b in range(2):
                    step(2 * i + b, b)
            step(n - 2, 0, end=True)
            step(n - 1, 1, end=True, last=True)
            outT(n - 1, 1)

        @block.vector
        def _(dve):
            def keys(c, b, first):
                dve.wait_ge(qk_ready, c + 1)
                if not first:
                    dve.wait_ge(scores_done, c - 1)
                dve.tensor_tensor(kbd[b][:], bc_at(qk[b][:, 1, :], 1, NH),
                                  bc(k.headmask[:, 0, :], WIN), ALU.mult).then_inc(kbd_ready, 1)

            def bias(c, b, first):
                dve.wait_ge(scores_done, c + 1)
                if not first:
                    dve.wait_ge(exp_done, c - 1)
                dve.scalar_tensor_tensor(sc[b][:], s_ps[b][:], float(HD) ** -0.5, k.relbias[:], ALU.mult,
                                         ALU.add).then_inc(biased, 1)
                dve.wait_ge(biased, c + 1)
                if not first:
                    dve.wait_ge(shifted, c - 1)
                dve.tensor_reduce(mx[b][:], sc[b][:], AX.X, ALU.max).then_inc(max_done, 1)

            def sums(c, b, first):
                dve.wait_ge(exp_done, c + 1)
                dve.tensor_reduce(sm[b][:], pr[b][:], AX.X, ALU.add).then_inc(sum_done, 1)
                dve.wait_ge(sum_done, c + 1)
                dve.reciprocal(rs[b][:], sm[b][:]).then_inc(rsum_done, 1)

            def scale(c, b, first):
                dve.wait_ge(rsum_done, c + 1)
                dve.wait_ge(o_done, c + 1)
                if not first:
                    dve.wait_ge(o_turned, c - 1)
                dve.tensor_tensor(o[b][:].rearrange("q (h d) -> q h d", d=HD),
                                  o_ps[b][:, 0:D].rearrange("q (h d) -> q h d", d=HD),
                                  bc(rs[b][:], HD), ALU.mult).then_inc(o_scaled, 1)

            def add(c, b):
                dve.wait_ge(proj_done, c + 1)
                dve.tensor_tensor(h[:, bass.ds(c, 1), :].rearrange("p a d -> p (a d)"),
                                  h[:, bass.ds(c, 1), :].rearrange("p a d -> p (a d)"),
                                  o_ps[b][:, 64:128], ALU.add).then_inc(added, 1)

            for b in range(2):
                dve.memset(oT[b][D:D + 1, :], 1.0).then_inc(ones, 1)
            for b in range(2):
                keys(b, b, True)
                bias(b, b, True)
            sums(0, 0, True)
            first_merge = MERGES_LOADING + MERGES_TOKENS
            for c in range(n):
                b = c % 2
                if c + 2 < n:
                    keys(c + 2, b, False)
                sort.merge(dve, first_merge + (len(sort.network) - first_merge) * (c + 1) // n)
                scale(c, b, c < 2)
                if c > 0:
                    add(c - 1, 1 - b)
                if c + 2 < n:
                    bias(c + 2, b, False)
                if c + 1 < n:
                    sums(c + 1, 1 - b, False)
            add(n - 1, 1)
            sort.find_digits(dve)


class EdgeSort:

    def __init__(self, mem):
        self.src, self.dst = mem.sb("edge_src", [P, EC], I32), mem.sb("edge_dst", [P, EC], I32)
        self.keys, self.other = mem.sb("edge_keys", [P, EC]), mem.sb("sort_other", [P, EC])
        self.lo, self.hi = mem.sb("edge_dst_lo", [P, EC], I32), mem.sb("edge_dst_hi", [P, EC], I32)
        self.last_lo, self.last_hi = mem.sb("last_dst_lo", [P, EC], BF16), mem.sb("last_dst_hi", [P, EC], BF16)
        self.stat, self.top = mem.sb("edge_stat", [P, 4]), mem.sb("edge_top", [P, 4])
        self.lim = mem.sb("edge_limits", [P, 4], I32)
        self.limits = mem.sb("column_limits", [P, 3], I32)
        self.loaded, self.step = mem.sem("edges_loaded"), mem.sem("sort_step")
        self.counted, self.reduced = mem.sem("classes_counted"), mem.sem("classes_reduced")
        self.network = []
        run = 2
        while run <= EC:
            self.network += [(run, None)] + [(run, run // 4 >> i) for i in range((run // 2).bit_length() - 1)]
            run *= 2
        self.done = 0
        self.merges = 0

    def load(self, sp, edges):
        edges = edges.rearrange("a (p c) -> a p c", p=P)
        sp.dma_start(self.src[:], edges[0]).then_inc(self.loaded, 16)
        sp.dma_start(self.dst[:], edges[1]).then_inc(self.loaded, 16)

    def after(self, dve, ins):
        ins.then_inc(self.step, 1)
        self.done += 1
        dve.wait_ge(self.step, self.done)

    def form_keys(self, dve):
        A, B, src, dst = self.keys[:], self.other[:], self.src, self.dst
        dve.wait_ge(self.loaded, 32)
        self.after(dve, dve.tensor_scalar(A, src[:], float(M - 1), None, ALU.min))
        self.after(dve, dve.scalar_tensor_tensor(B, dst[:], float(M), A, ALU.mult, ALU.add))
        C = self.lo[:].bitcast(F32)
        self.after(dve, dve.tensor_scalar(C, dst[:], float(2 - M), CLASS_LAST - (M - 1), ALU.mult, ALU.add))
        self.after(dve, dve.scalar_tensor_tensor(C, A, float(M - 1), C, ALU.is_equal, ALU.mult))
        self.after(dve, dve.tensor_tensor(B, B, C, ALU.add))
        self.after(dve, dve.tensor_scalar(C, dst[:], float(M), CLASS_NONE, ALU.is_ge, ALU.mult))
        self.after(dve, dve.scalar_tensor_tensor(A, B, CLASS_NONE, C, ALU.min, ALU.max))

    def merge(self, dve, until):
        while self.merges < until:
            run, dist = self.network[self.merges]
            cur, nxt = (self.keys, self.other) if self.merges % 2 == 0 else (self.other, self.keys)
            if dist is None:
                x, y = (t[:].rearrange("p (n r) -> p n r", r=run) for t in (cur, nxt))
                low, high = slice(0, run // 2), slice(run - 1, run // 2 - 1, -1)
                ins = ((y[:, :, low], x[:, :, low]), (y[:, :, high], x[:, :, high]))
            else:
                x, y = (t[:].rearrange("p (n t r) -> p n t r", t=2, r=dist) for t in (cur, nxt))
                ins = ((y[:, :, 0], x[:, :, 0]), (y[:, :, 1], x[:, :, 1]))
            dve.wait_ge(self.step, self.done)
            dve.tensor_tensor(ins[0][0], ins[0][1], ins[1][1], ALU.min).then_inc(self.step, 1)
            dve.tensor_tensor(ins[1][0], ins[0][1], ins[1][1], ALU.max).then_inc(self.step, 1)
            self.done += 2
            self.merges += 1

    def find_digits(self, dve):
        A, C = self.keys[:], self.other[:]
        assert self.merges == len(self.network) and self.merges % 2 == 0, "the sorted keys are in their place"
        key, src, dst, lo, hi, stat = self.hi, self.src, self.dst, self.lo, self.hi, self.stat
        dve.wait_ge(self.step, self.done)
        self.after(dve, dve.tensor_scalar(C, A, CLASS_LAST, 0.0, ALU.is_lt, ALU.add, accum_out=stat[:, 0:1]))
        self.after(dve, dve.tensor_scalar(C, A, CLASS_NONE, 0.0, ALU.is_lt, ALU.add, accum_out=stat[:, 1:2]))
        dve.tensor_scalar(stat[:, 2:3], stat[:, 0:1], -1.0, None, ALU.mult).then_inc(self.counted, 1)
        self.after(dve, dve.tensor_copy(key[:], A))
        self.after(dve, dve.tensor_scalar(lo[:], key[:], 8, None, ALU.arith_shift_right))
        self.after(dve, dve.tensor_scalar(self.last_hi[:], lo[:], CLASS_LAST / 256, None, ALU.subtract))
        self.after(dve, dve.tensor_scalar(lo[:], key[:], 1, P - 1, ALU.arith_shift_right, ALU.bitwise_and))
        self.after(dve, dve.tensor_copy(self.last_lo[:], lo[:]))
        self.after(dve, dve.tensor_scalar(src[:], key[:], M - 1, None, ALU.bitwise_and))
        self.after(dve, dve.tensor_scalar(dst[:], key[:], 12, None, ALU.arith_shift_right))
        self.after(dve, dve.tensor_scalar(lo[:], dst[:], P - 1, None, ALU.bitwise_and))
        self.after(dve, dve.tensor_scalar(hi[:], dst[:], 7, None, ALU.arith_shift_right))
        self.after(dve, dve.tensor_scalar(dst[:], dst[:], float(M - 1), None, ALU.min))

    def find_limits(self, nc):
        top, lim, limits = self.top, self.lim, self.limits
        with nc.Block() as block:
            @block.gpsimd
            def _(pool):
                pool.wait_ge(self.counted, 1)
                pool.partition_all_reduce(top[:, 0:3], self.stat[:, 0:3], P, bass.bass_isa.ReduceOp.max)\
                    .then_inc(self.reduced, 1)

            @block.vector
            def _(dve):
                def after(ins):
                    self.after(dve, ins)
                dve.wait_ge(self.reduced, 1)
                after(dve.tensor_scalar(lim[:, 0:1], top[:, 0:1], -1.0, None, ALU.add))
                after(dve.tensor_scalar(lim[:, 1:2], top[:, 1:2], float(2 * CCH - 1), None, ALU.add))
                after(dve.tensor_scalar(lim[:, 2:3], top[:, 2:3], -1.0, float(EC - 1), ALU.mult, ALU.min))
                sh = (2 * GCH).bit_length() - 1
                after(dve.tensor_scalar(lim[:, 0:1], lim[:, 0:1], sh, None, ALU.arith_shift_right))
                sh = (2 * CCH).bit_length() - 1
                after(dve.tensor_scalar(lim[:, 1:3], lim[:, 1:3], sh, None, ALU.arith_shift_right))
                after(dve.tensor_scalar(limits[:, 0:1], lim[:, 0:1], float(EXPERT_PAIRS), None, ALU.max))
                after(dve.tensor_scalar(lim[:, 2:3], lim[:, 2:3],
                                        float(EC // (2 * CCH) - COUNT_PAIRS - 1), None, ALU.min))
                after(dve.tensor_tensor(lim[:, 3:4], lim[:, 1:2], lim[:, 2:3], ALU.subtract))
                after(dve.tensor_scalar(limits[:, 1:2], lim[:, 3:4],
                                        float(COUNT_PAIRS + 1), None, ALU.max))
                after(dve.tensor_copy(limits[:, 2:3], lim[:, 2:3]))


def graph_router(nc, mem, a, k, hg, sort, xT, ys, gates):
    W = GH * GE
    srow, drow = mem.sb("src_rows", [P, TILES, NSRC]), mem.sb("dst_rows", [P, TILES, NDST])
    srow_dram = nc.dram_tensor("src_rows_dram", (M, NSRC), F32, kind="Internal").ap()
    drow_dram = nc.dram_tensor("dst_rows_dram", (M, NDST), F32, kind="Internal").ap()
    last, counts = mem.sb("last_row", [P, NSRC]), mem.sb("last_counts", [P, TILES])
    prod = mem.sb("router_prod", [P, TILES, W])
    e = mem.sb("router_e", [P, 3, TILES, GH])
    mx, top = mem.sb("src_max", [P, GH]), mem.sb("src_top", [P, GH])
    own = mem.sb("own_values", [P, TILES, GH, GE + 1])
    from_last = mem.sb("values_from_last", [P, TILES, GH, GE + 1])
    step, own_step = mem.sem("nodes_step"), mem.sem("own_step")
    src_ready, dst_ready, max_ready, top_ready = (
        mem.sem(x) for x in ("src_rows_ready", "dst_rows_ready", "src_max_ready", "src_top_ready"))
    src_stored, last_loaded, dst_stored = mem.sem("src_rows_stored"), mem.sem("last_row_loaded"), mem.sem("dst_rows_stored")
    self_shift, last_shift, self_exp, last_exp = (
        mem.sem(x) for x in ("self_shifted", "last_shifted", "self_exp", "last_exp"))
    sview = srow[:, :, W:NSRC]
    dview, mview = drow[:, :, 0:GH], drow[:, :, GH:NDST]
    with nc.Block() as block:
        @block.vector
        def _(dve):
            done = 0

            def after(ins):
                nonlocal done
                ins.then_inc(step, 1)
                done += 1
                dve.wait_ge(step, done)

            after(dve.tensor_tensor(prod[:], hg[:], bc_at(k.att_src[:], 1, TILES), ALU.mult))
            dve.tensor_copy(srow[:, :, 0:W], hg[:]).then_inc(src_ready, 1)
            dve.tensor_reduce(sview, prod[:].rearrange("p t (h e) -> p t h e", e=GE), AX.X,
                              ALU.add).then_inc(src_ready, 1)
            dve.wait_ge(src_ready, 2)
            dve.tensor_reduce(mx[:], sview.rearrange("p t h -> p h t"), AX.X, ALU.max).then_inc(max_ready, 1)
            after(dve.tensor_tensor(prod[:], hg[:], bc_at(k.att_dst[:], 1, TILES), ALU.mult))
            after(dve.tensor_reduce(dview, prod[:].rearrange("p t (h e) -> p t h e", e=GE), AX.X, ALU.add))
            dve.wait_ge(top_ready, 1)
            after(dve.tensor_tensor(e[:, 0], dview, bc_at(top[:], 1, TILES), ALU.add))
            dve.scalar_tensor_tensor(mview, e[:, 0], 0.2, e[:, 0], ALU.mult, ALU.max).then_inc(dst_ready, 1)
            dve.wait_ge(dst_ready, 1)

        @block.gpsimd
        def _(pool):
            pool.wait_ge(max_ready, 1)
            pool.partition_all_reduce(top[:], mx[:], P, bass.bass_isa.ReduceOp.max).then_inc(top_ready, 1)

        @block.sync
        def _(sp):
            sp.wait_ge(src_ready, 2)
            sp.dma_start(srow_dram.rearrange("(t p) f -> p t f", p=P), srow[:]).then_inc(src_stored, 16)
            sp.wait_ge(src_stored, 16)
            sp.dma_start(last[:], bass.AP(srow_dram.tensor, (M - 1) * NSRC, [[0, P], [1, NSRC]]))\
              .then_inc(last_loaded, 16)
            sp.wait_ge(dst_ready, 1)
            sp.dma_start(drow_dram.rearrange("(t p) f -> p t f", p=P), drow[:]).then_inc(dst_stored, 16)
            sp.wait_ge(dst_stored, 16)

    loop = Stage(mem)
    olo = [loop.sb(f"edge_onehot_lo{b}", [P, GCH, P]) for b in range(2)]
    ohi = [loop.sb(f"edge_onehot_hi{b}", [P, GCH, TILES]) for b in range(2)]
    gs = [loop.sb(f"edge_src_row{b}", [P, GCH, NSRC]) for b in range(2)]
    gd = [loop.sb(f"edge_dst_row{b}", [P, GCH, NDST]) for b in range(2)]
    ee = [loop.sb(f"edge_e{b}", [P, 2, GCH, GH]) for b in range(2)]
    spread = [loop.sb(f"edge_spread{b}", [P, GCH, TILES, NV]) for b in range(2)]
    si, di = ([loop.sb(f"edge_{x}_index{b}", [P, GCH], I32) for b in range(2)] for x in ("src", "dst"))
    clo = [loop.sb(f"count_onehot_lo{b}", [P, CCH, P], BF16) for b in range(2)]
    chi = [loop.sb(f"count_onehot_hi{b}", [P, CCH, TILES], BF16) for b in range(2)]
    hs = [loop.sb(f"moe0_hidden{b}", [P, 512]) for b in range(2)]
    vals = mem.ps("edge_values", [P, 2, GCH, GH, GE + 1])
    val = [vals[:, b] for b in range(2)]
    iota, iota_ready = mem.ps("iota_in_psum", [P, 512]), mem.sem("iota_ready")
    iota_row = iota[:, 0:P]
    acc = mem.ps("edge_acc", [P, 2, 512])
    HALF = TILES // 2 * NV
    count_acc = acc[:, 0, HALF:HALF + TILES]
    h_ps = [mem.ps(f"moe0_h_ps{b}", [P, 512]) for b in range(2)]
    y_ps = [mem.ps(f"moe0_y_ps{b}", [P, 512]) for b in range(2)]
    (index_ready, olo_ready, ohi_ready, added, leaky, shifted, exp_done, weighted, spread_ready, used,
     summed) = (mem.sem("edge_" + x) for x in (
         "index_ready", "olo_ready", "ohi_ready", "added", "leaky", "shifted", "exp_done", "weighted",
         "spread_ready", "used", "summed"))
    clo_ready, chi_ready, counted = (mem.sem("count_" + x) for x in ("lo_ready", "hi_ready", "used"))
    h_done, gelu_done, y_done, y_saved = (mem.sem("moe0_" + x) for x in ("h_done", "gelu_done", "y_done", "y_saved"))
    gathered = [mem.sem(f"edge_gathered{b}") for b in range(2)]
    PAIRS = EC // (2 * GCH)
    CPAIRS = EC // (2 * CCH)
    w1, w2 = k.w1[0], k.w2[0]

    with nc.Block() as block:
        @block.vector
        def _(dve):
            done = 0

            def after(ins):
                nonlocal done
                ins.then_inc(own_step, 1)
                done += 1
                dve.wait_ge(own_step, done)

            def chunk(c, b, first, turn):
                dve.wait_ge(gathered[b], turn)
                dve.tensor_tensor(ee[b][:, 0], gs[b][:, :, W:NSRC], gd[b][:, :, 0:GH], ALU.add).then_inc(added, 1)
                dve.wait_ge(added, c + 1)
                dve.scalar_tensor_tensor(ee[b][:, 1], ee[b][:, 0], 0.2, ee[b][:, 0], ALU.mult,
                                         ALU.max).then_inc(leaky, 1)
                dve.wait_ge(leaky, c + 1)
                dve.tensor_tensor(ee[b][:, 0], ee[b][:, 1], gd[b][:, :, GH:NDST], ALU.subtract).then_inc(shifted, 1)
                dve.wait_ge(exp_done, c + 1)
                dve.tensor_tensor(val[b][:, :, :, 0:GE], gs[b][:, :, 0:W].rearrange("p c (h e) -> p c h e", e=GE),
                                  bc(val[b][:, :, :, GE], GE), ALU.mult).then_inc(weighted, 1)
                if not first:
                    dve.wait_ge(used, c - 1)
                dve.tensor_tensor(olo[b][:], bc_at(iota_row, 1, GCH), bc(sort.lo[:, bass.ts(c, GCH)], P),
                                  ALU.is_equal).then_inc(olo_ready, 1)
                dve.tensor_tensor(ohi[b][:], bc_at(iota[:, 0:TILES], 1, GCH),
                                  bc(sort.hi[:, bass.ts(c, GCH)], TILES), ALU.is_equal).then_inc(ohi_ready, 1)
                dve.wait_ge(weighted, c + 1)
                dve.wait_ge(ohi_ready, c + 1)
                dve.tensor_tensor(spread[b][:], bc_at(val[b][:].rearrange("p c h e -> p c (h e)"), 2, TILES),
                                  bc(ohi[b][:], NV), ALU.mult).then_inc(spread_ready, 1)

            def count(pair):
                column = nc.s_assert_within(at + pair, 0, CPAIRS - 1)
                for q in range(2):
                    c = 2 * pair + q
                    dve.wait_ge(counted, c + 1)
                    part = bass.ds(column * (2 * CCH) + q * CCH, CCH)
                    dve.tensor_tensor(clo[q][:], bc_at(iota_row, 1, CCH), bc(sort.last_lo[:, part], P),
                                      ALU.is_equal).then_inc(clo_ready, 1)
                    dve.tensor_tensor(chi[q][:], bc_at(iota[:, 0:TILES], 1, CCH),
                                      bc(sort.last_hi[:, part], TILES), ALU.is_equal).then_inc(chi_ready, 1)

            def save(i, e):
                dve.wait_ge(y_done, 4 * i + e + 1)
                dve.tensor_tensor(ys[e][:, bass.ts(i, 4), :], y_ps[e % 2][:, 0:4 * D].rearrange("p (t d) -> p t d", d=D),
                                  bc_at(k.b2_rows[:, e, :], 1, 4), ALU.add).then_inc(y_saved, 1)

            n = dve.value_load(sort.limits[0:1, 0:1], min_val=EXPERT_PAIRS, max_val=PAIRS - 1)
            m = dve.value_load(sort.limits[0:1, 1:2], min_val=COUNT_PAIRS + 1, max_val=CPAIRS)
            at = dve.value_load(sort.limits[0:1, 2:3], min_val=0, max_val=CPAIRS - COUNT_PAIRS - 1)
            dve.tensor_copy(iota_row, k.iota_lo[:]).then_inc(iota_ready, 1)
            after(dve.tensor_tensor(e[:, 0], dview, sview, ALU.add))
            after(dve.scalar_tensor_tensor(e[:, 1], e[:, 0], 0.2, e[:, 0], ALU.mult, ALU.max))
            dve.tensor_tensor(e[:, 0], e[:, 1], mview, ALU.subtract).then_inc(self_shift, 1)
            dve.wait_ge(last_loaded, 16)
            dve.wait_ge(self_shift, 1)
            after(dve.tensor_tensor(e[:, 1], dview, bc_at(last[:, W:NSRC], 1, TILES), ALU.add))
            after(dve.scalar_tensor_tensor(e[:, 2], e[:, 1], 0.2, e[:, 1], ALU.mult, ALU.max))
            dve.tensor_tensor(e[:, 1], e[:, 2], mview, ALU.subtract).then_inc(last_shift, 1)
            dve.wait_ge(self_exp, 1)
            after(dve.tensor_tensor(own[:, :, :, 0:GE], hg[:].rearrange("p t (h e) -> p t h e", e=GE),
                                    bc(own[:, :, :, GE], GE), ALU.mult))
            dve.wait_ge(last_exp, 1)
            for hh in range(GH):
                after(dve.tensor_tensor(from_last[:, :, hh, 0:GE], bc_at(last[:, hh * GE:(hh + 1) * GE], 1, TILES),
                                        bc(from_last[:, :, hh, GE], GE), ALU.mult))
            dve.wait_ge(iota_ready, 1)
            for b in range(2):
                chunk(b, b, True, 256)
                for x in range(2 * b, 2 * b + 2):
                    save(0, x)
            with dve.Fori(1, EXPERT_PAIRS) as i:
                for b in range(2):
                    chunk(2 * i + b, b, False, 256 * i + 256)
                    count(2 * (i - 1) + b)
                    for x in range(2 * b, 2 * b + 2):
                        save(i, x)
            with dve.Fori(EXPERT_PAIRS, n + 1) as i:
                for b in range(2):
                    chunk(2 * i + b, b, False, 256 * i + 256)
            with dve.Fori(COUNT_PAIRS, m) as i:
                count(i)

        @block.gpsimd
        def _(pool):
            def gather(c, b, first):
                if not first:
                    pool.wait_ge(weighted, c - 1)
                pool.tensor_copy(si[b][:], sort.src[:, bass.ts(c, GCH)]).then_inc(index_ready, 1)
                pool.tensor_copy(di[b][:], sort.dst[:, bass.ts(c, GCH)]).then_inc(index_ready, 1)
                pool.wait_ge(index_ready, 2 * c + 2)
                pool.sem_inc(k.pool_passed, 1)
                for j in range(GCH):
                    pool.indirect_dma_start(gs[b][:, j, :], None, srow_dram,
                                            bass.IndirectOffsetOnAxis(si[b][:, j:j + 1], axis=0))\
                        .then_inc(gathered[b], 16)
                    pool.indirect_dma_start(gd[b][:, j, :], None, drow_dram,
                                            bass.IndirectOffsetOnAxis(di[b][:, j:j + 1], axis=0))\
                        .then_inc(gathered[b], 16)

            pool.wait_ge(dst_stored, 16)
            n = pool.value_load(sort.limits[0:1, 0:1], min_val=EXPERT_PAIRS, max_val=PAIRS - 1)
            gather(0, 0, True)
            gather(1, 1, True)
            with pool.Fori(1, n + 1) as i:
                for b in range(2):
                    gather(2 * i + b, b, False)

        @block.scalar
        def _(act):
            def exps(c, b):
                act.wait_ge(shifted, c + 1)
                act.activation(val[b][:, :, :, GE], ee[b][:, 0], ACT.Exp).then_inc(exp_done, 1)

            def gelu(i, e, first):
                act.wait_ge(h_done, 4 * i + e + 1)
                if not first:
                    act.wait_ge(y_done, 4 * i + e - 1)
                act.activation(hs[e % 2][:], h_ps[e % 2][:], ACT.Gelu).then_inc(gelu_done, 1)

            n = act.value_load(sort.limits[0:1, 0:1], min_val=EXPERT_PAIRS, max_val=PAIRS - 1)
            act.wait_ge(self_shift, 1)
            act.activation(own[:, :, :, GE], e[:, 0], ACT.Exp).then_inc(self_exp, 1)
            act.wait_ge(last_shift, 1)
            act.activation(from_last[:, :, :, GE], e[:, 1], ACT.Exp).then_inc(last_exp, 1)
            for b in range(2):
                exps(b, b)
                for x in range(2 * b, 2 * b + 2):
                    gelu(0, x, x < 2)
            with act.Fori(1, EXPERT_PAIRS) as i:
                for b in range(2):
                    exps(2 * i + b, b)
                    for x in range(2 * b, 2 * b + 2):
                        gelu(i, x, False)
            with act.Fori(EXPERT_PAIRS, n + 1) as i:
                for b in range(2):
                    exps(2 * i + b, b)

        @block.tensor
        def _(pe):
            def sums(c, b):
                pe.wait_ge(olo_ready, c + 1)
                pe.wait_ge(spread_ready, c + 1)
                for j in range(GCH):
                    rows = spread[b][:, j].rearrange("p t v -> p (t v)")
                    for half in range(2):
                        ins = pe.matmul(acc[:, half, 0:HALF], olo[b][:, j, :],
                                        rows[:, half * HALF:(half + 1) * HALF], start=False, stop=False,
                                        skip_group_check=True)
                ins.then_inc(used, 1)

            def count(pair):
                for q in range(2):
                    pe.wait_ge(clo_ready, 2 * pair + q + 1)
                    pe.wait_ge(chi_ready, 2 * pair + q + 1)
                    for j in range(CCH):
                        ins = pe.matmul(count_acc, clo[q][:, j, :], chi[q][:, j, :], start=False, stop=False,
                                        skip_group_check=True)
                    ins.then_inc(counted, 1)

            def experts(i, two, first):
                for x in two:
                    if not first:
                        pe.wait_ge(gelu_done, 4 * i + x - 1)
                    pe.matmul(h_ps[x % 2][:], w1[:, x, :], xT[:, bass.ts(i, 512)]).then_inc(h_done, 1)
                for x in two:
                    pe.wait_ge(gelu_done, 4 * i + x + 1)
                    if not first:
                        pe.wait_ge(y_saved, 4 * i + x - 1)
                    for t in range(4):
                        ins = pe.matmul(y_ps[x % 2][:, t * D:(t + 1) * D], hs[x % 2][:, t * P:(t + 1) * P],
                                        w2[:, x, :])
                    ins.then_inc(y_done, 1)

            n = pe.value_load(sort.limits[0:1, 0:1], min_val=EXPERT_PAIRS, max_val=PAIRS - 1)
            m = pe.value_load(sort.limits[0:1, 1:2], min_val=COUNT_PAIRS + 1, max_val=CPAIRS)
            pe.sem_inc(counted, 2)
            for part in (acc[:, 0, 0:HALF], acc[:, 1, 0:HALF], count_acc):
                pe.matmul(part, k.zero_mm[:, 0:P], k.zero_mm[:, 0:part.shape[1]], start=True, stop=False,
                          skip_group_check=True)
            experts(0, (0, 1), True)
            sums(0, 0)
            experts(0, (2, 3), False)
            with pe.Fori(1, EXPERT_PAIRS) as i:
                for b in range(2):
                    sums(2 * i + b - 1, 1 - b)
                    experts(i, (2 * b, 2 * b + 1), False)
                    count(2 * (i - 1) + b)
            with pe.Fori(EXPERT_PAIRS, n + 1) as i:
                for b in range(2):
                    sums(2 * i + b - 1, 1 - b)
            sums(2 * n + 1, 1)
            with pe.Fori(COUNT_PAIRS, m) as i:
                count(i)
            for part in (acc[:, 0, 0:HALF], acc[:, 1, 0:HALF], count_acc):
                ins = pe.matmul(part, k.zero_mm[:, 0:P], k.zero_mm[:, 0:part.shape[1]], start=False, stop=True,
                                skip_group_check=True)
            ins.then_inc(summed, 1)

    loop.ctx.close()
    agg, nrm, sq = mem.sb("agg", [P, TILES, W]), mem.sb("agg_norm", [P, TILES, W]), mem.sb("agg_sq", [P, TILES, W])
    st = mem.sb("agg_stats", [P, 5, TILES])
    scores = mem.sb("router_scores", [P, TILES, E0])
    rden = mem.sb("router_rden", [P, TILES, GH])
    centered, squared, var_ready, std_ready = (
        mem.sem(f"agg_{x}") for x in ("centered", "squared", "var_ready", "std_ready"))
    fstep = mem.sem("agg_step")
    with nc.Block() as block:
        @block.vector
        def _(dve):
            done = 0

            def after(ins):
                nonlocal done
                ins.then_inc(fstep, 1)
                done += 1
                dve.wait_ge(fstep, done)

            after(dve.tensor_copy(counts[:], count_acc))
            flat = from_last[:].rearrange("p t h e -> p t (h e)")
            after(dve.tensor_tensor(flat, flat, bc(counts[:], NV), ALU.mult))
            after(dve.tensor_tensor(own[:], own[:], from_last[:], ALU.add))
            for half in range(2):
                part = own[:, half * 16:(half + 1) * 16].rearrange("p t h e -> p (t h e)")
                after(dve.tensor_tensor(part, part, acc[:, half, 0:HALF], ALU.add))
            after(dve.tensor_scalar(rden[:], own[:, :, :, GE], 1e-16, None, ALU.add))
            after(dve.reciprocal(rden[:], rden[:]))
            after(dve.tensor_tensor(agg[:].rearrange("p t (h e) -> p t h e", e=GE), own[:, :, :, 0:GE],
                                    bc(rden[:], GE), ALU.mult))
            after(dve.tensor_tensor(agg[:], agg[:], bc_at(k.b_gat[:], 1, TILES), ALU.add))
            after(dve.tensor_reduce(st[:, 0], agg[:], AX.X, ALU.add))
            after(dve.tensor_scalar(st[:, 1], st[:, 0], 1.0 / W, None, ALU.mult))
            dve.tensor_tensor(nrm[:], agg[:], bc(st[:, 1], W), ALU.subtract).then_inc(centered, 1)
            dve.wait_ge(squared, 1)
            dve.tensor_reduce(st[:, 2], sq[:], AX.X, ALU.add).then_inc(var_ready, 1)
            dve.wait_ge(std_ready, 1)
            after(dve.reciprocal(st[:, 4], st[:, 3]))
            after(dve.tensor_tensor(agg[:], nrm[:], bc(st[:, 4], W), ALU.mult))
            after(dve.tensor_tensor(agg[:], agg[:], bc_at(k.ln_gamma[:], 1, TILES), ALU.mult))
            after(dve.tensor_tensor(agg[:], agg[:], bc_at(k.ln_beta[:], 1, TILES), ALU.add))
            after(dve.tensor_reduce(scores[:], agg[:].rearrange("p t (h e) -> p t e h", e=GE), AX.X, ALU.add))
            after(dve.tensor_scalar(scores[:], scores[:], 1.0 / GH, None, ALU.mult))

        @block.scalar
        def _(act):
            act.wait_ge(centered, 1)
            act.activation(sq[:], nrm[:], ACT.Square).then_inc(squared, 1)
            act.wait_ge(var_ready, 1)
            act.activation(st[:, 3], st[:, 2], ACT.Sqrt, bias=k.eps[:, 0:1], scale=1.0 / W).then_inc(std_ready, 1)

    choose(nc, mem, k.lower0, E0, scores, gates, "moe0")


def choose(nc, mem, lower, E, scores, gates, name):
    ahead, same = mem.sb(f"{name}_ahead", [P, TILES, E, E]), mem.sb(f"{name}_same", [P, TILES, E, E])
    sel, z = mem.sb(f"{name}_sel", [P, TILES, E]), mem.sb(f"{name}_z", [P, TILES, E])
    s = mem.sb(f"{name}_top", [P, 3, TILES])
    step, shifted, exp_done = (mem.sem(f"{name}_choose_{x}") for x in ("step", "shifted", "exp_done"))
    with nc.Block() as block:
        @block.vector
        def _(dve):
            done = 0

            def after(ins):
                nonlocal done
                ins.then_inc(step, 1)
                done += 1
                dve.wait_ge(step, done)

            after(dve.tensor_reduce(s[:, 0], scores[:], AX.X, ALU.max))
            dve.tensor_tensor(z[:], scores[:], bc(s[:, 0], E), ALU.subtract).then_inc(shifted, 1)
            others, own = bc_at(scores[:], 2, E), bc(scores[:], E)
            after(dve.tensor_tensor(same[:], others, own, ALU.is_equal))
            low = lower[:].rearrange("p e j -> p (e j)")
            after(dve.tensor_tensor(same[:].rearrange("p t e j -> p t (e j)"),
                                    same[:].rearrange("p t e j -> p t (e j)"), bc_at(low, 1, TILES), ALU.mult))
            after(dve.tensor_tensor(ahead[:], others, own, ALU.is_gt))
            after(dve.tensor_tensor(ahead[:], ahead[:], same[:], ALU.add))
            after(dve.tensor_reduce(sel[:], ahead[:], AX.X, ALU.add))
            dve.wait_ge(exp_done, 1)
            after(dve.scalar_tensor_tensor(sel[:], sel[:], 2.0, z[:], ALU.is_lt, ALU.mult))
            after(dve.tensor_reduce(s[:, 1], sel[:], AX.X, ALU.add))
            after(dve.reciprocal(s[:, 2], s[:, 1]))
            after(dve.tensor_tensor(gates[:], sel[:], bc(s[:, 2], E), ALU.mult))

        @block.scalar
        def _(act):
            act.wait_ge(shifted, 1)
            act.activation(z[:], z[:], ACT.Exp).then_inc(exp_done, 1)


def combine(nc, mem, ys, gates, h):
    parts = {"vector": slice(0, 20), "gpsimd": slice(20, TILES)}
    added, scaled = ({e: mem.sem(f"combine_{e}_{x}") for e in parts} for x in ("added", "scaled"))

    def total(eng, name):
        part = parts[name]
        for e in range(E0):
            y = ys[e][:, part, :]
            eng.tensor_tensor(y, y, bc(gates[:, part, e], D), ALU.mult).then_inc(scaled[name], 1)
        for e in range(E0):
            eng.wait_ge(scaled[name], e + 1)
            if e:
                eng.wait_ge(added[name], e)
            eng.tensor_tensor(h[:, part, :], h[:, part, :], ys[e][:, part, :], ALU.add).then_inc(added[name], 1)

    with nc.Block() as block:
        @block.vector
        def _(dve):
            total(dve, "vector")

        @block.gpsimd
        def _(pool):
            total(pool, "gpsimd")


def experts(nc, mem, k, layer, E, xT, gates, h):
    w1, w2, b2 = k.w1[layer], k.w2[layer], k.b2
    nm = f"moe{layer}_"
    g = mem.sb(nm + "g", [P, 4, E])
    gT = mem.sb(nm + "gT", [4 * E, P])
    hs = [mem.sb(f"{nm}hidden{b}", [P, 512]) for b in range(2)]
    tmp = [mem.sb(f"{nm}weighted{b}", [P, 4, D]) for b in range(2)]
    acc = mem.sb(nm + "acc", [P, 4, D])
    h_ps = [mem.ps(f"{nm}h_ps{b}", [P, 512]) for b in range(2)]
    y_ps = [mem.ps(f"{nm}y_ps{b}", [P, 4, D]) for b in range(2)]
    g_ps = mem.ps(nm + "g_ps", [4 * E, P])
    b_ps = mem.ps(nm + "b_ps", [P, 4, D])
    (g_ready, g_turned, gT_ready, b_done, acc_ready, h_done, gelu_done, y_done, weighted, added) = (
        mem.sem(nm + x) for x in ("g_ready", "g_turned", "gT_ready", "b_done", "acc_ready", "h_done", "gelu_done",
                                  "y_done", "weighted", "added"))
    n = TILES // 4
    with nc.Block() as block:
        @block.tensor
        def _(pe):
            pe.sem_inc(y_done, 2)
            with pe.Fori(0, n) as c:
                u = c * E

                def hidden(e):
                    pe.wait_ge(gelu_done, u + e + 1)
                    ins = pe.matmul(h_ps[e % 2][:], w1[:, e, :], xT[:, bass.ts(c, 512)])
                    ins.then_inc(h_done, 1)

                def output(e):
                    pe.wait_ge(gelu_done, u + e + 3)
                    pe.wait_ge(weighted, u + e + 1)
                    for t in range(4):
                        ins = pe.matmul(y_ps[e % 2][:, t, :], hs[e % 2][:, t * P:(t + 1) * P], w2[:, e, :])
                    ins.then_inc(y_done, 1)

                hidden(0)
                pe.wait_ge(g_ready, c + 1)
                pe.sem_inc(k.pe_passed, 1)
                pe.transpose(g_ps[:], g[:].rearrange("p t e -> p (t e)"), k.ident[:]).then_inc(g_turned, 1)
                hidden(1)
                pe.wait_ge(gT_ready, c + 1)
                pe.wait_ge(acc_ready, c)
                pe.sem_inc(k.pe_passed, 1)
                pe.matmul(b_ps[:].rearrange("p t d -> p (t d)"), gT[:], b2[:].rearrange("g t d -> g (t d)"))\
                  .then_inc(b_done, 1)
                output(0)
                for e in range(2, E):
                    hidden(e)
                    output(e - 1)
                output(E - 1)

        @block.scalar
        def _(act):
            act.sem_inc(gelu_done, 2)
            with act.Fori(0, n) as c:
                for e in range(E):
                    act.wait_ge(h_done, c * E + e + 1)
                    act.wait_ge(y_done, c * E + e + 1)
                    act.activation(hs[e % 2][:], h_ps[e % 2][:], ACT.Gelu).then_inc(gelu_done, 1)
                    if e == 0:
                        act.wait_ge(g_turned, c + 1)
                        act.wait_ge(b_done, c)
                        act.activation(gT[:], g_ps[:], ACT.Copy).then_inc(gT_ready, 1)

        @block.vector
        def _(dve):
            dve.sem_inc(weighted, 2)
            with dve.Fori(0, n) as c:
                dve.wait_ge(g_turned, c)
                dve.wait_ge(weighted, c * E + 2)
                dve.tensor_copy(g[:], gates[:, bass.ts(c, 4), :]).then_inc(g_ready, 1)
                dve.wait_ge(added, c * E + 2)
                dve.wait_ge(b_done, c + 1)
                dve.tensor_tensor(acc[:], b_ps[:], h[:, bass.ts(c, 4), :], ALU.add).then_inc(acc_ready, 1)
                for e in range(E):
                    dve.wait_ge(y_done, c * E + e + 3)
                    dve.wait_ge(added, c * E + e + 1)
                    dve.tensor_tensor(tmp[e % 2][:], y_ps[e % 2][:], bc(g[:, :, e], D), ALU.mult)\
                       .then_inc(weighted, 1)

        @block.gpsimd
        def _(pool):
            pool.sem_inc(added, 2)
            with pool.Fori(0, n) as c:
                pool.wait_ge(acc_ready, c + 1)
                for e in range(E):
                    pool.wait_ge(weighted, c * E + e + 3)
                    pool.wait_ge(added, c * E + e + 2)
                    out = acc[:] if e < E - 1 else h[:, bass.ts(c, 4), :]
                    pool.tensor_tensor(out, acc[:], tmp[e % 2][:], ALU.add).then_inc(added, 1)


def image_attention(nc, mem, k, xT, yT, stats):
    xs = [mem.sb(f"ia_x{b}", [D + 1, 4, 2, WIN]) for b in range(2)]
    qk = [mem.sb(f"ia_qk{b}", [P, 2, 4, WIN]) for b in range(2)]
    v = [mem.sb(f"ia_v{b}", [WIN, 8, D]) for b in range(2)]
    sc = [mem.sb(f"ia_scores{b}", [P, 4, WIN]) for b in range(2)]
    ex = [mem.sb(f"ia_exp{b}", [P, 4, WIN]) for b in range(2)]
    pr = [mem.sb(f"ia_probs{b}", [P, 4, WIN]) for b in range(2)]
    prT = [mem.sb(f"ia_probsT{b}", [WIN, 4, P]) for b in range(2)]
    oT = [mem.sb(f"ia_oT{b}", [D + 1, 512]) for b in range(2)]
    mx, sm, rs = ([mem.sb(f"ia_{x}{b}", [P, 4]) for b in range(2)] for x in ("max", "sum", "rsum"))
    qk_ps = [mem.ps(f"ia_qk_ps{b}", [P, 512]) for b in range(2)]
    v_ps = [mem.ps(f"ia_v_ps{b}", [D, 512]) for b in range(2)]
    s_ps = [mem.ps(f"ia_s_ps{b}", [P, 4, WIN]) for b in range(2)]
    t_ps = [mem.ps(f"ia_t_ps{b}", [WIN, 4, P]) for b in range(2)]
    names = ("x_ready", "qk_done", "v_done", "qk_ready", "v_ready", "scores_done", "max_done", "shifted", "exp_done",
             "sum_done", "rsum_done", "probs_done", "turned", "probsT_ready", "o_done", "oT_ready", "y_done",
             "y_saved", "counted", "ones")
    (x_ready, qk_done, v_done, qk_ready, v_ready, scores_done, max_done, shifted, exp_done, sum_done, rsum_done,
     probs_done, turned, probsT_ready, o_done, oT_ready, y_done, y_saved, counted, ones) = (
         mem.sem("ia_" + x) for x in names)
    n = 8

    def pipeline(eng, front, back):
        front(0, 0, True)
        front(1, 1, True)
        back(0, 0, True)
        front(2, 0, False)
        back(1, 1, True)
        front(3, 1, False)
        with eng.Fori(1, n // 2 - 1) as i:
            for b in range(2):
                back(2 * i + b, b, False)
                front(2 * i + b + 2, b, False)
        back(n - 2, 0, False)
        back(n - 1, 1, False)

    with nc.Block() as block:
        @block.gpsimd
        def _(pool):
            def take(c, b, first):
                if not first:
                    pool.wait_ge(v_done, c - 1)
                pool.tensor_copy(xs[b][:].rearrange("d a r s -> d (a r s)"), xT[:, bass.ts(c, 512)])\
                    .then_inc(x_ready, 1)

            def normal(c, b, first):
                pool.wait_ge(rsum_done, c + 1)
                if not first:
                    pool.wait_ge(turned, c - 1)
                pool.tensor_tensor(pr[b][:], ex[b][:], bc(rs[b][:], WIN), ALU.mult).then_inc(probs_done, 1)
            pipeline(pool, take, normal)

        @block.tensor
        def _(pe):
            pe.wait_ge(ones, 2)

            def front(c, b, first):
                pe.wait_ge(x_ready, c + 1)
                if not first:
                    pe.wait_ge(oT_ready, c - 1)
                    pe.wait_ge(counted, c - 1)
                pe.sem_inc(k.pe_passed, 1)
                for j in range(2):
                    for r in range(2):
                        out = qk_ps[b][r * D:(r + 1) * D, j * 256:(j + 1) * 256]
                        ins = pe.matmul(out.rearrange("d (a s) -> d a s", a=4), k.wl1[:, j, :], xs[b][:, :, r, :])
                ins.then_inc(qk_done, 1)
                for w in range(8):
                    ins = pe.matmul(v_ps[b][:, w * D:(w + 1) * D], xs[b][:, w // 2, w % 2, :], k.wl1[:, 2, :])
                ins.then_inc(v_done, 1)
                pe.wait_ge(qk_ready, c + 1)
                if not first:
                    pe.wait_ge(shifted, c - 1)
                pe.sem_inc(k.pe_passed, 1)
                for p in range(4):
                    for r in range(2):
                        half = slice(r * D, (r + 1) * D)
                        ins = pe.matmul(s_ps[b][half, p, :], qk[b][half, 0, p, :], qk[b][half, 1, p, :])
                ins.then_inc(scores_done, 1)

            def back(c, b, first):
                pe.wait_ge(probs_done, c + 1)
                if not first:
                    pe.wait_ge(probsT_ready, c - 1)
                pe.sem_inc(k.pe_passed, 1)
                for p in range(4):
                    ins = pe.transpose(t_ps[b][:, p, :], pr[b][:, p, :], k.ident[:])
                ins.then_inc(turned, 1)
                pe.wait_ge(probsT_ready, c + 1)
                pe.wait_ge(v_ready, c + 1)
                pe.sem_inc(k.pe_passed, 1)
                for w in range(8):
                    ins = pe.matmul(qk_ps[b][0:D, w * WIN:(w + 1) * WIN], v[b][:, w, :],
                                    prT[b][:, w // 2, w % 2 * WIN:(w % 2 + 1) * WIN])
                ins.then_inc(o_done, 1)
                pe.wait_ge(oT_ready, c + 1)
                pe.sem_inc(k.pe_passed, 1)
                pe.matmul(v_ps[b][:], k.wl1[:, 3, :], oT[b][:]).then_inc(y_done, 1)
            pipeline(pe, front, back)

        @block.scalar
        def _(act):
            def front(c, b, first):
                act.wait_ge(qk_done, c + 1)
                if not first:
                    act.wait_ge(scores_done, c - 1)
                act.activation(qk[b][:].rearrange("d j a s -> d (j a s)"), qk_ps[b][:], ACT.Copy)\
                   .then_inc(qk_ready, 1)
                act.wait_ge(v_done, c + 1)
                if not first:
                    act.wait_ge(o_done, c - 1)
                act.activation(v[b][:].rearrange("s w d -> s (w d)"), v_ps[b][:], ACT.Copy).then_inc(v_ready, 1)

            def back(c, b, first):
                act.wait_ge(shifted, c + 1)
                if not first:
                    act.wait_ge(probs_done, c - 1)
                act.activation(ex[b][:], sc[b][:], ACT.Exp, scale=1.0 / D).then_inc(exp_done, 1)
                act.wait_ge(turned, c + 1)
                if not first:
                    act.wait_ge(o_done, c - 1)
                act.activation(prT[b][:], t_ps[b][:], ACT.Copy).then_inc(probsT_ready, 1)
                act.wait_ge(o_done, c + 1)
                if not first:
                    act.wait_ge(y_done, c - 1)
                act.activation(oT[b][0:D, :], qk_ps[b][0:D, :], ACT.Copy).then_inc(oT_ready, 1)
            pipeline(act, front, back)

        @block.vector
        def _(dve):
            for b in range(2):
                dve.memset(oT[b][D:D + 1, :], 1.0).then_inc(ones, 1)

            def front(c, b, first):
                dve.wait_ge(scores_done, c + 1)
                dve.tensor_reduce(mx[b][:], s_ps[b][:], AX.X, ALU.max).then_inc(max_done, 1)
                dve.wait_ge(max_done, c + 1)
                if not first:
                    dve.wait_ge(exp_done, c - 1)
                dve.tensor_tensor(sc[b][:], s_ps[b][:], bc(mx[b][:], WIN), ALU.subtract).then_inc(shifted, 1)

            def back(c, b, first):
                dve.wait_ge(exp_done, c + 1)
                dve.tensor_reduce(sm[b][:], ex[b][:], AX.X, ALU.add).then_inc(sum_done, 1)
                dve.wait_ge(sum_done, c + 1)
                if not first:
                    dve.wait_ge(probs_done, c - 1)
                dve.reciprocal(rs[b][:], sm[b][:]).then_inc(rsum_done, 1)
                dve.wait_ge(y_done, c + 1)
                dve.tensor_copy(yT[:, bass.ts(c, 512)], v_ps[b][:]).then_inc(y_saved, 1)
                dve.bn_stats(stats[:, bass.ts(c, 6)], v_ps[b][:]).then_inc(counted, 1)
            pipeline(dve, front, back)


def batch_norm_add(nc, mem, k, xT, yT, stats, h):
    mv = mem.sb("bn_mv", [D, 4])
    z = [mem.sb(f"bn_z{b}", [D, 512]) for b in range(2)]
    r = [mem.sb(f"bn_r{b}", [D, 512]) for b in range(2)]
    s = [mem.sb(f"bn_s{b}", [D, 512]) for b in range(2)]
    t_ps = [mem.ps(f"bn_ps{b}", [P, 4, D]) for b in range(2)]
    step, var_ready, std_ready, scaled, relued, summed, turned, added = (
        mem.sem("bn_" + x) for x in ("step", "var_ready", "std_ready", "scaled", "relued", "summed", "turned", "added"))
    n = 8
    with nc.Block() as block:
        @block.vector
        def _(dve):
            dve.bn_aggr(mv[:, 0:2], stats[:]).then_inc(var_ready, 1)
            dve.wait_ge(std_ready, 1)
            dve.reciprocal(mv[:, 3:4], mv[:, 2:3]).then_inc(step, 1)
            dve.wait_ge(step, 1)
            dve.tensor_tensor(mv[:, 3:4], mv[:, 3:4], k.bn[:, 0:1], ALU.mult).then_inc(step, 1)
            dve.wait_ge(step, 2)

            def scale(c, b, first):
                if not first:
                    dve.wait_ge(relued, c - 1)
                dve.tensor_scalar(z[b][:], yT[:, bass.ts(c, 512)], mv[:, 0:1], mv[:, 3:4], ALU.subtract,
                                  ALU.mult).then_inc(scaled, 1)

            def total(c, b, first):
                dve.wait_ge(relued, c + 1)
                if not first:
                    dve.wait_ge(turned, c - 1)
                dve.tensor_tensor(s[b][:], r[b][:], xT[0:D, bass.ts(c, 512)], ALU.add).then_inc(summed, 1)

            def add(c, b):
                dve.wait_ge(turned, c + 1)
                dve.tensor_tensor(h[:, bass.ts(c, 4), :], h[:, bass.ts(c, 4), :], t_ps[b][:], ALU.add)\
                   .then_inc(added, 1)

            scale(0, 0, True)
            scale(1, 1, True)
            total(0, 0, True)
            scale(2, 0, False)
            total(1, 1, True)
            scale(3, 1, False)
            with dve.Fori(1, n // 2 - 1) as i:
                for b in range(2):
                    add(2 * i + b - 2, b)
                    total(2 * i + b, b, False)
                    scale(2 * i + b + 2, b, False)
            for c in (n - 2, n - 1):
                add(c - 2, c % 2)
                total(c, c % 2, False)
            for c in (n - 2, n - 1):
                add(c, c % 2)

        @block.scalar
        def _(act):
            act.wait_ge(var_ready, 1)
            act.activation(mv[:, 2:3], mv[:, 1:2], ACT.Sqrt, bias=k.eps[0:D, 0:1]).then_inc(std_ready, 1)

            def relu(c, b, first):
                act.wait_ge(scaled, c + 1)
                if not first:
                    act.wait_ge(summed, c - 1)
                act.activation(r[b][:], z[b][:], ACT.Relu, bias=k.bn[:, 1:2]).then_inc(relued, 1)
            twice(act, n, relu)

        @block.tensor
        def _(pe):
            def turn(c, b, first):
                pe.wait_ge(summed, c + 1)
                if not first:
                    pe.wait_ge(added, c - 1)
                pe.sem_inc(k.pe_passed, 1)
                for t in range(4):
                    ins = pe.transpose(t_ps[b][:, t, :], s[b][:, t * P:(t + 1) * P], k.ident[0:D, 0:D])
                ins.then_inc(turned, 1)
            twice(pe, n, turn)




class Names:
    pass


def program(nc, a, out):
    with ExitStack() as ctx:
        mem = Memory(nc, ctx)
        k = Names()
        h = mem.sb("h", [P, TILES, D])
        xn = mem.sb("xn", [P, TILES, D])
        xT = mem.sb("xT", [D + 1, M])
        k.big = mem.sb("squares", [P, TILES, D])
        k.ln_s = mem.sb("ln_stats", [P, 5, TILES])
        k.ln_xs = [mem.sb(f"ln_xs{b}", [P, 4, D]) for b in range(2)]
        k.ln_xts = [mem.sb(f"ln_xts{b}", [D + 1, 512]) for b in range(2)]
        hg = mem.sb("router_h", [P, TILES, GH * GE])
        gates = [mem.sb("gates0", [P, TILES, E0]), mem.sb("gates1", [P, TILES, E1])]
        logits = mem.sb("logits1", [P, TILES, E1])
        k.settled = mem.sem("constants_settled")
        k.pe_passed, k.pool_passed = mem.sem("tensor_waits_passed"), mem.sem("gpsimd_waits_passed")

        def stage():
            return Stage(mem)

        k.ln_sems = [mem.sem(f"ln_{x}") for x in (
            "step", "centered", "squared", "summed", "rooted", "scaled", "turned", "evacuated", "kept", "mapped",
            "saved")]
        calls = [0, 0]

        def norm(name, **kw):
            with stage() as m:
                k.ln_pT = [m.ps(f"{name}_pT{b}", [D, 512]) for b in range(2)]
                k.ln_pj = [m.ps(f"{name}_pj{b}", [P, 4, GH * GE]) for b in range(2)]
                normalize(nc, m, k, h, xn, xT, *calls, **kw)
            calls[0] += 1
            calls[1] += "weight" in kw

        sort = EdgeSort(mem)
        ys = [xn[:], k.big[:], *(t[:].rearrange("p (t d) -> p t d", d=D) for t in (sort.keys, sort.other))]
        with stage() as m:
            m.sb = mem.sb
            load_constants(nc, m, a, k, sort)
        with nc.Block() as block:
            @block.vector
            def _(dve):
                for b in range(2):
                    ins = dve.memset(k.ln_xts[b][D:D + 1, :], 1.0)
                ins.then_inc(k.settled, 1)
        with stage() as m:
            tokenize(nc, m, a, k, h, sort)
        norm("ln0")
        with stage() as m:
            window_attention(nc, m, k, xT, h, sort)
        sort.find_limits(nc)
        norm("ln1", weight=k.wgat[:], out=hg)
        with stage() as m:
            graph_router(nc, m, a, k, hg, sort, xT, ys, gates[0])
        with stage() as m:
            combine(nc, m, ys, gates[0], h)
        norm("ln2")
        with stage() as m:
            yT = m.sb("yT", [D, M])
            stats = m.sb("bn_stats", [D, 8 * 6])
            with stage() as m2:
                image_attention(nc, m2, k, xT, yT, stats)
            with stage() as m2:
                batch_norm_add(nc, m2, k, xT, yT, stats, h)
        norm("ln3", weight=k.wr[:], out=logits, affine=k.affine)
        with stage() as m:
            choose(nc, m, k.lower, E1, logits, gates[1], "moe1")
        with stage() as m:
            experts(nc, m, k, 1, E1, xT, gates[1], h)
        stored = mem.sem("output_stored")
        with nc.Block() as block:
            @block.sync
            def _(sp):
                sp.dma_start(out.rearrange("(t r) s d -> (r s) t d", r=2), h[:]).then_inc(stored, 16)
                sp.wait_ge(stored, 16)


_INS = ['x', 'L0_tok_W', 'L0_tok_b', 'L0_attn_w_qkv', 'L0_attn_b_qkv', 'L0_attn_w_proj', 'L0_attn_b_proj',
        'L0_attn_rel_pos_bias', 'L0_ffn_W_gat', 'L0_ffn_att_src', 'L0_ffn_att_dst', 'L0_ffn_b_gat',
        'L0_ffn_ln_gamma', 'L0_ffn_ln_beta', 'L0_ffn_W1', 'L0_ffn_b1', 'L0_ffn_W2', 'L0_ffn_b2',
        'L0_ffn_edge_index', 'L1_attn_Wq', 'L1_attn_bq', 'L1_attn_Wk', 'L1_attn_bk', 'L1_attn_Wv',
        'L1_attn_bv', 'L1_attn_Wl', 'L1_attn_bl', 'L1_attn_gamma', 'L1_attn_beta', 'L1_ffn_gamma',
        'L1_ffn_beta', 'L1_ffn_Wr', 'L1_ffn_br', 'L1_ffn_W1', 'L1_ffn_b1', 'L1_ffn_W2', 'L1_ffn_b2']


def kernel(**inputs):
    import numpy as np
    import concourse.bacc as bacc
    from concourse.bass_utils import run_bass_kernel_spmd

    nc = bacc.Bacc("TRN2", target_bir_lowering=False, num_devices=1)
    arrays, args = {}, {}
    for name in _INS:
        v = np.ascontiguousarray(inputs[name])
        arrays["in_" + name] = v
        args[name] = nc.dram_tensor("in_" + name, v.shape, mybir.dt.from_np(v.dtype), kind="ExternalInput").ap()
    out = nc.dram_tensor("out_h", (IMG, WIN, D), F32, kind="ExternalOutput").ap()
    program(nc, args, out)
    return run_bass_kernel_spmd(nc, [arrays], core_ids=[0]).results[0]["out_h"]
```

```python
from contextlib import ExitStack

import concourse.bass as bass
from concourse import mybir

F32 = mybir.dt.float32
BF16 = mybir.dt.bfloat16
I32 = mybir.dt.int32
ALU = mybir.AluOpType
ACT = mybir.ActivationFunctionType
AX = mybir.AxisListType

P = 128
D = 64
IMG = 64
WIN = 64
M = IMG * WIN
TILES = M // P
HD = 8
NH = D // HD
GH, GE = 4, 4
E0, E1 = 4, 8
HID = 128
EDGES = 262144
EC = EDGES // P
EPS = 1e-5
CLASS_LAST = float(1 << 24)
CLASS_NONE = float(1 << 25)
GCH = 8
CCH = 16
NSRC = GH * GE + GH
NDST = 2 * GH
EXPERT_PAIRS = TILES // 4
COUNT_PAIRS = 2 * (EXPERT_PAIRS - 1)
MERGES_TOKENS = 6
NV = GH * (GE + 1)


def twice(eng, n, body):
    body(0, 0, True)
    body(1, 1, True)
    with eng.Fori(1, n // 2) as i:
        for b in range(2):
            body(2 * i + b, b, False)


def bc(ap, n):
    return ap.unsqueeze(len(ap.shape)).broadcast_to([*ap.shape, n])


def bc_at(ap, axis, n):
    a = ap.unsqueeze(axis)
    return a.broadcast_to([*a.shape[:axis], n, *a.shape[axis + 1:]])


class Memory:

    def __init__(self, nc, ctx):
        self.nc, self.ctx = nc, ctx

    def sb(self, name, shape, dt=F32):
        return self.ctx.enter_context(self.nc.sbuf_tensor(name, shape, dt))

    def ps(self, name, shape, dt=F32):
        return self.ctx.enter_context(self.nc.psum_tensor(name, shape, dt))

    def sem(self, name):
        return self.ctx.enter_context(self.nc.semaphore(name))


class Stage:

    def __init__(self, mem):
        self.nc, self.sem, self.ctx = mem.nc, mem.sem, ExitStack()
        m = Memory(mem.nc, self.ctx)
        self.sb, self.ps = m.sb, m.ps

    def __enter__(self):
        return self

    def __exit__(self, *exc):
        self.ctx.close()


def allocate_constants(mem, a, k):
    k.ident = mem.sb("ident", [P, P])
    k.wqkv = mem.sb("wqkv", [D + 1, 3 * D])
    k.wproj = mem.sb("wproj", [D + 1, D])
    k.wtok = mem.sb("wtok", [D + 1, D])
    k.relbias = mem.sb("relbias", [P, NH, WIN])
    k.wgat = mem.sb("wgat", [D + 1, GH * GE])
    k.att_src = mem.sb("att_src", [P, GH * GE])
    k.att_dst = mem.sb("att_dst", [P, GH * GE])
    k.b_gat = mem.sb("b_gat", [P, GH * GE])
    k.ln_gamma = mem.sb("ln_gamma", [P, GH * GE])
    k.ln_beta = mem.sb("ln_beta", [P, GH * GE])
    k.w1 = [mem.sb("moe0_w1", [D + 1, E0, HID]), mem.sb("moe1_w1", [P, E1, HID])]
    k.w2 = [mem.sb("moe0_w2", [HID, E0, D]), mem.sb("moe1_w2", [HID, E1, D])]
    k.b2_cols = mem.sb("moe1_b2_cols", [P, E1 // 2])
    k.pick = mem.sb("pick", [12 * E1, E1 // 2, 4, P], BF16)
    k.pick_small = mem.sb("pick_small", [12 * E1, E1 // 2, 4, 2])
    k.fold = mem.sb("fold", [P, D])
    k.b2_rows = mem.sb("moe0_b2_rows", [P, E0, D])
    k.wl1 = mem.sb("attn1_w", [P, 4, D])
    k.bn = mem.sb("attn1_bn", [D, 2])
    k.affine = mem.sb("moe1_affine", [D, 2])
    k.wr = mem.sb("moe1_wr", [D + 1, E1])
    k.eps = mem.sb("eps", [P, 1])
    k.headmask = mem.sb("headmask", [P, 2, NH])
    k.iota_lo = mem.sb("iota_lo", [P, P])
    k.lower = mem.sb("lower", [P, E1, E1])
    k.lower0 = mem.sb("lower0", [P, E0, E0])
    k.zero_mm = mem.sb("zero_mm", [P, 512])

    def row(v):
        return v.rearrange("(a n) -> a n", a=1)

    def everywhere(v, n):
        return bass.AP(v.tensor, 0, [[0, P], [1, n]])

    loads = [
        (k.wqkv[0:D, :], a["L0_attn_w_qkv"]), (k.wqkv[D:D + 1, :], row(a["L0_attn_b_qkv"])),
        (k.wproj[0:D, :], a["L0_attn_w_proj"]), (k.wproj[D:D + 1, :], row(a["L0_attn_b_proj"])),
        (k.wgat[0:D, :], a["L0_ffn_W_gat"]),
        (k.bn[:, 0:1], a["L1_attn_gamma"].rearrange("(p a) -> p a", a=1)),
        (k.bn[:, 1:2], a["L1_attn_beta"].rearrange("(p a) -> p a", a=1)),
        (k.affine[:, 0:1], a["L1_ffn_gamma"].rearrange("(p a) -> p a", a=1)),
        (k.affine[:, 1:2], a["L1_ffn_beta"].rearrange("(p a) -> p a", a=1)),
        (k.wr[0:D, :], a["L1_ffn_Wr"]), (k.wr[D:D + 1, :], row(a["L1_ffn_br"])),
    ]
    for dst, name in ((k.att_src, "L0_ffn_att_src"), (k.att_dst, "L0_ffn_att_dst")):
        loads.append((dst[:], everywhere(a[name], GH * GE)))
    for p in range(E1 // 2):
        loads.append((k.b2_cols[:, p:p + 1], a["L1_ffn_b2"][2 * p:2 * p + 2, :].rearrange("r (d a) -> (r d) a", a=1)))
    loads.append((k.b2_rows[:].rearrange("p e d -> p (e d)"), everywhere(a["L0_ffn_b2"], E0 * D)))
    for dst, name in ((k.b_gat, "L0_ffn_b_gat"), (k.ln_gamma, "L0_ffn_ln_gamma"), (k.ln_beta, "L0_ffn_ln_beta")):
        loads.append((dst[:], everywhere(a[name], GH * GE)))
    for n, e in ((0, E0), (1, E1)):
        loads += [
            (k.w1[n][0:D], a[f"L{n}_ffn_W1"].rearrange("e d h -> d e h")),
            (k.w1[n][D:D + 1], a[f"L{n}_ffn_b1"].rearrange("(a e) h -> a e h", a=1)),
            (k.w2[n][:], a[f"L{n}_ffn_W2"].rearrange("e h d -> h e d")),
        ]
    for n, (w, b) in enumerate((("Wq", "bq"), ("Wk", "bk"), ("Wv", "bv"), ("Wl", "bl"))):
        loads += [(k.wl1[0:D, n, :], a[f"L1_attn_{w}"]), (k.wl1[D:D + 1, n, :], row(a[f"L1_attn_{b}"]))]
    return loads


def tokenize(nc, mem, a, k, h, xT_all, sort, loads):
    rows = a["x"].rearrange("b c (i p) w -> (b c i) (p w)", p=8)
    n = 4
    xrow = [mem.sb(f"xrow{c}", [P, 512]) for c in range(n)]
    patch = [mem.sb(f"patch{b}", [P, 8, D]) for b in range(2)]
    xT = [mem.sb(f"patchT{b}", [D + 1, 1024]) for b in range(2)]
    pT = [mem.ps(f"patchT_ps{b}", [D, 8, P]) for b in range(2)]
    ph = [mem.ps(f"token_ps{b}", [P, 8, D]) for b in range(2)]
    weight_rows, weight_ps = mem.sb("wtok_rows", [D, D]), mem.ps("wtok_ps", [D, D])
    bias_rows, bias_ps = mem.sb("bias_rows", [WIN, NH, WIN]), mem.ps("bias_ps", [P, NH, WIN])
    reverse = mem.sb("reverse", [WIN, 2, WIN])
    loaded = [mem.sem(f"images_loaded{c}") for c in range(n)]
    weight_loaded, bias_loaded, constants_loaded = (
        mem.sem(f"{x}_loaded") for x in ("wtok", "window_bias", "constants"))
    filled, padded, xT_padded, selected, masked, picked, ones = (
        mem.sem(x) for x in ("constants_filled", "weights_padded", "xT_padded", "constants_selected",
                             "headmask_made", "pick_made", "patch_ones"))
    weight_turned, weight_ready, bias_turned = (
        mem.sem(x) for x in ("wtok_turned", "wtok_ready", "window_bias_turned"))
    cut, turned, copied, mapped, saved = (
        mem.sem(f"patch_{x}") for x in ("cut", "turned", "copied", "mapped", "saved"))
    with nc.Block() as block:
        @block.sync
        def _(sp):
            sp.dma_start(xrow[0][:], rows[0:P, :]).then_inc(loaded[0], 16)
            sp.dma_start(weight_rows[:], a["L0_tok_W"]).then_inc(weight_loaded, 16)
            sp.dma_start(k.wtok[D:D + 1, :], a["L0_tok_b"].rearrange("(a n) -> a n", a=1)).then_inc(weight_loaded, 16)
            sort.load(sp, a["L0_ffn_edge_index"])
            for c in range(1, n):
                sp.dma_start(xrow[c][:], rows[c * P:(c + 1) * P, :]).then_inc(loaded[c], 16)
            sp.dma_start(bias_rows[:], bass.AP(a["L0_attn_rel_pos_bias"].tensor, 0,
                                               [[1, WIN], [2 * WIN - 1, NH], [1, WIN]])).then_inc(bias_loaded, 16)
            sp.wait_ge(padded, 2)
            for dst, src in loads:
                sp.dma_start(dst, src).then_inc(constants_loaded, 16)
            sp.wait_ge(constants_loaded, 16 * len(loads))

        @block.gpsimd
        def _(pool):
            fills = ((k.ident, 0.0), (reverse, 0.0), (k.eps, EPS), (k.headmask, 1.0), (k.lower, 1.0),
                     (k.lower0, 1.0), (k.zero_mm, 0.0), (k.pick_small, 0.0))
            for t, v in fills:
                pool.memset(t[:], v).then_inc(filled, 1)
            for t in (k.wl1, k.w1[1]):
                pool.memset(t[:], 0.0).then_inc(padded, 1)
            pool.wait_ge(filled, len(fills))
            pool.wait_ge(padded, 2)
            pool.affine_select(k.ident[:], k.ident[:], [[-1, P]], ALU.not_equal, 1.0, base=0,
                               channel_multiplier=1).then_inc(selected, 1)
            pool.affine_select(reverse[:], reverse[:], [[0, 2], [1, WIN]], ALU.not_equal, 1.0,
                               base=1 - WIN, channel_multiplier=1).then_inc(selected, 1)
            pool.affine_select(k.headmask[:], k.headmask[:], [[-D, 2], [-HD, NH]], ALU.is_ge, 0.0,
                               base=0, channel_multiplier=1).then_inc(selected, 1)
            for t, e in ((k.lower, E1), (k.lower0, E0)):
                pool.affine_select(t[:], t[:], [[1, e], [-1, e]], ALU.is_gt, 0.0, base=0,
                                   channel_multiplier=0).then_inc(selected, 1)
            pool.iota(k.iota_lo[:], [[1, P]], base=0, channel_multiplier=0,
                      allow_small_or_imprecise_dtypes=True).then_inc(selected, 1)
            pool.wait_ge(selected, 3)
            pool.affine_select(k.headmask[:], k.headmask[:], [[D, 2], [HD, NH]], ALU.is_ge, 0.0,
                               base=HD - 1, channel_multiplier=-1).then_inc(masked, 1)
            pool.memset(xT_all[:], 0.0).then_inc(xT_padded, 1)
            pool.wait_ge(xT_padded, 1)
            pool.wait_ge(masked, 1)
            pool.wait_ge(selected, 6)
            pool.memset(xT_all[D:D + 1, :], 1.0).then_inc(xT_padded, 1)
            pool.wait_ge(xT_padded, 2)
            for j in range(3):
                pool.affine_select(k.pick_small[:], k.pick_small[:], [[-2, E1 // 2], [-3 * E1, 4], [-1, 2]],
                                   ALU.not_equal, 1.0, base=-j * E1, channel_multiplier=1).then_inc(picked, 1)
                pool.wait_ge(picked, j + 1)

        @block.tensor
        def _(pe):
            pe.wait_ge(selected, 1)
            pe.wait_ge(weight_loaded, 32)
            pe.transpose(weight_ps[:], weight_rows[:], k.ident[0:D, 0:D]).then_inc(weight_turned, 1)
            for c in range(n):
                b = c % 2
                pe.wait_ge(cut, c + 1)
                if c > 1:
                    pe.wait_ge(copied, c - 1)
                for j in range(8):
                    ins = pe.transpose(pT[b][:, j, :], patch[b][:, j, :], k.ident[:])
                ins.then_inc(turned, 1)
                pe.wait_ge(copied, c + 1)
                if c > 1:
                    pe.wait_ge(saved, c - 1)
                elif c == 0:
                    pe.wait_ge(ones, 2)
                    pe.wait_ge(weight_ready, 1)
                for t in range(8):
                    ins = pe.matmul(ph[b][:, t, :], xT[b][:, t * P:(t + 1) * P], k.wtok[:])
                ins.then_inc(mapped, 1)
            pe.wait_ge(bias_loaded, 16)
            pe.wait_ge(selected, 2)
            pe.matmul(bias_ps[:].rearrange("q h j -> q (h j)"), reverse[:].rearrange("r t q -> r (t q)"),
                      bias_rows[:].rearrange("r h j -> r (h j)")).then_inc(bias_turned, 1)

        @block.scalar
        def _(act):
            for c in range(n):
                act.wait_ge(turned, c + 1)
                if c > 1:
                    act.wait_ge(mapped, c - 1)
                act.activation(xT[c % 2][0:D, :].rearrange("k (s j) -> k s j", j=8),
                               pT[c % 2][:].rearrange("k j s -> k s j"), ACT.Copy).then_inc(copied, 1)
            act.wait_ge(bias_turned, 1)
            act.activation(k.relbias[:], bias_ps[:], ACT.Copy)

        @block.vector
        def _(dve):
            def take(c):
                dve.wait_ge(loaded[c], 16)
                if c > 1:
                    dve.wait_ge(turned, c - 1)
                dve.tensor_copy(patch[c % 2][:].rearrange("s j (p q) -> s j p q", p=8),
                                xrow[c][:].rearrange("s (p j q) -> s j p q", p=8, j=8)).then_inc(cut, 1)

            def save(c):
                dve.wait_ge(mapped, c + 1)
                dve.tensor_copy(h[:, 8 * c:8 * c + 8, :], ph[c % 2][:]).then_inc(saved, 1)

            for b in range(2):
                dve.memset(xT[b][D:D + 1, :], 1.0).then_inc(ones, 1)
            take(0)
            dve.wait_ge(weight_turned, 1)
            dve.tensor_copy(k.wtok[0:D, :], weight_ps[:]).then_inc(weight_ready, 1)
            take(1)
            sort.form_keys(dve, 0)
            for c in range(n):
                if c + 2 < n:
                    take(c + 2)
                save(c)
                if c == 0:
                    sort.form_keys(dve, 1)
                sort.merge(dve, MERGES_TOKENS * (c + 1) // n)
            for rows in (sort.src_rows, sort.dst_rows):
                dve.memset(rows[:, EC:EC + 2 * GCH], 0)
            dve.memset(k.wgat[D:D + 1, :], 0.0)
            dve.tensor_tensor(k.fold[:], k.ident[:, 0:D], k.ident[:, D:P], ALU.add)
            dve.wait_ge(picked, 3)
            dve.tensor_copy(k.pick[:].rearrange("r p t (x m) -> r (p t x) m", x=2),
                            bc(k.pick_small[:].rearrange("r p t x -> r (p t x)"), D))
            dve.wait_ge(masked, 1)
            dve.tensor_tensor(k.headmask[:, 0, :], k.headmask[:, 0, :], k.headmask[:, 1, :], ALU.add)


def normalize(nc, mem, k, h, xn, xT, call, projections, weight=None, out=None, affine=None,
              beside=None):
    s, xc, sq, xs, pT, pj = k.ln_s, xn, k.big, k.ln_xs, k.ln_pT, k.ln_pj
    step, centered, squared, summed, rooted, inverted, scaled, turned, evacuated, mapped, saved = k.ln_sems
    N = weight.shape[-1] if weight is not None else 0
    G, n = TILES // 8, TILES // 4
    steps, groups, chunks, projected = call * 2 * G, call * G, call * n, projections * n
    with nc.Block() as block:
        @block.vector
        def _(dve):
            def center(g):
                part = slice(8 * g, 8 * g + 8)
                dve.tensor_reduce(s[:, 0, part], h[:, part, :], AX.X, ALU.add).then_inc(step, 1)
                dve.wait_ge(step, steps + 2 * g + 1)
                dve.tensor_scalar(s[:, 1, part], s[:, 0, part], 1.0 / D, None, ALU.mult).then_inc(step, 1)
                dve.wait_ge(step, steps + 2 * g + 2)
                dve.tensor_tensor(xc[:, part, :], h[:, part, :], bc(s[:, 1, part], D), ALU.subtract)\
                    .then_inc(centered, 1)

            def square_sum(g):
                part = slice(8 * g, 8 * g + 8)
                dve.wait_ge(squared, groups + g + 1)
                dve.tensor_reduce(s[:, 2, part], sq[:, part, :], AX.X, ALU.add).then_inc(summed, 1)

            def invert(g):
                part = slice(8 * g, 8 * g + 8)
                dve.wait_ge(rooted, groups + g + 1)
                dve.reciprocal(s[:, 4, part], s[:, 3, part]).then_inc(inverted, 1)

            def save(c):
                dve.wait_ge(mapped, projected + c + 1)
                dve.tensor_copy(out[:, 4 * c:4 * c + 4, :], pj[c % 2][:, :, 0:N]).then_inc(saved, 1)

            for g in range(G + 2):
                if g < G:
                    center(g)
                if 0 < g <= G:
                    square_sum(g - 1)
                if g > 1:
                    invert(g - 2)
            if N:
                for c in range(n):
                    save(c)
                    if beside:
                        beside(dve, c)

        @block.gpsimd
        def _(pool):
            for c in range(n):
                pool.wait_ge(inverted, groups + c // 2 + 1)
                if c > 1:
                    pool.wait_ge(turned, chunks + c - 1)
                part = slice(4 * c, 4 * c + 4)
                pool.tensor_tensor(xs[c % 2][:], xc[:, part, :], bc(s[:, 4, part], D), ALU.mult)\
                    .then_inc(scaled, 1)

        @block.scalar
        def _(act):
            def evacuate(c):
                act.wait_ge(turned, chunks + c + 1)
                x = xT[0:D, c * 512:(c + 1) * 512]
                if affine is None:
                    ins = act.activation(x, pT[c % 2][:], ACT.Copy)
                else:
                    ins = act.activation(x, pT[c % 2][:], ACT.Identity, bias=affine[:, 1:2], scale=affine[:, 0:1])
                ins.then_inc(evacuated, 1)

            for g in range(G + 3):
                if g < G:
                    part = slice(8 * g, 8 * g + 8)
                    act.wait_ge(centered, groups + g + 1)
                    act.activation(sq[:, part, :], xc[:, part, :], ACT.Square).then_inc(squared, 1)
                if 0 < g <= G:
                    part = slice(8 * g - 8, 8 * g)
                    act.wait_ge(summed, groups + g)
                    act.activation(s[:, 3, part], s[:, 2, part], ACT.Sqrt, bias=k.eps[:, 0:1], scale=1.0 / D)\
                       .then_inc(rooted, 1)
                if g > 2:
                    evacuate(2 * g - 6)
                    evacuate(2 * g - 5)

        @block.tensor
        def _(pe):
            def project(c):
                pe.wait_ge(evacuated, chunks + c + 1)
                if c > 1:
                    pe.wait_ge(saved, projected + c - 1)
                for t in range(4):
                    tile = slice((4 * c + t) * P, (4 * c + t + 1) * P)
                    ins = pe.matmul(pj[c % 2][:, t, 0:N], xT[:, tile], weight)
                ins.then_inc(mapped, 1)

            for c in range(n):
                pe.wait_ge(scaled, chunks + c + 1)
                if c > 1:
                    pe.wait_ge(evacuated, chunks + c - 1)
                for t in range(4):
                    ins = pe.transpose(pT[c % 2][:, t * P:(t + 1) * P], xs[c % 2][:, t, :], k.ident[:])
                ins.then_inc(turned, 1)
                if N and c > 0:
                    project(c - 1)
            if N:
                project(n - 1)


def window_attention(nc, mem, k, xT, h, sort):
    xs = [mem.sb(f"wa_x{b}", [D + 1, 2, 2, WIN]) for b in range(2)]
    qk = [mem.sb(f"wa_qk{b}", [P, 2, WIN]) for b in range(2)]
    kbd = [mem.sb(f"wa_kbd{b}", [P, NH, WIN]) for b in range(2)]
    vbd = [mem.sb(f"wa_vbd{b}", [P, 2, NH // 2, 2, HD + 1]) for b in range(2)]
    sc = [mem.sb(f"wa_scores{b}", [P, NH, WIN]) for b in range(2)]
    pr = [mem.sb(f"wa_probs{b}", [P, NH, WIN]) for b in range(2)]
    prT = [mem.sb(f"wa_probsT{b}", [P, NH // 2, P]) for b in range(2)]
    mx = [mem.sb(f"wa_max{b}", [P, NH]) for b in range(2)]
    rs = [mem.sb(f"wa_rsum{b}", [P, NH]) for b in range(2)]
    o = [mem.sb(f"wa_o{b}", [P, D]) for b in range(2)]
    oT = [mem.sb(f"wa_oT{b}", [D + 1, P]) for b in range(2)]
    qkv_ps = [mem.ps(f"wa_qkv_ps{b}", [P, 512]) for b in range(2)]
    s_ps = [mem.ps(f"wa_s_ps{b}", [P, NH, WIN]) for b in range(2)]
    t_ps = [mem.ps(f"wa_t_ps{b}", [P, NH // 2, P]) for b in range(2)]
    o_ps = [mem.ps(f"wa_o_ps{b}", [P, 512]) for b in range(2)]
    names = ("x_ready", "qkv_done", "qk_ready", "kbd_ready", "v0_ready", "vbd_ready", "scores_done", "biased",
             "max_done", "shifted", "exp_done", "rsum_done", "probs_turned", "probsT_ready",
             "o_done", "o_scaled", "o_turned", "oT_ready", "proj_done", "added", "zeroed", "ones")
    (x_ready, qkv_done, qk_ready, kbd_ready, v0_ready, vbd_ready, scores_done, biased, max_done, shifted,
     exp_done, rsum_done, probs_turned, probsT_ready, o_done, o_scaled, o_turned, oT_ready,
     proj_done, added, zeroed, ones) = (mem.sem("wa_" + x) for x in names)
    n = TILES
    OW = 2 * (HD + 1)

    with nc.Block() as block:
        @block.gpsimd
        def _(pool):

            def take(c, b, first):
                if not first:
                    pool.wait_ge(qkv_done, c - 1)
                pair = xT[:, bass.ts(c, P)].rearrange("d (r s) -> d r s", r=2)
                pool.tensor_copy(xs[b][:], bc_at(pair, 2, 2)).then_inc(x_ready, 1)

            def keys(c, b, first):
                pool.wait_ge(qk_ready, c + 1)
                if not first:
                    pool.wait_ge(scores_done, c - 1)
                pool.tensor_tensor(kbd[b][:], bc_at(qk[b][:, 1, :], 1, NH),
                                   bc(k.headmask[:, 0, :], WIN), ALU.mult).then_inc(kbd_ready, 1)

            def shift(c, b):
                pool.wait_ge(max_done, c + 1)
                pool.tensor_tensor(sc[b][:], sc[b][:], bc(mx[b][:], WIN), ALU.subtract).then_inc(shifted, 1)

            for b in range(2):
                take(b, b, True)
            for b in range(2):
                keys(b, b, True)
                take(b + 2, b, False)
            for b in range(2):
                shift(b, b)
            with pool.Fori(0, n // 2 - 2) as i:
                for b in range(2):
                    keys(2 * i + b + 2, b, False)
                    shift(2 * i + b + 2, b)
                    take(2 * i + b + 4, b, False)
            for b in range(2):
                keys(n - 2 + b, b, False)
                shift(n - 2 + b, b)

        @block.tensor
        def _(pe):
            def qkv(c, b, first):
                pe.wait_ge(x_ready, c + 1)
                if not first:
                    pe.wait_ge(qk_ready, c - 1)
                    pe.wait_ge(vbd_ready, c - 1)
                pe.sem_inc(k.pe_passed, 1)
                for r in range(2):
                    half = xs[b][:, r, 0, :]
                    for j in range(2):
                        pe.matmul(qkv_ps[b][r * D:(r + 1) * D, j * WIN:(j + 1) * WIN],
                                  k.wqkv[:, j * D:(j + 1) * D], half)
                for r in range(2):
                    both = xs[b][:, r].rearrange("d t s -> d (t s)")
                    ins = pe.matmul(qkv_ps[b][:, (2 + r) * D:(3 + r) * D], both, k.wqkv[:, 2 * D:3 * D])
                ins.then_inc(qkv_done, 1)

            def scores(c, b, first):
                pe.wait_ge(qk_ready, c + 1)
                pe.wait_ge(kbd_ready, c + 1)
                if not first:
                    pe.wait_ge(biased, c - 1)
                pe.sem_inc(k.pe_passed, 1)
                for r in range(2):
                    half = slice(r * D, (r + 1) * D)
                    ins = pe.matmul(s_ps[b][half], qk[b][half, 0, :], kbd[b][half])
                ins.then_inc(scores_done, 1)

            def turn(c, b, first):
                pe.wait_ge(exp_done, c + 1)
                if not first:
                    pe.wait_ge(probsT_ready, c - 1)
                for g in range(NH // 2):
                    ins = pe.transpose(t_ps[b][:, g, :], pr[b][:, 2 * g:2 * g + 2, :], k.ident[:])
                ins.then_inc(probs_turned, 1)

            def values(c, b, first):
                pe.wait_ge(probsT_ready, c + 1)
                pe.wait_ge(vbd_ready, c + 1)
                if not first:
                    pe.wait_ge(added, c - 1)
                for r in range(2):
                    for g in range(NH // 2):
                        ins = pe.matmul(o_ps[b][r * WIN:(r + 1) * WIN, OW * g:OW * (g + 1)],
                                        prT[b][:, g, r * WIN:(r + 1) * WIN], vbd[b][:, r, g])
                ins.then_inc(o_done, 1)

            def turn_out(c, b):
                pe.wait_ge(o_scaled, c + 1)
                pe.sem_inc(k.pe_passed, 1)
                pe.transpose(o_ps[b][0:D, 128:256], o[b][:], k.ident[:]).then_inc(o_turned, 1)

            def project(c, b):
                pe.wait_ge(oT_ready, c + 1)
                pe.matmul(o_ps[b][:, 256:256 + D], oT[b][:], k.wproj[:]).then_inc(proj_done, 1)

            def step(c, b, first=False, start=False, end=False):
                turn(c, b, first)
                if not end:
                    qkv(c + 2, b, False)
                if not start:
                    turn_out(c - 1, 1 - b)
                values(c, b, first)
                if not start:
                    project(c - 1, 1 - b)
                if not end:
                    scores(c + 2, b, False)

            pe.wait_ge(ones, 6)
            qkv(0, 0, True)
            qkv(1, 1, True)
            scores(0, 0, True)
            scores(1, 1, True)
            step(0, 0, first=True, start=True)
            step(1, 1, first=True)
            with pe.Fori(1, n // 2 - 1) as i:
                for b in range(2):
                    step(2 * i + b, b)
            step(n - 2, 0, end=True)
            step(n - 1, 1, end=True)
            turn_out(n - 1, 1)
            project(n - 1, 1)

        @block.scalar
        def _(act):
            act.wait_ge(zeroed, 2)

            def queries(c, b, first):
                act.wait_ge(qkv_done, c + 1)
                if not first:
                    act.wait_ge(scores_done, c - 1)
                act.activation(qk[b][:].rearrange("d j s -> d (j s)"), qkv_ps[b][:, 0:2 * WIN],
                               ACT.Copy).then_inc(qk_ready, 1)

            def values(c, b, first):
                if not first:
                    act.wait_ge(o_done, c - 1)
                v = qkv_ps[b][:, 2 * D:4 * D].rearrange("s (r g t d) -> s r g t d", r=2, t=2, d=HD)
                for t in range(2):
                    half = slice(t * WIN, (t + 1) * WIN)
                    act.activation(vbd[b][half, :, :, t, 0:HD], v[half, :, :, t, :], ACT.Copy)\
                       .then_inc((v0_ready, vbd_ready)[t], 1)

            def probs(c, b, first):
                act.wait_ge(shifted, c + 1)
                if not first:
                    act.wait_ge(probs_turned, c - 1)
                act.activation(pr[b][:], sc[b][:], ACT.Exp).then_inc(exp_done, 1)

            def turned(c, b, first):
                act.wait_ge(probs_turned, c + 1)
                if not first:
                    act.wait_ge(o_done, c - 1)
                act.activation(prT[b][:], t_ps[b][:], ACT.Copy).then_inc(probsT_ready, 1)

            def outT(c, b):
                act.wait_ge(o_turned, c + 1)
                act.activation(oT[b][0:D, :], o_ps[b][0:D, 128:256], ACT.Copy).then_inc(oT_ready, 1)

            def step(c, b, first=False, start=False, end=False, last=False):
                turned(c, b, first)
                if not end:
                    queries(c + 2, b, False)
                if not start:
                    outT(c - 1, 1 - b)
                if not last:
                    probs(c + 1, 1 - b, start)
                if not end:
                    values(c + 2, b, False)

            for b in range(2):
                queries(b, b, True)
                values(b, b, True)
            probs(0, 0, True)
            step(0, 0, first=True, start=True)
            step(1, 1, first=True)
            with act.Fori(1, n // 2 - 1) as i:
                for b in range(2):
                    step(2 * i + b, b)
            step(n - 2, 0, end=True)
            step(n - 1, 1, end=True, last=True)
            outT(n - 1, 1)

        @block.vector
        def _(dve):
            def bias(c, b, first):
                dve.wait_ge(scores_done, c + 1)
                if not first:
                    dve.wait_ge(exp_done, c - 1)
                dve.scalar_tensor_tensor(sc[b][:], s_ps[b][:], float(HD) ** -0.5, k.relbias[:], ALU.mult,
                                         ALU.add).then_inc(biased, 1)
                dve.wait_ge(biased, c + 1)
                if not first:
                    dve.wait_ge(shifted, c - 1)
                dve.tensor_reduce(mx[b][:], sc[b][:], AX.X, ALU.max).then_inc(max_done, 1)

            def scale(c, b, first):
                dve.wait_ge(o_done, c + 1)
                out = o_ps[b][:, 0:NH * (HD + 1)].rearrange("q (h d) -> q h d", d=HD + 1)
                dve.reciprocal(rs[b][:], out[:, :, HD]).then_inc(rsum_done, 1)
                dve.wait_ge(rsum_done, c + 1)
                if not first:
                    dve.wait_ge(o_turned, c - 1)
                dve.tensor_tensor(o[b][:].rearrange("q (h d) -> q h d", d=HD), out[:, :, 0:HD],
                                  bc(rs[b][:], HD), ALU.mult).then_inc(o_scaled, 1)

            def add(c, b):
                dve.wait_ge(proj_done, c + 1)
                dve.tensor_tensor(h[:, bass.ds(c, 1), :].rearrange("p a d -> p (a d)"),
                                  h[:, bass.ds(c, 1), :].rearrange("p a d -> p (a d)"),
                                  o_ps[b][:, 256:256 + D], ALU.add).then_inc(added, 1)

            for b in range(2):
                dve.memset(vbd[b][:], 0.0).then_inc(zeroed, 1)
            dve.wait_ge(zeroed, 2)
            for b in range(2):
                for x in range(2):
                    dve.memset(vbd[b][x * WIN:(x + 1) * WIN, :, :, x, HD:HD + 1], 1.0).then_inc(ones, 1)
                dve.memset(oT[b][D:D + 1, :], 1.0).then_inc(ones, 1)
            for b in range(2):
                bias(b, b, True)
            for c in range(n):
                b = c % 2
                sort.merge(dve, MERGES_TOKENS + (len(sort.network) - MERGES_TOKENS) * (c + 1) // n)
                scale(c, b, c < 2)
                if c > 0:
                    add(c - 1, 1 - b)
                if c + 2 < n:
                    bias(c + 2, b, False)
            add(n - 1, 1)


class EdgeSort:

    def __init__(self, mem):
        self.src_rows, self.dst_rows = (mem.sb(f"edge_{x}", [P, EC + 2 * GCH], I32) for x in ("src", "dst"))
        self.src, self.dst = self.src_rows[:, 0:EC], self.dst_rows[:, 0:EC]
        self.keys, self.other = mem.sb("edge_keys", [P, EC]), mem.sb("sort_other", [P, EC])
        self.lo, self.hi = mem.sb("edge_dst_lo", [P, EC], I32), mem.sb("edge_dst_hi", [P, EC], I32)
        self.last_lo, self.last_hi = mem.sb("last_dst_lo", [P, EC], BF16), mem.sb("last_dst_hi", [P, EC], BF16)
        self.stat, self.top = mem.sb("edge_stat", [P, 4]), mem.sb("edge_top", [P, 4])
        self.lim = mem.sb("edge_limits", [P, 4], I32)
        self.limits = mem.sb("column_limits", [P, 3], I32)
        self.loaded, self.step = mem.sem("edges_loaded"), mem.sem("sort_step")
        self.counted, self.reduced = mem.sem("classes_counted"), mem.sem("classes_reduced")
        self.network = []
        run = 2
        while run <= EC:
            self.network += [(run, None)] + [(run, run // 4 >> i) for i in range((run // 2).bit_length() - 1)]
            run *= 2
        self.done = 0
        self.merges = 0

    def load(self, sp, edges):
        edges = edges.rearrange("a (p c) -> a p c", p=P)
        sp.dma_start(self.src[:], edges[0]).then_inc(self.loaded, 16)
        sp.dma_start(self.dst[:], edges[1]).then_inc(self.loaded, 16)

    def after(self, dve, ins):
        ins.then_inc(self.step, 1)
        self.done += 1
        dve.wait_ge(self.step, self.done)

    def form_keys(self, dve, part):
        A, B, C = self.keys[:], self.other[:], self.lo[:].bitcast(F32)
        src, dst = self.src, self.dst
        if part == 0:
            dve.wait_ge(self.loaded, 32)
            self.after(dve, dve.tensor_scalar(A, src[:], float(M - 1), None, ALU.min))
            self.after(dve, dve.scalar_tensor_tensor(B, dst[:], float(M), A, ALU.mult, ALU.add))
            self.after(dve, dve.tensor_scalar(C, dst[:], float(2 - M), CLASS_LAST - (M - 1), ALU.mult, ALU.add))
        else:
            self.after(dve, dve.scalar_tensor_tensor(C, A, float(M - 1), C, ALU.is_equal, ALU.mult))
            self.after(dve, dve.tensor_tensor(B, B, C, ALU.add))
            self.after(dve, dve.tensor_scalar(C, dst[:], float(M), CLASS_NONE, ALU.is_ge, ALU.mult))
            self.after(dve, dve.scalar_tensor_tensor(A, B, CLASS_NONE, C, ALU.min, ALU.max))

    def merge(self, dve, until):
        while self.merges < until:
            run, dist = self.network[self.merges]
            cur, nxt = (self.keys, self.other) if self.merges % 2 == 0 else (self.other, self.keys)
            if dist is None:
                x, y = (t[:].rearrange("p (n r) -> p n r", r=run) for t in (cur, nxt))
                low, high = slice(0, run // 2), slice(run - 1, run // 2 - 1, -1)
                ins = ((y[:, :, low], x[:, :, low]), (y[:, :, high], x[:, :, high]))
            else:
                x, y = (t[:].rearrange("p (n t r) -> p n t r", t=2, r=dist) for t in (cur, nxt))
                ins = ((y[:, :, 0], x[:, :, 0]), (y[:, :, 1], x[:, :, 1]))
            dve.wait_ge(self.step, self.done)
            dve.tensor_tensor(ins[0][0], ins[0][1], ins[1][1], ALU.min).then_inc(self.step, 1)
            dve.tensor_tensor(ins[1][0], ins[0][1], ins[1][1], ALU.max).then_inc(self.step, 1)
            self.done += 2
            self.merges += 1

    def find_digits(self, dve, part):
        A, C = self.keys[:], self.other[:]
        key, src, dst, lo, hi, stat = self.hi, self.src, self.dst, self.lo, self.hi, self.stat
        if part == 0:
            assert self.merges == len(self.network) and self.merges % 2 == 0, "the sorted keys are in their place"
            dve.wait_ge(self.step, self.done)
            self.after(dve, dve.tensor_scalar(C, A, CLASS_LAST, 0.0, ALU.is_lt, ALU.add, accum_out=stat[:, 0:1]))
        elif part == 1:
            self.after(dve, dve.tensor_scalar(C, A, CLASS_NONE, 0.0, ALU.is_lt, ALU.add, accum_out=stat[:, 1:2]))
            dve.tensor_scalar(stat[:, 2:3], stat[:, 0:1], -1.0, None, ALU.mult).then_inc(self.counted, 1)
        elif part == 2:
            self.after(dve, dve.tensor_copy(key[:], A))
            self.after(dve, dve.tensor_scalar(lo[:], key[:], 8, None, ALU.arith_shift_right))
        elif part == 3:
            self.after(dve, dve.tensor_scalar(self.last_hi[:], lo[:], CLASS_LAST / 256, None, ALU.subtract))
            self.after(dve, dve.tensor_scalar(lo[:], key[:], 1, P - 1, ALU.arith_shift_right, ALU.bitwise_and))
        elif part == 4:
            self.after(dve, dve.tensor_copy(self.last_lo[:], lo[:]))
            self.after(dve, dve.tensor_scalar(src[:], key[:], M - 1, None, ALU.bitwise_and))
        elif part == 5:
            self.after(dve, dve.tensor_scalar(dst[:], key[:], 12, None, ALU.arith_shift_right))
            self.after(dve, dve.tensor_scalar(lo[:], dst[:], P - 1, None, ALU.bitwise_and))
        elif part == 6:
            self.after(dve, dve.tensor_scalar(hi[:], dst[:], 7, None, ALU.arith_shift_right))
            self.after(dve, dve.tensor_scalar(dst[:], dst[:], float(M - 1), None, ALU.min))

    def reduce_counts(self, pool):
        pool.wait_ge(self.counted, 1)
        pool.partition_all_reduce(self.top[:, 0:3], self.stat[:, 0:3], P, bass.bass_isa.ReduceOp.max)\
            .then_inc(self.reduced, 1)

    def find_limits(self, dve):
        top, lim, limits = self.top, self.lim, self.limits
        dve.wait_ge(self.reduced, 1)
        self.after(dve, dve.tensor_scalar(lim[:, 0:1], top[:, 0:1], -1.0, None, ALU.add))
        self.after(dve, dve.tensor_scalar(lim[:, 1:2], top[:, 1:2], float(2 * CCH - 1), None, ALU.add))
        self.after(dve, dve.tensor_scalar(lim[:, 2:3], top[:, 2:3], -1.0, float(EC - 1), ALU.mult, ALU.min))
        sh = (2 * GCH).bit_length() - 1
        self.after(dve, dve.tensor_scalar(lim[:, 0:1], lim[:, 0:1], sh, None, ALU.arith_shift_right))
        sh = (2 * CCH).bit_length() - 1
        self.after(dve, dve.tensor_scalar(lim[:, 1:3], lim[:, 1:3], sh, None, ALU.arith_shift_right))
        self.after(dve, dve.tensor_scalar(limits[:, 0:1], lim[:, 0:1], float(EXPERT_PAIRS), None, ALU.max))
        self.after(dve, dve.tensor_scalar(lim[:, 2:3], lim[:, 2:3], float(EC // (2 * CCH) - COUNT_PAIRS - 1),
                                          None, ALU.min))
        self.after(dve, dve.tensor_tensor(lim[:, 3:4], lim[:, 1:2], lim[:, 2:3], ALU.subtract))
        self.after(dve, dve.tensor_scalar(limits[:, 1:2], lim[:, 3:4], float(COUNT_PAIRS + 1), None, ALU.max))
        self.after(dve, dve.tensor_copy(limits[:, 2:3], lim[:, 2:3]))


def graph_router(nc, mem, a, k, hg, sort, xT, ys, gates):
    W = GH * GE
    srow, drow = mem.sb("src_rows", [P, TILES, NSRC]), mem.sb("dst_rows", [P, TILES, NDST])
    srow_dram = nc.dram_tensor("src_rows_dram", (M, NSRC), F32, kind="Internal").ap()
    drow_dram = nc.dram_tensor("dst_rows_dram", (M, NDST), F32, kind="Internal").ap()
    last, counts = mem.sb("last_row", [P, NSRC]), mem.sb("last_counts", [P, TILES])
    prod = mem.sb("router_prod", [P, TILES, W])
    e = mem.sb("router_e", [P, 3, TILES, GH])
    mx, top = mem.sb("src_max", [P, GH]), mem.sb("src_top", [P, GH])
    own = mem.sb("own_values", [P, TILES, GH, GE + 1])
    from_last = mem.sb("values_from_last", [P, TILES, GH, GE + 1])
    step, own_step = mem.sem("nodes_step"), mem.sem("own_step")
    src_ready, dst_ready, max_ready, top_ready = (
        mem.sem(x) for x in ("src_rows_ready", "dst_rows_ready", "src_max_ready", "src_top_ready"))
    src_stored, last_loaded, dst_stored = (
        mem.sem(x) for x in ("src_rows_stored", "last_row_loaded", "dst_rows_stored"))
    self_shift, last_shift, self_exp, last_exp = (
        mem.sem(x) for x in ("self_shifted", "last_shifted", "self_exp", "last_exp"))
    sview = srow[:, :, W:NSRC]
    dview, mview = drow[:, :, 0:GH], drow[:, :, GH:NDST]
    with nc.Block() as block:
        @block.vector
        def _(dve):
            done = 0

            def after(ins):
                nonlocal done
                ins.then_inc(step, 1)
                done += 1
                dve.wait_ge(step, done)

            after(dve.tensor_tensor(prod[:], hg[:], bc_at(k.att_src[:], 1, TILES), ALU.mult))
            dve.tensor_copy(srow[:, :, 0:W], hg[:]).then_inc(src_ready, 1)
            dve.tensor_reduce(sview, prod[:].rearrange("p t (h e) -> p t h e", e=GE), AX.X,
                              ALU.add).then_inc(src_ready, 1)
            dve.wait_ge(src_ready, 2)
            dve.tensor_reduce(mx[:], sview.rearrange("p t h -> p h t"), AX.X, ALU.max).then_inc(max_ready, 1)
            after(dve.tensor_tensor(prod[:], hg[:], bc_at(k.att_dst[:], 1, TILES), ALU.mult))
            after(dve.tensor_reduce(dview, prod[:].rearrange("p t (h e) -> p t h e", e=GE), AX.X, ALU.add))
            sort.find_limits(dve)
            dve.wait_ge(top_ready, 1)
            after(dve.tensor_tensor(e[:, 0], dview, bc_at(top[:], 1, TILES), ALU.add))
            dve.scalar_tensor_tensor(mview, e[:, 0], 0.2, e[:, 0], ALU.mult, ALU.max).then_inc(dst_ready, 1)
            dve.wait_ge(dst_ready, 1)

        @block.gpsimd
        def _(pool):
            sort.reduce_counts(pool)
            pool.wait_ge(max_ready, 1)
            pool.partition_all_reduce(top[:], mx[:], P, bass.bass_isa.ReduceOp.max).then_inc(top_ready, 1)

        @block.sync
        def _(sp):
            sp.wait_ge(src_ready, 2)
            sp.dma_start(srow_dram.rearrange("(t p) f -> p t f", p=P), srow[:]).then_inc(src_stored, 16)
            sp.wait_ge(src_stored, 16)
            sp.dma_start(last[:], bass.AP(srow_dram.tensor, (M - 1) * NSRC, [[0, P], [1, NSRC]]))\
              .then_inc(last_loaded, 16)
            sp.wait_ge(dst_ready, 1)
            sp.dma_start(drow_dram.rearrange("(t p) f -> p t f", p=P), drow[:]).then_inc(dst_stored, 16)
            sp.wait_ge(dst_stored, 16)

    loop = Stage(mem)
    olo = [loop.sb(f"edge_onehot_lo{b}", [P, GCH, P]) for b in range(2)]
    ohi = [loop.sb(f"edge_onehot_hi{b}", [P, GCH, TILES]) for b in range(2)]
    gs = [loop.sb(f"edge_src_row{b}", [P, GCH, NSRC]) for b in range(2)]
    gd = [loop.sb(f"edge_dst_row{b}", [P, GCH, NDST]) for b in range(2)]
    ee = [loop.sb(f"edge_e{b}", [P, 2, GCH, GH]) for b in range(2)]
    spread = [loop.sb(f"edge_spread{b}", [P, GCH, TILES, NV]) for b in range(2)]
    si, di = ([loop.sb(f"edge_{x}_index{b}", [P, GCH], I32) for b in range(2)] for x in ("src", "dst"))
    clo = [loop.sb(f"count_onehot_lo{b}", [P, CCH, P], BF16) for b in range(2)]
    chi = [loop.sb(f"count_onehot_hi{b}", [P, CCH, TILES], BF16) for b in range(2)]
    hs = [loop.sb(f"moe0_hidden{b}", [P, 512]) for b in range(2)]
    vals = mem.ps("edge_values", [P, 2, GCH, GH, GE + 1])
    val = [vals[:, b] for b in range(2)]
    iota, iota_ready = mem.ps("iota_in_psum", [P, 512]), mem.sem("iota_ready")
    iota_row = iota[:, 0:P]
    acc = mem.ps("edge_acc", [P, 2, 512])
    HALF = TILES // 2 * NV
    count_acc = acc[:, 0, HALF:HALF + TILES]
    h_ps = [mem.ps(f"moe0_h_ps{b}", [P, 512]) for b in range(2)]
    y_ps = [mem.ps(f"moe0_y_ps{b}", [P, 512]) for b in range(2)]
    (index_ready, olo_ready, ohi_ready, added, leaky, shifted, exp_done, weighted, spread_ready, used,
     summed) = (mem.sem("edge_" + x) for x in (
         "index_ready", "olo_ready", "ohi_ready", "added", "leaky", "shifted", "exp_done", "weighted",
         "spread_ready", "used", "summed"))
    clo_ready, chi_ready, counted = (mem.sem("count_" + x) for x in ("lo_ready", "hi_ready", "used"))
    h_done, gelu_done, y_done, y_saved = (mem.sem("moe0_" + x) for x in ("h_done", "gelu_done", "y_done", "y_saved"))
    gathered = [mem.sem(f"edge_gathered{b}") for b in range(2)]
    PAIRS = EC // (2 * GCH)
    CPAIRS = EC // (2 * CCH)
    w1, w2 = k.w1[0], k.w2[0]

    with nc.Block() as block:
        @block.vector
        def _(dve):
            done = 0

            def after(ins):
                nonlocal done
                ins.then_inc(own_step, 1)
                done += 1
                dve.wait_ge(own_step, done)

            def chunk(c, b, first, turn):
                dve.wait_ge(gathered[b], turn)
                dve.tensor_tensor(ee[b][:, 0], gs[b][:, :, W:NSRC], gd[b][:, :, 0:GH], ALU.add).then_inc(added, 1)
                dve.wait_ge(added, c + 1)
                dve.scalar_tensor_tensor(ee[b][:, 1], ee[b][:, 0], 0.2, ee[b][:, 0], ALU.mult,
                                         ALU.max).then_inc(leaky, 1)
                dve.wait_ge(leaky, c + 1)
                dve.tensor_tensor(ee[b][:, 0], ee[b][:, 1], gd[b][:, :, GH:NDST], ALU.subtract).then_inc(shifted, 1)
                dve.wait_ge(exp_done, c + 1)
                dve.tensor_tensor(val[b][:, :, :, 0:GE], gs[b][:, :, 0:W].rearrange("p c (h e) -> p c h e", e=GE),
                                  bc(val[b][:, :, :, GE], GE), ALU.mult).then_inc(weighted, 1)
                if not first:
                    dve.wait_ge(used, c - 1)
                dve.tensor_tensor(olo[b][:], bc_at(iota_row, 1, GCH), bc(sort.lo[:, bass.ts(c, GCH)], P),
                                  ALU.is_equal).then_inc(olo_ready, 1)
                dve.tensor_tensor(ohi[b][:], bc_at(iota[:, 0:TILES], 1, GCH),
                                  bc(sort.hi[:, bass.ts(c, GCH)], TILES), ALU.is_equal).then_inc(ohi_ready, 1)
                dve.wait_ge(weighted, c + 1)
                dve.wait_ge(ohi_ready, c + 1)
                dve.tensor_tensor(spread[b][:], bc_at(val[b][:].rearrange("p c h e -> p c (h e)"), 2, TILES),
                                  bc(ohi[b][:], NV), ALU.mult).then_inc(spread_ready, 1)

            def count(pair):
                column = nc.s_assert_within(at + pair, 0, CPAIRS - 1)
                for q in range(2):
                    c = 2 * pair + q
                    dve.wait_ge(counted, c + 1)
                    part = bass.ds(column * (2 * CCH) + q * CCH, CCH)
                    dve.tensor_tensor(clo[q][:], bc_at(iota_row, 1, CCH), bc(sort.last_lo[:, part], P),
                                      ALU.is_equal).then_inc(clo_ready, 1)
                    dve.tensor_tensor(chi[q][:], bc_at(iota[:, 0:TILES], 1, CCH),
                                      bc(sort.last_hi[:, part], TILES), ALU.is_equal).then_inc(chi_ready, 1)

            def save(i, e):
                dve.wait_ge(y_done, 4 * i + e + 1)
                dve.tensor_tensor(ys[e][:, bass.ts(i, 4), :], y_ps[e % 2][:, 0:4 * D].rearrange("p (t d) -> p t d", d=D),
                                  bc_at(k.b2_rows[:, e, :], 1, 4), ALU.add).then_inc(y_saved, 1)

            n = dve.value_load(sort.limits[0:1, 0:1], min_val=EXPERT_PAIRS, max_val=PAIRS - 1)
            m = dve.value_load(sort.limits[0:1, 1:2], min_val=COUNT_PAIRS + 1, max_val=CPAIRS)
            at = dve.value_load(sort.limits[0:1, 2:3], min_val=0, max_val=CPAIRS - COUNT_PAIRS - 1)
            dve.tensor_copy(iota_row, k.iota_lo[:]).then_inc(iota_ready, 1)
            after(dve.tensor_tensor(e[:, 0], dview, sview, ALU.add))
            after(dve.scalar_tensor_tensor(e[:, 1], e[:, 0], 0.2, e[:, 0], ALU.mult, ALU.max))
            dve.tensor_tensor(e[:, 0], e[:, 1], mview, ALU.subtract).then_inc(self_shift, 1)
            dve.wait_ge(last_loaded, 16)
            dve.wait_ge(self_shift, 1)
            after(dve.tensor_tensor(e[:, 1], dview, bc_at(last[:, W:NSRC], 1, TILES), ALU.add))
            after(dve.scalar_tensor_tensor(e[:, 2], e[:, 1], 0.2, e[:, 1], ALU.mult, ALU.max))
            dve.tensor_tensor(e[:, 1], e[:, 2], mview, ALU.subtract).then_inc(last_shift, 1)
            dve.wait_ge(self_exp, 1)
            after(dve.tensor_tensor(own[:, :, :, 0:GE], hg[:].rearrange("p t (h e) -> p t h e", e=GE),
                                    bc(own[:, :, :, GE], GE), ALU.mult))
            dve.wait_ge(last_exp, 1)
            for hh in range(GH):
                after(dve.tensor_tensor(from_last[:, :, hh, 0:GE], bc_at(last[:, hh * GE:(hh + 1) * GE], 1, TILES),
                                        bc(from_last[:, :, hh, GE], GE), ALU.mult))
            dve.wait_ge(iota_ready, 1)
            for b in range(2):
                chunk(b, b, True, 256)
                for x in range(2 * b, 2 * b + 2):
                    save(0, x)
            with dve.Fori(1, EXPERT_PAIRS) as i:
                for b in range(2):
                    chunk(2 * i + b, b, False, 256 * i + 256)
                    count(2 * (i - 1) + b)
                    for x in range(2 * b, 2 * b + 2):
                        save(i, x)
            with dve.Fori(EXPERT_PAIRS, n + 1) as i:
                for b in range(2):
                    chunk(2 * i + b, b, False, 256 * i + 256)
            with dve.Fori(COUNT_PAIRS, m) as i:
                count(i)

        @block.gpsimd
        def _(pool):
            def gather(c, b, first):
                if not first:
                    pool.wait_ge(weighted, c - 1)
                pool.wait_ge(index_ready, 2 * c + 2)
                pool.sem_inc(k.pool_passed, 1)
                for j in range(GCH):
                    pool.indirect_dma_start(gs[b][:, j, :], None, srow_dram,
                                            bass.IndirectOffsetOnAxis(si[b][:, j:j + 1], axis=0))\
                        .then_inc(gathered[b], 16)
                    pool.indirect_dma_start(gd[b][:, j, :], None, drow_dram,
                                            bass.IndirectOffsetOnAxis(di[b][:, j:j + 1], axis=0))\
                        .then_inc(gathered[b], 16)

            pool.wait_ge(dst_stored, 16)
            n = pool.value_load(sort.limits[0:1, 0:1], min_val=EXPERT_PAIRS, max_val=PAIRS - 1)
            gather(0, 0, True)
            gather(1, 1, True)
            with pool.Fori(1, n + 1) as i:
                for b in range(2):
                    gather(2 * i + b, b, False)

        @block.scalar
        def _(act):
            def exps(c, b):
                act.wait_ge(shifted, c + 1)
                act.activation(val[b][:, :, :, GE], ee[b][:, 0], ACT.Exp).then_inc(exp_done, 1)

            def indices(c, b, first):
                if not first:
                    act.wait_ge(weighted, c - 1)
                act.activation(si[b][:], sort.src_rows[:, bass.ts(c, GCH)], ACT.Copy).then_inc(index_ready, 1)
                act.activation(di[b][:], sort.dst_rows[:, bass.ts(c, GCH)], ACT.Copy).then_inc(index_ready, 1)

            def gelu(i, e, first):
                act.wait_ge(h_done, 4 * i + e + 1)
                if not first:
                    act.wait_ge(y_done, 4 * i + e - 1)
                act.activation(hs[e % 2][:], h_ps[e % 2][:], ACT.Gelu).then_inc(gelu_done, 1)

            n = act.value_load(sort.limits[0:1, 0:1], min_val=EXPERT_PAIRS, max_val=PAIRS - 1)
            for b in range(2):
                indices(b, b, True)
            act.wait_ge(self_shift, 1)
            act.activation(own[:, :, :, GE], e[:, 0], ACT.Exp).then_inc(self_exp, 1)
            act.wait_ge(last_shift, 1)
            act.activation(from_last[:, :, :, GE], e[:, 1], ACT.Exp).then_inc(last_exp, 1)
            for b in range(2):
                exps(b, b)
                indices(b + 2, b, False)
                for x in range(2 * b, 2 * b + 2):
                    gelu(0, x, x < 2)
            with act.Fori(1, EXPERT_PAIRS) as i:
                for b in range(2):
                    exps(2 * i + b, b)
                    indices(2 * i + b + 2, b, False)
                    for x in range(2 * b, 2 * b + 2):
                        gelu(i, x, False)
            with act.Fori(EXPERT_PAIRS, n + 1) as i:
                for b in range(2):
                    exps(2 * i + b, b)
                    indices(2 * i + b + 2, b, False)

        @block.tensor
        def _(pe):
            def sums(c, b):
                pe.wait_ge(olo_ready, c + 1)
                pe.wait_ge(spread_ready, c + 1)
                for j in range(GCH):
                    rows = spread[b][:, j].rearrange("p t v -> p (t v)")
                    for half in range(2):
                        ins = pe.matmul(acc[:, half, 0:HALF], olo[b][:, j, :],
                                        rows[:, half * HALF:(half + 1) * HALF], start=False, stop=False,
                                        skip_group_check=True)
                ins.then_inc(used, 1)

            def count(pair):
                for q in range(2):
                    pe.wait_ge(clo_ready, 2 * pair + q + 1)
                    pe.wait_ge(chi_ready, 2 * pair + q + 1)
                    for j in range(CCH):
                        ins = pe.matmul(count_acc, clo[q][:, j, :], chi[q][:, j, :], start=False, stop=False,
                                        skip_group_check=True)
                    ins.then_inc(counted, 1)

            def experts(i, two, first):
                for x in two:
                    if not first:
                        pe.wait_ge(gelu_done, 4 * i + x - 1)
                    pe.matmul(h_ps[x % 2][:], w1[:, x, :], xT[:, bass.ts(i, 512)]).then_inc(h_done, 1)
                for x in two:
                    pe.wait_ge(gelu_done, 4 * i + x + 1)
                    if not first:
                        pe.wait_ge(y_saved, 4 * i + x - 1)
                    for t in range(4):
                        ins = pe.matmul(y_ps[x % 2][:, t * D:(t + 1) * D], hs[x % 2][:, t * P:(t + 1) * P],
                                        w2[:, x, :])
                    ins.then_inc(y_done, 1)

            n = pe.value_load(sort.limits[0:1, 0:1], min_val=EXPERT_PAIRS, max_val=PAIRS - 1)
            m = pe.value_load(sort.limits[0:1, 1:2], min_val=COUNT_PAIRS + 1, max_val=CPAIRS)
            pe.sem_inc(counted, 2)
            for part in (acc[:, 0, 0:HALF], acc[:, 1, 0:HALF], count_acc):
                pe.matmul(part, k.zero_mm[:, 0:P], k.zero_mm[:, 0:part.shape[1]], start=True, stop=False,
                          skip_group_check=True)
            experts(0, (0, 1), True)
            sums(0, 0)
            experts(0, (2, 3), False)
            with pe.Fori(1, EXPERT_PAIRS) as i:
                for b in range(2):
                    sums(2 * i + b - 1, 1 - b)
                    experts(i, (2 * b, 2 * b + 1), False)
                    count(2 * (i - 1) + b)
            with pe.Fori(EXPERT_PAIRS, n + 1) as i:
                for b in range(2):
                    sums(2 * i + b - 1, 1 - b)
            sums(2 * n + 1, 1)
            with pe.Fori(COUNT_PAIRS, m) as i:
                count(i)
            for part in (acc[:, 0, 0:HALF], acc[:, 1, 0:HALF], count_acc):
                ins = pe.matmul(part, k.zero_mm[:, 0:P], k.zero_mm[:, 0:part.shape[1]], start=False, stop=True,
                                skip_group_check=True)
            ins.then_inc(summed, 1)

    loop.ctx.close()
    agg, nrm, sq = mem.sb("agg", [P, TILES, W]), mem.sb("agg_norm", [P, TILES, W]), mem.sb("agg_sq", [P, TILES, W])
    st = mem.sb("agg_stats", [P, 5, TILES])
    scores = mem.sb("router_scores", [P, TILES, E0])
    rden = mem.sb("router_rden", [P, TILES, GH])
    centered, squared, var_ready, std_ready = (
        mem.sem(f"agg_{x}") for x in ("centered", "squared", "var_ready", "std_ready"))
    fstep = mem.sem("agg_step")
    with nc.Block() as block:
        @block.vector
        def _(dve):
            done = 0

            def after(ins):
                nonlocal done
                ins.then_inc(fstep, 1)
                done += 1
                dve.wait_ge(fstep, done)

            after(dve.tensor_copy(counts[:], count_acc))
            flat = from_last[:].rearrange("p t h e -> p t (h e)")
            after(dve.tensor_tensor(flat, flat, bc(counts[:], NV), ALU.mult))
            after(dve.tensor_tensor(own[:], own[:], from_last[:], ALU.add))
            for half in range(2):
                part = own[:, half * 16:(half + 1) * 16].rearrange("p t h e -> p (t h e)")
                after(dve.tensor_tensor(part, part, acc[:, half, 0:HALF], ALU.add))
            after(dve.tensor_scalar(rden[:], own[:, :, :, GE], 1e-16, None, ALU.add))
            after(dve.reciprocal(rden[:], rden[:]))
            after(dve.tensor_tensor(agg[:].rearrange("p t (h e) -> p t h e", e=GE), own[:, :, :, 0:GE],
                                    bc(rden[:], GE), ALU.mult))
            after(dve.tensor_tensor(agg[:], agg[:], bc_at(k.b_gat[:], 1, TILES), ALU.add))
            after(dve.tensor_reduce(st[:, 0], agg[:], AX.X, ALU.add))
            after(dve.tensor_scalar(st[:, 1], st[:, 0], 1.0 / W, None, ALU.mult))
            dve.tensor_tensor(nrm[:], agg[:], bc(st[:, 1], W), ALU.subtract).then_inc(centered, 1)
            dve.wait_ge(squared, 1)
            dve.tensor_reduce(st[:, 2], sq[:], AX.X, ALU.add).then_inc(var_ready, 1)
            dve.wait_ge(std_ready, 1)
            after(dve.reciprocal(st[:, 4], st[:, 3]))
            after(dve.tensor_tensor(agg[:], nrm[:], bc(st[:, 4], W), ALU.mult))
            after(dve.tensor_tensor(agg[:], agg[:], bc_at(k.ln_gamma[:], 1, TILES), ALU.mult))
            after(dve.tensor_tensor(agg[:], agg[:], bc_at(k.ln_beta[:], 1, TILES), ALU.add))
            after(dve.tensor_reduce(scores[:], agg[:].rearrange("p t (h e) -> p t e h", e=GE), AX.X, ALU.add))
            after(dve.tensor_scalar(scores[:], scores[:], 1.0 / GH, None, ALU.mult))

        @block.scalar
        def _(act):
            act.wait_ge(centered, 1)
            act.activation(sq[:], nrm[:], ACT.Square).then_inc(squared, 1)
            act.wait_ge(var_ready, 1)
            act.activation(st[:, 3], st[:, 2], ACT.Sqrt, bias=k.eps[:, 0:1], scale=1.0 / W).then_inc(std_ready, 1)

    top = TopTwo(mem, k.lower0, E0, scores, gates, "moe0")
    with nc.Block() as block:
        @block.vector
        def _(dve):
            top.shift(dve)
            top.choose(dve, slice(0, TILES))

        @block.scalar
        def _(act):
            top.exponentials(act)


class TopTwo:

    def __init__(self, mem, lower, E, scores, gates, name):
        self.ahead, self.same = (mem.sb(f"{name}_{x}", [P, TILES, E, E]) for x in ("ahead", "same"))
        self.sel, self.z = (mem.sb(f"{name}_{x}", [P, TILES, E]) for x in ("sel", "z"))
        self.s = mem.sb(f"{name}_top", [P, 3, TILES])
        self.step, self.shifted, self.exp_done = (
            mem.sem(f"{name}_choose_{x}") for x in ("step", "shifted", "exp_done"))
        self.lower, self.E, self.scores, self.gates = lower, E, scores, gates
        self.done = 0

    def after(self, dve, ins):
        ins.then_inc(self.step, 1)
        self.done += 1
        dve.wait_ge(self.step, self.done)

    def shift(self, dve):
        self.after(dve, dve.tensor_reduce(self.s[:, 0], self.scores[:], AX.X, ALU.max))
        dve.tensor_tensor(self.z[:], self.scores[:], bc(self.s[:, 0], self.E), ALU.subtract).then_inc(self.shifted, 1)

    def exponentials(self, act):
        act.wait_ge(self.shifted, 1)
        act.activation(self.z[:], self.z[:], ACT.Exp).then_inc(self.exp_done, 1)

    def choose(self, dve, tiles):
        E, scores, sel = self.E, self.scores[:, tiles], self.sel[:, tiles]
        same, ahead = self.same[:, tiles], self.ahead[:, tiles]
        others, own = bc_at(scores, 2, E), bc(scores, E)
        self.after(dve, dve.tensor_tensor(same, others, own, ALU.is_equal))
        low = self.lower[:].rearrange("p e j -> p (e j)")
        flat = same.rearrange("p t e j -> p t (e j)")
        self.after(dve, dve.tensor_tensor(flat, flat, bc_at(low, 1, tiles.stop - tiles.start), ALU.mult))
        self.after(dve, dve.tensor_tensor(ahead, others, own, ALU.is_gt))
        self.after(dve, dve.tensor_tensor(ahead, ahead, same, ALU.add))
        self.after(dve, dve.tensor_reduce(sel, ahead, AX.X, ALU.add))
        dve.wait_ge(self.exp_done, 1)
        self.after(dve, dve.scalar_tensor_tensor(sel, sel, 2.0, self.z[:, tiles], ALU.is_lt, ALU.mult))
        self.after(dve, dve.tensor_reduce(self.s[:, 1, tiles], sel, AX.X, ALU.add))
        self.after(dve, dve.reciprocal(self.s[:, 2, tiles], self.s[:, 1, tiles]))
        self.after(dve, dve.tensor_tensor(self.gates[:, tiles], sel, bc(self.s[:, 2, tiles], E), ALU.mult))


def combine(nc, mem, ys, gates, h):
    parts = {"vector": slice(0, 21), "gpsimd": slice(21, TILES)}
    last = E0 - 1
    added, scaled, helped = (
        {e: mem.sem(f"combine_{e}_{x}") for e in parts} for x in ("added", "scaled", "helped"))

    def total(eng, name):
        part = parts[name]
        for e in range(last):
            y = ys[e][:, part, :]
            eng.tensor_tensor(y, y, bc(gates[:, part, e], D), ALU.mult).then_inc(scaled[name], 1)
        for e in range(E0):
            if e < last:
                eng.wait_ge(scaled[name], e + 1)
            else:
                eng.wait_ge(helped[name], part.stop - part.start)
            if e:
                eng.wait_ge(added[name], e)
            eng.tensor_tensor(h[:, part, :], h[:, part, :], ys[e][:, part, :], ALU.add).then_inc(added[name], 1)

    with nc.Block() as block:
        @block.vector
        def _(dve):
            total(dve, "vector")

        @block.gpsimd
        def _(pool):
            total(pool, "gpsimd")

        @block.scalar
        def _(act):
            for name, part in parts.items():
                for t in range(part.start, part.stop):
                    y = ys[last][:, t, :]
                    act.activation(y, y, ACT.Copy, scale=gates[:, t, last:E0]).then_inc(helped[name], 1)


def experts(nc, mem, k, xT, logits, gates, h, out):
    top = TopTwo(mem, k.lower, E1, logits, gates, "moe1")
    w1, w2, E, PAIRS = k.w1[1], k.w2[1], E1, E1 // 2
    R = 3 * E
    rest = mem.sb("gate_rest", [P, TILES, E])
    part = [mem.sb(f"gate_part{j}", [P, TILES, E], BF16) for j in range(3)]
    parts = mem.sb("gate_parts", [P, TILES, 3, E])
    g, gT = mem.sb("moe1_g", [P, 4, R]), mem.sb("moe1_gT", [4 * R, P], BF16)
    hs = [mem.sb(f"moe1_hidden{b}", [P, 512]) for b in range(4)]
    tmp = [mem.sb(f"moe1_weighted{b}", [P, 512]) for b in range(2)]
    acc = mem.sb("moe1_acc", [P, 512])
    h_ps = [mem.ps(f"moe1_h_ps{b}", [P, 512]) for b in range(2)]
    y_ps = [mem.ps(f"moe1_y_ps{b}", [P, 512]) for b in range(2)]
    G = [mem.sb(f"moe1_G{b}", [P, 512]) for b in range(2)]
    G_ps = [mem.ps(f"moe1_G_ps{b}", [P, 512]) for b in range(2)]
    g_ps, f_ps = mem.ps("moe1_g_ps", [4 * R, P]), mem.ps("moe1_fold_ps", [P, 4, D])
    (split, g_ready, g_turned, gT_ready, spread, G_ready, h_done, gelu_done, y_done, weighted, added, folded,
     summed) = (mem.sem("moe1_" + x) for x in (
         "split", "g_ready", "g_turned", "gT_ready", "spread", "G_ready", "h_done", "gelu_done", "y_done",
         "weighted", "added", "folded", "summed"))
    stored = mem.sem("output_stored")
    n = TILES // 4
    with nc.Block() as block:
        @block.tensor
        def _(pe):
            def hidden(c, e):
                pe.wait_ge(gelu_done, c * E + e + 1)
                pe.matmul(h_ps[e % 2][:], w1[:, e, :], xT[:, bass.ts(c, 512)]).then_inc(h_done, 1)

            def output(c, p):
                u = c * PAIRS + p
                pe.wait_ge(gelu_done, 2 * u + 4)
                pe.wait_ge(weighted, u + 1)
                for r in range(2):
                    e = 2 * p + r
                    ins = pe.matmul(y_ps[p % 2][r * D:(r + 1) * D, :], w2[:, e, :], hs[e % 4][:])
                ins.then_inc(y_done, 1)

            def turn(c):
                pe.wait_ge(g_ready, c + 1)
                pe.transpose(g_ps[:], g[:].rearrange("p t e -> p (t e)"), k.ident[:]).then_inc(g_turned, 1)

            def gates_of(c, p):
                pe.wait_ge(gT_ready, c + 1)
                pe.wait_ge(G_ready, c * PAIRS + p + 1)
                for t in range(4):
                    ins = pe.matmul(G_ps[p % 2][:, t * P:(t + 1) * P], k.pick[:, p, t, :], gT[:])
                ins.then_inc(spread, 1)

            def fold(c):
                pe.wait_ge(added, c * PAIRS + 2)
                pe.wait_ge(summed, c)
                for t in range(4):
                    ins = pe.matmul(f_ps[:, t, :], acc[:, t * P:(t + 1) * P], k.fold[:])
                ins.then_inc(folded, 1)

            def chunk(c, first):
                if not first:
                    turn(c)
                for half in range(2):
                    for e in range(4 * half, 4 * half + 4):
                        hidden(c, e)
                    for p in (2 * half, 2 * half + 1):
                        output(c, p)
                    if first and half == 0:
                        turn(c)
                    for p in (2 * half, 2 * half + 1):
                        gates_of(c, p)
                    if half == 0 and not first:
                        fold(c)

            pe.sem_inc(y_done, 2)
            chunk(0, True)
            with pe.Fori(1, n) as c:
                chunk(c, False)
            fold(n)

        @block.scalar
        def _(act):
            def turned(c):
                act.wait_ge(g_turned, c + 1)
                act.activation(gT[:], g_ps[:], ACT.Copy).then_inc(gT_ready, 1)

            def chunk(c, first):
                if not first:
                    turned(c)
                for half in range(2):
                    for e in range(4 * half, 4 * half + 4):
                        act.wait_ge(h_done, c * E + e + 1)
                        act.wait_ge(y_done, c * PAIRS + e // 2 + 1)
                        act.activation(hs[e % 4][:], h_ps[e % 2][:], ACT.Gelu).then_inc(gelu_done, 1)
                    if first and half == 0:
                        turned(c)
                    for p in (2 * half, 2 * half + 1):
                        act.wait_ge(spread, c * PAIRS + p + 1)
                        act.wait_ge(weighted, c * PAIRS + p + 1)
                        act.activation(G[p % 2][:], G_ps[p % 2][:], ACT.Copy).then_inc(G_ready, 1)

            top.exponentials(act)
            act.sem_inc(gelu_done, 2)
            act.sem_inc(G_ready, 2)
            chunk(0, True)
            with act.Fori(1, n) as c:
                chunk(c, False)

        @block.vector
        def _(dve):
            def weigh(c, p):
                u = c * PAIRS + p
                dve.wait_ge(y_done, u + 3)
                dve.wait_ge(G_ready, u + 3)
                dve.wait_ge(added, u + 1)
                dve.scalar_tensor_tensor(tmp[p % 2][:], y_ps[p % 2][:], k.b2_cols[:, p:p + 1],
                                         G[p % 2][:], ALU.add, ALU.mult).then_inc(weighted, 1)

            def total(c):
                dve.wait_ge(folded, c)
                tiles = h[:, bass.ds(c * 4 - 4, 4), :]
                dve.tensor_tensor(tiles, tiles, f_ps[:], ALU.add).then_inc(summed, 1)

            def take(c, first=False):
                if not first:
                    dve.wait_ge(g_turned, c)
                dve.tensor_copy(g[:], parts[:, bass.ts(c, 4), :, :].rearrange("p t j e -> p t (j e)"))\
                   .then_inc(g_ready, 1)

            def chunk(c, last=False):
                weigh(c, 0)
                weigh(c, 1)
                if not last:
                    take(c + 1)
                total(c)
                weigh(c, 2)
                weigh(c, 3)

            ranges = [slice(x, y) for x, y in ((0, 4), (4, 13), (13, 22), (22, TILES))]

            def form_gates(i):
                tiles = ranges[i]
                top.choose(dve, tiles)
                source = gates[:, tiles]
                for j in range(3):
                    dve.tensor_copy(part[j][:, tiles], source).then_inc(split, 1)
                    dve.wait_ge(split, 8 * i + 3 * j + 1)
                    dve.tensor_copy(parts[:, tiles, j, :], part[j][:, tiles]).then_inc(split, 1)
                    if j < 2:
                        dve.tensor_tensor(rest[:, tiles], source, part[j][:, tiles], ALU.subtract).then_inc(split, 1)
                        source = rest[:, tiles]
                    dve.wait_ge(split, 8 * i + min(3 * j + 3, 8))

            dve.sem_inc(weighted, 2)
            dve.sem_inc(summed, 1)
            top.shift(dve)
            form_gates(0)
            take(0, first=True)
            form_gates(1)
            weigh(0, 0)
            weigh(0, 1)
            take(1)
            form_gates(2)
            weigh(0, 2)
            weigh(0, 3)
            form_gates(3)
            with dve.Fori(1, n - 1) as c:
                chunk(c)
            chunk(n - 1, last=True)
            total(n)

        @block.gpsimd
        def _(pool):
            def chunk(c, first):
                for p in range(PAIRS):
                    pool.wait_ge(weighted, c * PAIRS + p + 3)
                    if p == 0:
                        if not first:
                            pool.wait_ge(folded, c)
                        pool.sem_inc(k.pool_passed, 1)
                        pool.tensor_copy(acc[:], tmp[0][:]).then_inc(added, 1)
                    else:
                        pool.wait_ge(added, c * PAIRS + p + 2)
                        pool.tensor_tensor(acc[:], acc[:], tmp[p % 2][:], ALU.add).then_inc(added, 1)
            pool.sem_inc(added, 2)
            chunk(0, True)
            with pool.Fori(1, n) as c:
                chunk(c, False)

        @block.sync
        def _(sp):
            tokens = out.rearrange("(t r) s d -> (r s) t d", r=2)
            for i in range(4):
                sp.wait_ge(summed, (i + 1) * n // 4 + 1)
                tiles = slice(i * TILES // 4, (i + 1) * TILES // 4)
                sp.dma_start(tokens[:, tiles, :], h[:, tiles, :]).then_inc(stored, 16)
            sp.wait_ge(stored, 64)


def image_attention(nc, mem, k, xT, yT, stats):
    xs = [mem.sb(f"ia_x{b}", [P, 4, 2, WIN]) for b in range(2)]
    qk = [mem.sb(f"ia_qk{b}", [P, 2, 4, WIN]) for b in range(2)]
    v = [mem.sb(f"ia_v{b}", [WIN, 8, D]) for b in range(2)]
    sc = [mem.sb(f"ia_scores{b}", [P, 4, WIN]) for b in range(2)]
    ex = [mem.sb(f"ia_exp{b}", [P, 4, WIN]) for b in range(2)]
    pr = [mem.sb(f"ia_probs{b}", [P, 4, WIN]) for b in range(2)]
    prT = [mem.sb(f"ia_probsT{b}", [WIN, 4, P]) for b in range(2)]
    oT = [mem.sb(f"ia_oT{b}", [P, 512]) for b in range(2)]
    mx, sm, rs = ([mem.sb(f"ia_{x}{b}", [P, 4]) for b in range(2)] for x in ("max", "sum", "rsum"))
    qk_ps = [mem.ps(f"ia_qk_ps{b}", [P, 512]) for b in range(2)]
    v_ps = [mem.ps(f"ia_v_ps{b}", [D, 512]) for b in range(2)]
    s_ps = [mem.ps(f"ia_s_ps{b}", [P, 4, WIN]) for b in range(2)]
    t_ps = [mem.ps(f"ia_t_ps{b}", [WIN, 4, P]) for b in range(2)]
    names = ("x_ready", "qk_done", "v_done", "qk_ready", "v_ready", "scores_done", "max_done", "shifted", "exp_done",
             "sum_done", "rsum_done", "probs_done", "turned", "probsT_ready", "o_done", "oT_ready", "y_done",
             "y_saved", "counted", "ones", "xs_zeroed", "oT_zeroed")
    (x_ready, qk_done, v_done, qk_ready, v_ready, scores_done, max_done, shifted, exp_done, sum_done, rsum_done,
     probs_done, turned, probsT_ready, o_done, oT_ready, y_done, y_saved, counted, ones, xs_zeroed, oT_zeroed) = (
         mem.sem("ia_" + x) for x in names)
    n = 8

    def steps(eng, step):
        step(0, 0, True)
        step(1, 1, True)
        with eng.Fori(1, n // 2 - 1) as i:
            for b in range(2):
                step(2 * i + b, b, False)
        step(n - 2, 0, False)
        step(n - 1, 1, False)

    def has(c, more):
        return not isinstance(c, int) or c + more < n

    with nc.Block() as block:
        @block.gpsimd
        def _(pool):
            def take(c, b, first):
                if not first:
                    pool.wait_ge(v_done, c - 1)
                pool.tensor_copy(xs[b][0:D + 1].rearrange("d a r s -> d (a r s)"), xT[:, bass.ts(c, 512)])\
                    .then_inc(x_ready, 1)

            def normal(c, b, first):
                pool.wait_ge(rsum_done, c + 1)
                if not first:
                    pool.wait_ge(turned, c - 1)
                pool.tensor_tensor(pr[b][:], ex[b][:], bc(rs[b][:], WIN), ALU.mult).then_inc(probs_done, 1)

            def step(c, b, first):
                if has(c, 2):
                    take(c + 2, b, False)
                if has(c, 1):
                    normal(c + 1, 1 - b, isinstance(c, int) and c == 0)
            for b in range(2):
                pool.memset(xs[b][D:P], 0.0).then_inc(xs_zeroed, 1)
            pool.wait_ge(xs_zeroed, 2)
            take(0, 0, True)
            take(1, 1, True)
            normal(0, 0, True)
            steps(pool, step)

        @block.tensor
        def _(pe):
            def queries(c, b, first):
                pe.wait_ge(x_ready, c + 1)
                if not first:
                    pe.wait_ge(oT_ready, c - 1)
                pe.sem_inc(k.pe_passed, 1)
                for j in range(2):
                    for r in range(2):
                        out = qk_ps[b][r * D:(r + 1) * D, j * 256:(j + 1) * 256]
                        ins = pe.matmul(out.rearrange("d (a s) -> d a s", a=4), k.wl1[:, j, :], xs[b][:, :, r, :])
                ins.then_inc(qk_done, 1)

            def values_in(c, b, first):
                if not first:
                    pe.wait_ge(y_saved, c - 1)
                    pe.sem_inc(k.pe_passed, 1)
                for w in range(8):
                    ins = pe.matmul(v_ps[b][:, w * D:(w + 1) * D], xs[b][:, w // 2, w % 2, :], k.wl1[:, 2, :])
                ins.then_inc(v_done, 1)

            def scores(c, b, first):
                pe.wait_ge(qk_ready, c + 1)
                if not first:
                    pe.wait_ge(shifted, c - 1)
                pe.sem_inc(k.pe_passed, 1)
                for p in range(2):
                    for r in range(2):
                        half = slice(r * D, (r + 1) * D)
                        pe.matmul(s_ps[b][half, p, :], qk[b][half, 0, p, :], qk[b][half, 1, p, :])

            def more_scores(b):
                for p in range(2, 4):
                    for r in range(2):
                        half = slice(r * D, (r + 1) * D)
                        ins = pe.matmul(s_ps[b][half, p, :], qk[b][half, 0, p, :], qk[b][half, 1, p, :])
                ins.then_inc(scores_done, 1)

            def turn(c, b, first):
                pe.wait_ge(probs_done, c + 1)
                if not first:
                    pe.wait_ge(probsT_ready, c - 1)
                pe.sem_inc(k.pe_passed, 1)
                for p in range(4):
                    ins = pe.transpose(t_ps[b][:, p, :], pr[b][:, p, :], k.ident[:])
                ins.then_inc(turned, 1)

            def values_out(c, b):
                pe.wait_ge(probsT_ready, c + 1)
                pe.wait_ge(v_ready, c + 1)
                pe.sem_inc(k.pe_passed, 1)
                for w in range(8):
                    ins = pe.matmul(qk_ps[b][0:D, w * WIN:(w + 1) * WIN], v[b][:, w, :],
                                    prT[b][:, w // 2, w % 2 * WIN:(w % 2 + 1) * WIN])
                ins.then_inc(o_done, 1)

            def project(c, b):
                pe.wait_ge(oT_ready, c + 1)
                pe.sem_inc(k.pe_passed, 1)
                pe.matmul(v_ps[b][:], k.wl1[:, 3, :], oT[b][:]).then_inc(y_done, 1)

            def step(c, b, first):
                turn(c, b, first)
                if has(c, 1):
                    scores(c + 1, 1 - b, isinstance(c, int) and c == 0)
                values_out(c, b)
                if has(c, 1):
                    more_scores(1 - b)
                project(c, b)
                if has(c, 2):
                    queries(c + 2, b, False)
                    values_in(c + 2, b, False)

            pe.wait_ge(ones, 2)
            for b in range(2):
                queries(b, b, True)
                values_in(b, b, True)
                if b == 0:
                    scores(0, 0, True)
                    more_scores(0)
            steps(pe, step)

        @block.scalar
        def _(act):
            def queries(c, b, first):
                act.wait_ge(qk_done, c + 1)
                if not first:
                    act.wait_ge(scores_done, c - 1)
                act.activation(qk[b][:].rearrange("d j a s -> d (j a s)"), qk_ps[b][:], ACT.Copy)\
                   .then_inc(qk_ready, 1)

            def values_in(c, b, first):
                act.wait_ge(v_done, c + 1)
                if not first:
                    act.wait_ge(o_done, c - 1)
                act.activation(v[b][:].rearrange("s w d -> s (w d)"), v_ps[b][:], ACT.Copy).then_inc(v_ready, 1)

            def exps(c, b, first):
                act.wait_ge(shifted, c + 1)
                if not first:
                    act.wait_ge(probs_done, c - 1)
                act.activation(ex[b][:], sc[b][:], ACT.Exp, scale=1.0 / D).then_inc(exp_done, 1)

            def turn(c, b, first):
                act.wait_ge(turned, c + 1)
                if not first:
                    act.wait_ge(o_done, c - 1)
                act.activation(prT[b][:], t_ps[b][:], ACT.Copy).then_inc(probsT_ready, 1)

            def output(c, b, first):
                act.wait_ge(o_done, c + 1)
                if not first:
                    act.wait_ge(y_done, c - 1)
                act.activation(oT[b][0:D, :], qk_ps[b][0:D, :], ACT.Copy).then_inc(oT_ready, 1)

            def step(c, b, first):
                turn(c, b, first)
                output(c, b, first)
                if has(c, 1):
                    exps(c + 1, 1 - b, isinstance(c, int) and c == 0)
                if has(c, 2):
                    queries(c + 2, b, False)
                    values_in(c + 2, b, False)
            queries(0, 0, True)
            values_in(0, 0, True)
            queries(1, 1, True)
            exps(0, 0, True)
            values_in(1, 1, True)
            steps(act, step)

        @block.vector
        def _(dve):
            for b in range(2):
                dve.memset(oT[b][D:P, :], 0.0).then_inc(oT_zeroed, 1)
            dve.wait_ge(oT_zeroed, 2)
            for b in range(2):
                dve.memset(oT[b][D:D + 1, :], 1.0).then_inc(ones, 1)

            def shift(c, b, first):
                dve.wait_ge(scores_done, c + 1)
                dve.tensor_reduce(mx[b][:], s_ps[b][:], AX.X, ALU.max).then_inc(max_done, 1)
                dve.wait_ge(max_done, c + 1)
                if not first:
                    dve.wait_ge(exp_done, c - 1)
                dve.tensor_tensor(sc[b][:], s_ps[b][:], bc(mx[b][:], WIN), ALU.subtract).then_inc(shifted, 1)

            def sums(c, b, first):
                dve.wait_ge(exp_done, c + 1)
                dve.tensor_reduce(sm[b][:], ex[b][:], AX.X, ALU.add).then_inc(sum_done, 1)
                dve.wait_ge(sum_done, c + 1)
                if not first:
                    dve.wait_ge(probs_done, c - 1)
                dve.reciprocal(rs[b][:], sm[b][:]).then_inc(rsum_done, 1)

            def save(c, b):
                dve.wait_ge(y_done, c + 1)
                dve.tensor_copy(yT[:, bass.ts(c, 512)], v_ps[b][:]).then_inc(y_saved, 1)

            def step(c, b, first):
                if has(c, 1):
                    shift(c + 1, 1 - b, isinstance(c, int) and c == 0)
                    sums(c + 1, 1 - b, isinstance(c, int) and c == 0)
                save(c, b)
                dve.wait_ge(y_saved, c + 1)
                dve.bn_stats(stats[:, bass.ts(c, 6)], yT[:, bass.ts(c, 512)]).then_inc(counted, 1)
            shift(0, 0, True)
            sums(0, 0, True)
            steps(dve, step)


def batch_norm_add(nc, mem, k, xT, yT, stats, h):
    mv = mem.sb("bn_mv", [D, 4])
    z = [mem.sb(f"bn_z{b}", [D, 512]) for b in range(2)]
    r = [mem.sb(f"bn_r{b}", [D, 512]) for b in range(2)]
    s = [mem.sb(f"bn_s{b}", [D, 512]) for b in range(2)]
    t_ps = [mem.ps(f"bn_ps{b}", [P, 4, D]) for b in range(2)]
    step, var_ready, std_ready, scaled, relued, summed, turned, added = (
        mem.sem("bn_" + x) for x in ("step", "var_ready", "std_ready", "scaled", "relued", "summed", "turned", "added"))
    n = 8
    with nc.Block() as block:
        @block.vector
        def _(dve):
            dve.bn_aggr(mv[:, 0:2], stats[:]).then_inc(var_ready, 1)
            dve.wait_ge(std_ready, 1)
            dve.reciprocal(mv[:, 3:4], mv[:, 2:3]).then_inc(step, 1)
            dve.wait_ge(step, 1)
            dve.tensor_tensor(mv[:, 3:4], mv[:, 3:4], k.bn[:, 0:1], ALU.mult).then_inc(step, 1)
            dve.wait_ge(step, 2)

            def scale(c, b, first):
                if not first:
                    dve.wait_ge(relued, c - 1)
                dve.tensor_scalar(z[b][:], yT[:, bass.ts(c, 512)], mv[:, 0:1], mv[:, 3:4], ALU.subtract,
                                  ALU.mult).then_inc(scaled, 1)

            def total(c, b, first):
                dve.wait_ge(relued, c + 1)
                if not first:
                    dve.wait_ge(turned, c - 1)
                dve.tensor_tensor(s[b][:], r[b][:], xT[0:D, bass.ts(c, 512)], ALU.add).then_inc(summed, 1)

            def add(c, b):
                dve.wait_ge(turned, c + 1)
                dve.tensor_tensor(h[:, bass.ts(c, 4), :], h[:, bass.ts(c, 4), :], t_ps[b][:], ALU.add)\
                   .then_inc(added, 1)

            scale(0, 0, True)
            scale(1, 1, True)
            total(0, 0, True)
            scale(2, 0, False)
            total(1, 1, True)
            scale(3, 1, False)
            with dve.Fori(1, n // 2 - 1) as i:
                for b in range(2):
                    add(2 * i + b - 2, b)
                    total(2 * i + b, b, False)
                    scale(2 * i + b + 2, b, False)
            for c in (n - 2, n - 1):
                add(c - 2, c % 2)
                total(c, c % 2, False)
            for c in (n - 2, n - 1):
                add(c, c % 2)

        @block.scalar
        def _(act):
            act.wait_ge(var_ready, 1)
            act.activation(mv[:, 2:3], mv[:, 1:2], ACT.Sqrt, bias=k.eps[0:D, 0:1]).then_inc(std_ready, 1)

            def relu(c, b, first):
                act.wait_ge(scaled, c + 1)
                if not first:
                    act.wait_ge(summed, c - 1)
                act.activation(r[b][:], z[b][:], ACT.Relu, bias=k.bn[:, 1:2]).then_inc(relued, 1)
            twice(act, n, relu)

        @block.tensor
        def _(pe):
            def turn(c, b, first):
                pe.wait_ge(summed, c + 1)
                if not first:
                    pe.wait_ge(added, c - 1)
                pe.sem_inc(k.pe_passed, 1)
                for t in range(4):
                    ins = pe.transpose(t_ps[b][:, t, :], s[b][:, t * P:(t + 1) * P], k.ident[0:D, 0:D])
                ins.then_inc(turned, 1)
            twice(pe, n, turn)


class Names:
    pass


def program(nc, a, out):
    with ExitStack() as ctx:
        mem = Memory(nc, ctx)
        k = Names()
        h = mem.sb("h", [P, TILES, D])
        xn = mem.sb("xn", [P, TILES, D])
        xT_padded = mem.sb("xT", [P, M])
        xT = xT_padded[0:D + 1, :]
        k.big = mem.sb("squares", [P, TILES, D])
        k.ln_s = mem.sb("ln_stats", [P, 5, TILES])
        k.ln_xs = [mem.sb(f"ln_xs{b}", [P, 4, D]) for b in range(2)]
        hg = mem.sb("router_h", [P, TILES, GH * GE])
        gates = [mem.sb("gates0", [P, TILES, E0]), mem.sb("gates1", [P, TILES, E1])]
        logits = mem.sb("logits1", [P, TILES, E1])
        k.pe_passed, k.pool_passed = mem.sem("tensor_waits_passed"), mem.sem("gpsimd_waits_passed")

        def stage():
            return Stage(mem)

        k.ln_sems = [mem.sem(f"ln_{x}") for x in (
            "step", "centered", "squared", "summed", "rooted", "inverted", "scaled", "turned", "evacuated",
            "mapped", "saved")]
        calls = [0, 0]

        def norm(name, **kw):
            with stage() as m:
                k.ln_pT = [m.ps(f"{name}_pT{b}", [D, 512]) for b in range(2)]
                k.ln_pj = [m.ps(f"{name}_pj{b}", [P, 4, GH * GE]) for b in range(2)]
                normalize(nc, m, k, h, xn, xT, *calls, **kw)
            calls[0] += 1
            calls[1] += "weight" in kw

        sort = EdgeSort(mem)
        ys = [xn[:], k.big[:], *(t[:].rearrange("p (t d) -> p t d", d=D) for t in (sort.keys, sort.other))]
        loads = allocate_constants(mem, a, k)
        with stage() as m:
            tokenize(nc, m, a, k, h, xT_padded, sort, loads)
        norm("ln0")
        with stage() as m:
            window_attention(nc, m, k, xT, h, sort)
        norm("ln1", weight=k.wgat[:], out=hg, beside=sort.find_digits)
        with stage() as m:
            graph_router(nc, m, a, k, hg, sort, xT, ys, gates[0])
        with stage() as m:
            combine(nc, m, ys, gates[0], h)
        norm("ln2")
        with stage() as m:
            yT = m.sb("yT", [D, M])
            stats = m.sb("bn_stats", [D, 8 * 6])
            with stage() as m2:
                image_attention(nc, m2, k, xT, yT, stats)
            with stage() as m2:
                batch_norm_add(nc, m2, k, xT, yT, stats, h)
        norm("ln3", weight=k.wr[:], out=logits, affine=k.affine)
        with stage() as m:
            experts(nc, m, k, xT_padded, logits, gates[1], h, out)


_INS = ['x', 'L0_tok_W', 'L0_tok_b', 'L0_attn_w_qkv', 'L0_attn_b_qkv', 'L0_attn_w_proj', 'L0_attn_b_proj',
        'L0_attn_rel_pos_bias', 'L0_ffn_W_gat', 'L0_ffn_att_src', 'L0_ffn_att_dst', 'L0_ffn_b_gat',
        'L0_ffn_ln_gamma', 'L0_ffn_ln_beta', 'L0_ffn_W1', 'L0_ffn_b1', 'L0_ffn_W2', 'L0_ffn_b2',
        'L0_ffn_edge_index', 'L1_attn_Wq', 'L1_attn_bq', 'L1_attn_Wk', 'L1_attn_bk', 'L1_attn_Wv',
        'L1_attn_bv', 'L1_attn_Wl', 'L1_attn_bl', 'L1_attn_gamma', 'L1_attn_beta', 'L1_ffn_gamma',
        'L1_ffn_beta', 'L1_ffn_Wr', 'L1_ffn_br', 'L1_ffn_W1', 'L1_ffn_b1', 'L1_ffn_W2', 'L1_ffn_b2']


def kernel(**inputs):
    import numpy as np
    import concourse.bacc as bacc
    from concourse.bass_utils import run_bass_kernel_spmd

    nc = bacc.Bacc("TRN2", target_bir_lowering=False, num_devices=1)
    arrays, args = {}, {}
    for name in _INS:
        v = np.ascontiguousarray(inputs[name])
        arrays["in_" + name] = v
        args[name] = nc.dram_tensor("in_" + name, v.shape, mybir.dt.from_np(v.dtype), kind="ExternalInput").ap()
    out = nc.dram_tensor("out_h", (IMG, WIN, D), F32, kind="ExternalOutput").ap()
    program(nc, args, out)
    return run_bass_kernel_spmd(nc, [arrays], core_ids=[0]).results[0]["out_h"]
```
